# Optimizing a Trainium2 kernel written in Bass

```python
import numpy as np
import jax
import jax.numpy as jnp

def _softmax(x, axis=-1):
    return jax.nn.softmax(x, axis=axis)

def _gelu(x):
    return jax.nn.gelu(x, approximate=True)

def _silu(x):
    return jax.nn.silu(x)

def _sigmoid(x):
    return jax.nn.sigmoid(x)

def _layernorm(x, axis=-1, eps=1e-05):
    m = jnp.mean(x, axis=axis, keepdims=True)
    v = jnp.var(x, axis=axis, keepdims=True)
    return (x - m) / jnp.sqrt(v + eps)

def _scatter_add(tgt, idx, src, axis=0):
    return tgt.at[idx].add(src)

def _segment_sum(src, seg, n):
    return jax.ops.segment_sum(src, seg, n)
kernel_name = 'mk_recurrent_d2_jaxref_r8_b454f6'

def setup_inputs(seed: int=0):
    np.random.seed(seed)
    _w = jnp.asarray

    def _L0_attn_setup():
        import jax, jax.numpy as jnp
        import numpy as np
        from jax import lax
        D_MODEL = 128
        B, T = (4, 256)
        LN_EPS = 1e-05

        def _ln(x, w, b):
            mu = jnp.mean(x, axis=-1, keepdims=True)
            var = jnp.mean((x - mu) ** 2, axis=-1, keepdims=True)
            return (x - mu) * lax.rsqrt(var + LN_EPS) * w + b

        def _wkv(u, k, v):
            Bb, Tt, C = k.shape

            def step(carry, kv):
                aa, bb = carry
                kk, vv = kv
                p = jnp.maximum(bb, u + kk)
                e1 = jnp.exp(bb - p)
                e2 = jnp.exp(u + kk - p)
                out = (e1 * aa + e2 * vv) / (e1 + e2)
                p2 = jnp.maximum(bb, kk)
                e1b = jnp.exp(bb - p2)
                e2b = jnp.exp(kk - p2)
                return ((e1b * aa + e2b * vv, p2 + jnp.log(e1b + e2b)), out)
            init = (jnp.zeros((Bb, C), k.dtype), jnp.zeros((Bb, C), k.dtype))
            _, outs = lax.scan(step, init, (jnp.swapaxes(k, 0, 1), jnp.swapaxes(v, 0, 1)))
            return jnp.swapaxes(outs, 0, 1)
        key = jax.random.key(seed)
        ks = jax.random.split(key, 12)
        C = D_MODEL
        s = 0.02
        return {'x': jax.random.normal(ks[0], (B, T, C), jnp.float32), 'time_decay': jax.random.normal(ks[1], (C,), jnp.float32), 'time_first': jax.random.normal(ks[2], (C,), jnp.float32) * 0.5, 'time_shift': jax.random.normal(ks[3], (1, 1, C), jnp.float32) * 0.1, 'Wk': jax.random.normal(ks[4], (C, C), jnp.float32) * s, 'Wv': jax.random.normal(ks[5], (C, C), jnp.float32) * s, 'Wr': jax.random.normal(ks[6], (C, C), jnp.float32) * s, 'Wck': jax.random.normal(ks[7], (4 * C, C), jnp.float32) * s, 'Wcv': jax.random.normal(ks[8], (C, 4 * C), jnp.float32) * s, 'Wcr': jax.random.normal(ks[9], (C, C), jnp.float32) * s, 'ln1_w': jnp.ones((C,), jnp.float32), 'ln1_b': jnp.zeros((C,), jnp.float32), 'ln2_w': jnp.ones((C,), jnp.float32), 'ln2_b': jnp.zeros((C,), jnp.float32)}
    _L0_attn_in = _L0_attn_setup()

    def _L0_ffn_setup():
        import jax, jax.numpy as jnp
        import numpy as np
        B, S, DIM = (4, 512, 128)
        BASE_COUPLING = 0.1
        NUM_CYCLES = 3

        def _gelu(x):
            return jax.nn.gelu(x, approximate=False)

        def _coupling_net(h, w1, b1, w2, b2, w3, b3, w4, b4):
            h = _gelu(h @ w1 + b1)
            h = _gelu(h @ w2 + b2)
            h = _gelu(h @ w3 + b3)
            return jax.nn.sigmoid(h @ w4 + b4)

        def _global_net(h, w1, b1, w2, b2, w3, b3):
            h = _gelu(h @ w1 + b1)
            h = _gelu(h @ w2 + b2)
            return jax.nn.sigmoid(h @ w3 + b3)

        def _twist(x):
            o_r, o_i, p_r, p_i = jnp.split(x, 4, axis=-1)
            return jnp.concatenate([p_r, -p_i, -o_r, o_i], axis=-1)
        key = jax.random.key(seed)
        ks = jax.random.split(key, 9)
        d = DIM

        def w(k, fan_in, fan_out):
            return jax.random.normal(k, (fan_in, fan_out), dtype=jnp.float32) / np.sqrt(fan_in).astype(np.float32)
        inp = {'x': jax.random.normal(ks[0], (B, S, d), dtype=jnp.float32)}
        cn_dims = [(d, d), (d, d // 2), (d // 2, d // 4), (d // 4, 1)]
        for i, (a, b) in enumerate(cn_dims):
            inp[f'cn_w{i + 1}'] = w(ks[1 + i], a, b)
            inp[f'cn_b{i + 1}'] = jnp.zeros((b,), dtype=jnp.float32)
        gc_dims = [(d, d // 2), (d // 2, d // 4), (d // 4, 1)]
        for i, (a, b) in enumerate(gc_dims):
            inp[f'gc_w{i + 1}'] = w(ks[5 + i], a, b)
            inp[f'gc_b{i + 1}'] = jnp.zeros((b,), dtype=jnp.float32)
        inp['adaptive_range'] = jnp.full((1,), 0.2, dtype=jnp.float32)
        return inp
    _L0_ffn_in = _L0_ffn_setup()

    def _L1_attn_setup():
        import jax, jax.numpy as jnp
        import numpy as np
        import math
        D_MODEL = 128
        HEAD_DIM = 128
        BATCH, SEQ = (4, 512)
        key = jax.random.key(seed)
        ks = jax.random.split(key, 10)
        s_in = 1.0 / math.sqrt(D_MODEL)
        s_out = 1.0 / math.sqrt(HEAD_DIM)
        x = jax.random.normal(ks[0], (BATCH, SEQ, D_MODEL), dtype=jnp.float32)
        wavelengths = jnp.arange(1, HEAD_DIM + 1, dtype=jnp.float32) * 2.0 * math.pi / HEAD_DIM
        phase_bias = jnp.zeros((HEAD_DIM,), dtype=jnp.float32)
        Wq = jax.random.uniform(ks[1], (HEAD_DIM, D_MODEL), jnp.float32, -s_in, s_in)
        bq = jax.random.uniform(ks[2], (HEAD_DIM,), jnp.float32, -s_in, s_in)
        Wk = jax.random.uniform(ks[3], (HEAD_DIM, D_MODEL), jnp.float32, -s_in, s_in)
        bk = jax.random.uniform(ks[4], (HEAD_DIM,), jnp.float32, -s_in, s_in)
        Wv = jax.random.uniform(ks[5], (HEAD_DIM, D_MODEL), jnp.float32, -s_in, s_in)
        bv = jax.random.uniform(ks[6], (HEAD_DIM,), jnp.float32, -s_in, s_in)
        Wo = jax.random.uniform(ks[7], (D_MODEL, HEAD_DIM), jnp.float32, -s_out, s_out)
        bo = jax.random.uniform(ks[8], (D_MODEL,), jnp.float32, -s_out, s_out)
        return {'x': x, 'wavelengths': wavelengths, 'phase_bias': phase_bias, 'Wq': Wq, 'bq': bq, 'Wk': Wk, 'bk': bk, 'Wv': Wv, 'bv': bv, 'Wo': Wo, 'bo': bo}
    _L1_attn_in = _L1_attn_setup()

    def _L1_ffn_setup():
        import jax, jax.numpy as jnp
        import numpy as np
        DIM = 128
        DEPTH = 2
        HEADS = 8
        DIM_HEAD = 64
        WINDOW = 64
        INNER = HEADS * DIM_HEAD
        HID = int(DIM * 4 * 2 / 3)
        B, N = (2, 1024)
        QK_SCALE = 8.0

        def shift_token(t):
            t1, t2 = jnp.split(t, 2, axis=-1)
            t2 = jnp.pad(t2, ((0, 0), (1, 0), (0, 0)))[:, :-1]
            return jnp.concatenate([t1, t2], axis=-1)

        def l2norm(t):
            return t / jnp.clip(jnp.linalg.norm(t, axis=-1, keepdims=True), 1e-12)

        def rotate_half(x):
            x1, x2 = jnp.split(x, 2, axis=-1)
            return jnp.concatenate([-x2, x1], axis=-1)

        def rotary_xpos(q, k):
            n = q.shape[-2]
            half_idx = jnp.arange(0, DIM_HEAD, 2, dtype=jnp.float32)
            inv_freq = 1.0 / 10000.0 ** (half_idx / DIM_HEAD)
            t = jnp.arange(n, dtype=jnp.float32)
            freqs = t[:, None] * inv_freq[None, :]
            freqs = jnp.concatenate([freqs, freqs], axis=-1)
            base = (half_idx + 0.4 * DIM_HEAD) / (1.4 * DIM_HEAD)
            power = (t - n // 2) / float(WINDOW // 2)
            scale = base[None, :] ** power[:, None]
            scale = jnp.concatenate([scale, scale], axis=-1)
            cos, sin = (jnp.cos(freqs), jnp.sin(freqs))
            q = q * cos * scale + rotate_half(q) * sin * scale
            k = k * cos / scale + rotate_half(k) * sin / scale
            return (q, k)

        def local_attention(q, k, v):
            b, h, n, d = q.shape
            w = n // WINDOW
            bq = q.reshape(b, h, w, WINDOW, d) * QK_SCALE
            bk = k.reshape(b, h, w, WINDOW, d)
            bv = v.reshape(b, h, w, WINDOW, d)

            def look_around(t):
                p = jnp.pad(t, ((0, 0), (0, 0), (1, 0), (0, 0), (0, 0)))
                return jnp.concatenate([p[:, :, :w], p[:, :, 1:]], axis=3)
            bk, bv = (look_around(bk), look_around(bv))
            bt = jnp.arange(n).reshape(w, WINDOW)
            btp = jnp.pad(bt, ((1, 0), (0, 0)), constant_values=-1)
            btk = jnp.concatenate([btp[:w], btp[1:]], axis=1)
            sim = jnp.einsum('bhwid,bhwjd->bhwij', bq, bk)
            i = bt[:, :, None]
            j = btk[:, None, :]
            mask = (i < j) | (i > j + WINDOW) | (j == -1)
            sim = jnp.where(mask, -jnp.finfo(sim.dtype).max, sim)
            attn = jax.nn.softmax(sim, axis=-1)
            out = jnp.einsum('bhwij,bhwjd->bhwid', attn, bv)
            return out.reshape(b, h, n, d)

        def _layer(x, wqkv, qs, ksc, wo, lg, lb, w1, b1, w2, b2):
            b, n, _ = x.shape
            h = shift_token(x)
            qkv = h @ wqkv
            q, k, v = jnp.split(qkv, 3, axis=-1)
            to_heads = lambda t: t.reshape(b, n, HEADS, DIM_HEAD).transpose(0, 2, 1, 3)
            q, k, v = (to_heads(q), to_heads(k), to_heads(v))
            q = l2norm(q) * qs
            k = l2norm(k) * ksc
            q, k = rotary_xpos(q, k)
            o = local_attention(q, k, v)
            o = o.transpose(0, 2, 1, 3).reshape(b, n, INNER)
            x = x + o @ wo
            h = shift_token(x)
            mu = h.mean(-1, keepdims=True)
            var = h.var(-1, keepdims=True)
            h = (h - mu) / jnp.sqrt(var + 1e-05) * lg + lb
            h = h @ w1 + b1
            a, g = jnp.split(h, 2, axis=-1)
            h = a * jax.nn.gelu(g, approximate=False)
            x = x + h @ w2 + b2
            return x
        key = jax.random.key(seed)
        ks = jax.random.split(key, 6)
        return {'x': jax.random.normal(ks[0], (B, N, DIM), jnp.float32), 'wqkv': jax.random.normal(ks[1], (DEPTH, DIM, 3 * INNER), jnp.float32) * 0.02, 'q_scale': jnp.ones((DEPTH, DIM_HEAD), jnp.float32), 'k_scale': jnp.ones((DEPTH, DIM_HEAD), jnp.float32), 'wo': jax.random.normal(ks[2], (DEPTH, INNER, DIM), jnp.float32) * 0.02, 'ln_g': jnp.ones((DEPTH, DIM), jnp.float32), 'ln_b': jnp.zeros((DEPTH, DIM), jnp.float32), 'w1': jax.random.normal(ks[3], (DEPTH, DIM, 2 * HID), jnp.float32) * 0.02, 'b1': jnp.zeros((DEPTH, 2 * HID), jnp.float32), 'w2': jax.random.normal(ks[4], (DEPTH, HID, DIM), jnp.float32) * 0.02, 'b2': jnp.zeros((DEPTH, DIM), jnp.float32)}
    _L1_ffn_in = _L1_ffn_setup()
    _d = {'L0_attn_x': _L0_attn_in['x'], 'L0_attn_time_decay': _L0_attn_in['time_decay'], 'L0_attn_time_first': _L0_attn_in['time_first'], 'L0_attn_time_shift': _L0_attn_in['time_shift'], 'L0_attn_Wk': _L0_attn_in['Wk'], 'L0_attn_Wv': _L0_attn_in['Wv'], 'L0_attn_Wr': _L0_attn_in['Wr'], 'L0_attn_Wck': _L0_attn_in['Wck'], 'L0_attn_Wcv': _L0_attn_in['Wcv'], 'L0_attn_Wcr': _L0_attn_in['Wcr'], 'L0_attn_ln1_w': _L0_attn_in['ln1_w'], 'L0_attn_ln1_b': _L0_attn_in['ln1_b'], 'L0_attn_ln2_w': _L0_attn_in['ln2_w'], 'L0_attn_ln2_b': _L0_attn_in['ln2_b'], 'L0_ffn_cn_w1': _L0_ffn_in['cn_w1'], 'L0_ffn_cn_b1': _L0_ffn_in['cn_b1'], 'L0_ffn_cn_w2': _L0_ffn_in['cn_w2'], 'L0_ffn_cn_b2': _L0_ffn_in['cn_b2'], 'L0_ffn_cn_w3': _L0_ffn_in['cn_w3'], 'L0_ffn_cn_b3': _L0_ffn_in['cn_b3'], 'L0_ffn_cn_w4': _L0_ffn_in['cn_w4'], 'L0_ffn_cn_b4': _L0_ffn_in['cn_b4'], 'L0_ffn_gc_w1': _L0_ffn_in['gc_w1'], 'L0_ffn_gc_b1': _L0_ffn_in['gc_b1'], 'L0_ffn_gc_w2': _L0_ffn_in['gc_w2'], 'L0_ffn_gc_b2': _L0_ffn_in['gc_b2'], 'L0_ffn_gc_w3': _L0_ffn_in['gc_w3'], 'L0_ffn_gc_b3': _L0_ffn_in['gc_b3'], 'L0_ffn_adaptive_range': _L0_ffn_in['adaptive_range'], 'L1_attn_wavelengths': _L1_attn_in['wavelengths'], 'L1_attn_phase_bias': _L1_attn_in['phase_bias'], 'L1_attn_Wq': _L1_attn_in['Wq'], 'L1_attn_bq': _L1_attn_in['bq'], 'L1_attn_Wk': _L1_attn_in['Wk'], 'L1_attn_bk': _L1_attn_in['bk'], 'L1_attn_Wv': _L1_attn_in['Wv'], 'L1_attn_bv': _L1_attn_in['bv'], 'L1_attn_Wo': _L1_attn_in['Wo'], 'L1_attn_bo': _L1_attn_in['bo'], 'L1_ffn_wqkv': _L1_ffn_in['wqkv'], 'L1_ffn_q_scale': _L1_ffn_in['q_scale'], 'L1_ffn_k_scale': _L1_ffn_in['k_scale'], 'L1_ffn_wo': _L1_ffn_in['wo'], 'L1_ffn_ln_g': _L1_ffn_in['ln_g'], 'L1_ffn_ln_b': _L1_ffn_in['ln_b'], 'L1_ffn_w1': _L1_ffn_in['w1'], 'L1_ffn_b1': _L1_ffn_in['b1'], 'L1_ffn_w2': _L1_ffn_in['w2'], 'L1_ffn_b2': _L1_ffn_in['b2']}
    _x0 = _d['L0_attn_x']
    _d['L0_attn_x'] = jax.random.normal(jax.random.fold_in(jax.random.key(seed), 1), (8, 1024, 128), dtype=_x0.dtype)
    del _x0
    return _d

def reference(L0_attn_x, L0_attn_time_decay, L0_attn_time_first, L0_attn_time_shift, L0_attn_Wk, L0_attn_Wv, L0_attn_Wr, L0_attn_Wck, L0_attn_Wcv, L0_attn_Wcr, L0_attn_ln1_w, L0_attn_ln1_b, L0_attn_ln2_w, L0_attn_ln2_b, L0_ffn_cn_w1, L0_ffn_cn_b1, L0_ffn_cn_w2, L0_ffn_cn_b2, L0_ffn_cn_w3, L0_ffn_cn_b3, L0_ffn_cn_w4, L0_ffn_cn_b4, L0_ffn_gc_w1, L0_ffn_gc_b1, L0_ffn_gc_w2, L0_ffn_gc_b2, L0_ffn_gc_w3, L0_ffn_gc_b3, L0_ffn_adaptive_range, L1_attn_wavelengths, L1_attn_phase_bias, L1_attn_Wq, L1_attn_bq, L1_attn_Wk, L1_attn_bk, L1_attn_Wv, L1_attn_bv, L1_attn_Wo, L1_attn_bo, L1_ffn_wqkv, L1_ffn_q_scale, L1_ffn_k_scale, L1_ffn_wo, L1_ffn_ln_g, L1_ffn_ln_b, L1_ffn_w1, L1_ffn_b1, L1_ffn_w2, L1_ffn_b2):

    def _L0_attn_ref(x, time_decay, time_first, time_shift, Wk, Wv, Wr, Wck, Wcv, Wcr, ln1_w, ln1_b, ln2_w, ln2_b):
        import jax, jax.numpy as jnp
        import numpy as np
        from jax import lax
        D_MODEL = 128
        B, T = (4, 256)
        LN_EPS = 1e-05

        def _ln(x, w, b):
            mu = jnp.mean(x, axis=-1, keepdims=True)
            var = jnp.mean((x - mu) ** 2, axis=-1, keepdims=True)
            return (x - mu) * lax.rsqrt(var + LN_EPS) * w + b

        def _wkv(u, k, v):
            Bb, Tt, C = k.shape

            def step(carry, kv):
                aa, bb = carry
                kk, vv = kv
                p = jnp.maximum(bb, u + kk)
                e1 = jnp.exp(bb - p)
                e2 = jnp.exp(u + kk - p)
                out = (e1 * aa + e2 * vv) / (e1 + e2)
                p2 = jnp.maximum(bb, kk)
                e1b = jnp.exp(bb - p2)
                e2b = jnp.exp(kk - p2)
                return ((e1b * aa + e2b * vv, p2 + jnp.log(e1b + e2b)), out)
            init = (jnp.zeros((Bb, C), k.dtype), jnp.zeros((Bb, C), k.dtype))
            _, outs = lax.scan(step, init, (jnp.swapaxes(k, 0, 1), jnp.swapaxes(v, 0, 1)))
            return jnp.swapaxes(outs, 0, 1)
        Bb, Tt, C = x.shape
        ts = time_shift
        h = _ln(x, ln1_w, ln1_b)
        x_shifted = jnp.concatenate([jnp.broadcast_to(ts, (Bb, 1, C)), h[:, :-1, :]], axis=1)
        xxx = h + (h - x_shifted) * ts
        k = jnp.einsum('btc,oc->bto', xxx, Wk)
        v = jnp.einsum('btc,oc->bto', xxx, Wv)
        r = jax.nn.sigmoid(jnp.einsum('btc,oc->bto', xxx, Wr))
        wkv = _wkv(time_first, k, v)
        x = x + r * wkv
        h2 = _ln(x, ln2_w, ln2_b)
        xx2 = jnp.concatenate([h2[:, -1:, :], h2[:, :-1, :]], axis=1)
        xxx2 = h2 + (xx2 - h2) * ts
        kc = jnp.einsum('btc,oc->bto', xxx2, Wck)
        rc = jax.nn.sigmoid(jnp.einsum('btc,oc->bto', xxx2, Wcr))
        vv = jnp.einsum('bth,ch->btc', jax.nn.relu(kc) ** 2, Wcv)
        return x + rc * vv

    def _L0_ffn_ref(x, cn_w1, cn_b1, cn_w2, cn_b2, cn_w3, cn_b3, cn_w4, cn_b4, gc_w1, gc_b1, gc_w2, gc_b2, gc_w3, gc_b3, adaptive_range):
        import jax, jax.numpy as jnp
        import numpy as np
        B, S, DIM = (4, 512, 128)
        BASE_COUPLING = 0.1
        NUM_CYCLES = 3

        def _gelu(x):
            return jax.nn.gelu(x, approximate=False)

        def _coupling_net(h, w1, b1, w2, b2, w3, b3, w4, b4):
            h = _gelu(h @ w1 + b1)
            h = _gelu(h @ w2 + b2)
            h = _gelu(h @ w3 + b3)
            return jax.nn.sigmoid(h @ w4 + b4)

        def _global_net(h, w1, b1, w2, b2, w3, b3):
            h = _gelu(h @ w1 + b1)
            h = _gelu(h @ w2 + b2)
            return jax.nn.sigmoid(h @ w3 + b3)

        def _twist(x):
            o_r, o_i, p_r, p_i = jnp.split(x, 4, axis=-1)
            return jnp.concatenate([p_r, -p_i, -o_r, o_i], axis=-1)
        global_context = x.mean(axis=1, keepdims=True)
        gf = _global_net(global_context, gc_w1, gc_b1, gc_w2, gc_b2, gc_w3, gc_b3)
        out = x
        for _ in range(NUM_CYCLES):
            tf = _coupling_net(out, cn_w1, cn_b1, cn_w2, cn_b2, cn_w3, cn_b3, cn_w4, cn_b4)
            combined = 0.7 * gf + 0.3 * tf
            coupling = BASE_COUPLING + adaptive_range * (combined - 0.5) * 2.0
            out = out + coupling * _twist(out)
        return out

    def _L1_attn_ref(x, wavelengths, phase_bias, Wq, bq, Wk, bk, Wv, bv, Wo, bo):
        import jax, jax.numpy as jnp
        import numpy as np
        import math
        D_MODEL = 128
        HEAD_DIM = 128
        BATCH, SEQ = (4, 512)
        Q = jnp.einsum('bsd,hd->bsh', x, Wq) + bq
        K = jnp.einsum('bsd,hd->bsh', x, Wk) + bk
        V = jnp.einsum('bsd,hd->bsh', x, Wv) + bv
        inv_w = 1.0 / (wavelengths + 1e-08)
        theta_q = Q * inv_w + phase_bias
        theta_k = K * inv_w + phase_bias
        sim = jnp.einsum('bqh,bkh->bqk', jnp.cos(theta_q), jnp.cos(theta_k)) + jnp.einsum('bqh,bkh->bqk', jnp.sin(theta_q), jnp.sin(theta_k))
        weights = jax.nn.softmax(sim / math.sqrt(HEAD_DIM), axis=-1)
        out = jnp.einsum('bqk,bkh->bqh', weights, V)
        return jnp.einsum('bqh,dh->bqd', out, Wo) + bo

    def _L1_ffn_ref(x, wqkv, q_scale, k_scale, wo, ln_g, ln_b, w1, b1, w2, b2):
        import jax, jax.numpy as jnp
        import numpy as np
        DIM = 128
        DEPTH = 2
        HEADS = 8
        DIM_HEAD = 64
        WINDOW = 64
        INNER = HEADS * DIM_HEAD
        HID = int(DIM * 4 * 2 / 3)
        B, N = (2, 1024)
        QK_SCALE = 8.0

        def shift_token(t):
            t1, t2 = jnp.split(t, 2, axis=-1)
            t2 = jnp.pad(t2, ((0, 0), (1, 0), (0, 0)))[:, :-1]
            return jnp.concatenate([t1, t2], axis=-1)

        def l2norm(t):
            return t / jnp.clip(jnp.linalg.norm(t, axis=-1, keepdims=True), 1e-12)

        def rotate_half(x):
            x1, x2 = jnp.split(x, 2, axis=-1)
            return jnp.concatenate([-x2, x1], axis=-1)

        def rotary_xpos(q, k):
            n = q.shape[-2]
            half_idx = jnp.arange(0, DIM_HEAD, 2, dtype=jnp.float32)
            inv_freq = 1.0 / 10000.0 ** (half_idx / DIM_HEAD)
            t = jnp.arange(n, dtype=jnp.float32)
            freqs = t[:, None] * inv_freq[None, :]
            freqs = jnp.concatenate([freqs, freqs], axis=-1)
            base = (half_idx + 0.4 * DIM_HEAD) / (1.4 * DIM_HEAD)
            power = (t - n // 2) / float(WINDOW // 2)
            scale = base[None, :] ** power[:, None]
            scale = jnp.concatenate([scale, scale], axis=-1)
            cos, sin = (jnp.cos(freqs), jnp.sin(freqs))
            q = q * cos * scale + rotate_half(q) * sin * scale
            k = k * cos / scale + rotate_half(k) * sin / scale
            return (q, k)

        def local_attention(q, k, v):
            b, h, n, d = q.shape
            w = n // WINDOW
            bq = q.reshape(b, h, w, WINDOW, d) * QK_SCALE
            bk = k.reshape(b, h, w, WINDOW, d)
            bv = v.reshape(b, h, w, WINDOW, d)

            def look_around(t):
                p = jnp.pad(t, ((0, 0), (0, 0), (1, 0), (0, 0), (0, 0)))
                return jnp.concatenate([p[:, :, :w], p[:, :, 1:]], axis=3)
            bk, bv = (look_around(bk), look_around(bv))
            bt = jnp.arange(n).reshape(w, WINDOW)
            btp = jnp.pad(bt, ((1, 0), (0, 0)), constant_values=-1)
            btk = jnp.concatenate([btp[:w], btp[1:]], axis=1)
            sim = jnp.einsum('bhwid,bhwjd->bhwij', bq, bk)
            i = bt[:, :, None]
            j = btk[:, None, :]
            mask = (i < j) | (i > j + WINDOW) | (j == -1)
            sim = jnp.where(mask, -jnp.finfo(sim.dtype).max, sim)
            attn = jax.nn.softmax(sim, axis=-1)
            out = jnp.einsum('bhwij,bhwjd->bhwid', attn, bv)
            return out.reshape(b, h, n, d)

        def _layer(x, wqkv, qs, ksc, wo, lg, lb, w1, b1, w2, b2):
            b, n, _ = x.shape
            h = shift_token(x)
            qkv = h @ wqkv
            q, k, v = jnp.split(qkv, 3, axis=-1)
            to_heads = lambda t: t.reshape(b, n, HEADS, DIM_HEAD).transpose(0, 2, 1, 3)
            q, k, v = (to_heads(q), to_heads(k), to_heads(v))
            q = l2norm(q) * qs
            k = l2norm(k) * ksc
            q, k = rotary_xpos(q, k)
            o = local_attention(q, k, v)
            o = o.transpose(0, 2, 1, 3).reshape(b, n, INNER)
            x = x + o @ wo
            h = shift_token(x)
            mu = h.mean(-1, keepdims=True)
            var = h.var(-1, keepdims=True)
            h = (h - mu) / jnp.sqrt(var + 1e-05) * lg + lb
            h = h @ w1 + b1
            a, g = jnp.split(h, 2, axis=-1)
            h = a * jax.nn.gelu(g, approximate=False)
            x = x + h @ w2 + b2
            return x
        for l in range(DEPTH):
            x = _layer(x, wqkv[l], q_scale[l], k_scale[l], wo[l], ln_g[l], ln_b[l], w1[l], b1[l], w2[l], b2[l])
        return x
    x = L0_attn_x
    xn = _layernorm(x, axis=-1)
    s = _L0_attn_ref(xn, L0_attn_time_decay, L0_attn_time_first, L0_attn_time_shift, L0_attn_Wk, L0_attn_Wv, L0_attn_Wr, L0_attn_Wck, L0_attn_Wcv, L0_attn_Wcr, L0_attn_ln1_w, L0_attn_ln1_b, L0_attn_ln2_w, L0_attn_ln2_b)
    g = _silu(_L0_ffn_ref(xn, L0_ffn_cn_w1, L0_ffn_cn_b1, L0_ffn_cn_w2, L0_ffn_cn_b2, L0_ffn_cn_w3, L0_ffn_cn_b3, L0_ffn_cn_w4, L0_ffn_cn_b4, L0_ffn_gc_w1, L0_ffn_gc_b1, L0_ffn_gc_w2, L0_ffn_gc_b2, L0_ffn_gc_w3, L0_ffn_gc_b3, L0_ffn_adaptive_range))
    x = x + s * g
    xn = _layernorm(x, axis=-1)
    s = _L1_attn_ref(xn, L1_attn_wavelengths, L1_attn_phase_bias, L1_attn_Wq, L1_attn_bq, L1_attn_Wk, L1_attn_bk, L1_attn_Wv, L1_attn_bv, L1_attn_Wo, L1_attn_bo)
    g = _silu(_L1_ffn_ref(xn, L1_ffn_wqkv, L1_ffn_q_scale, L1_ffn_k_scale, L1_ffn_wo, L1_ffn_ln_g, L1_ffn_ln_b, L1_ffn_w1, L1_ffn_b1, L1_ffn_w2, L1_ffn_b2))
    x = x + s * g
    return x

_drawn_inputs = setup_inputs


def setup_inputs(seed=0):
    import zlib

    import numpy as np

    out = dict(_drawn_inputs(seed))
    spreads = {'L0_attn_ln1_w': (1.0, 0.6),
     'L0_attn_ln1_b': (0.0, 0.303),
     'L0_attn_ln2_w': (1.0, 0.6),
     'L0_attn_ln2_b': (0.0, 0.8),
     'L0_ffn_cn_b1': (0.0, 0.8),
     'L0_ffn_cn_b2': (0.0, 0.8),
     'L0_ffn_cn_b3': (0.0, 2.0),
     'L0_ffn_gc_b1': (0.0, 0.8),
     'L0_ffn_gc_b2': (0.0, 2.0),
     'L1_attn_phase_bias': (0.0, 2.0),
     'L1_ffn_q_scale': (1.0, 0.6),
     'L1_ffn_k_scale': (1.0, 0.6),
     'L1_ffn_ln_g': (1.0, 0.6),
     'L1_ffn_ln_b': (0.0, 0.8),
     'L1_ffn_b1': (0.0, 0.8),
     'L1_ffn_b2': (0.0, 0.8)}
    factors = {'L0_attn_time_first': 8.0,
     'L0_attn_time_shift': 8.0,
     'L0_attn_Wk': 5.044,
     'L0_attn_Wr': 8.0,
     'L0_attn_Wck': 8.0,
     'L0_attn_Wcv': 8.0,
     'L0_attn_Wcr': 8.0,
     'L0_ffn_cn_w1': 8.0,
     'L0_ffn_cn_w2': 8.0,
     'L0_ffn_cn_w3': 8.0,
     'L0_ffn_cn_w4': 5.349,
     'L0_ffn_gc_w1': 64.0,
     'L0_ffn_gc_w2': 64.0,
     'L0_ffn_gc_w3': 8.0,
     'L1_attn_wavelengths': 8.0,
     'L1_attn_Wq': 8.0,
     'L1_attn_bq': 28.258,
     'L1_attn_Wk': 8.0,
     'L1_attn_bk': 39.562,
     'L1_attn_Wv': 8.0,
     'L1_attn_bv': 4.066,
     'L1_attn_Wo': 3.851,
     'L1_ffn_wqkv': 8.0,
     'L1_ffn_wo': 8.0,
     'L1_ffn_w1': 8.0,
     'L1_ffn_w2': 8.0}
    for name, (base, spread) in spreads.items():
        noise = np.random.default_rng([zlib.crc32(name.encode()), seed]).standard_normal(out[name].shape)
        drawn = base * np.exp(spread * noise) if base else spread * noise
        out[name] = jnp.asarray(drawn.astype(out[name].dtype))
    for name, factor in factors.items():
        out[name] = (out[name] * factor).astype(out[name].dtype)
    return out
```

```python
from contextlib import ExitStack

import numpy as np
import concourse.bass as bass
from concourse import mybir
from concourse.alu_op_type import AluOpType as ALU

F32 = mybir.dt.float32
BF16 = mybir.dt.bfloat16
ACT = mybir.ActivationFunctionType
AX = mybir.AxisListType.X

B, T, D = 8, 1024, 128
P = 128
NT = T // P
HALF = 512
LAYERS = 2
HEADS, DH, WIN = 8, 64, 64
INNER = HEADS * DH
PAIRS = HEADS // 2
HID = int(D * 4 * 2 / 3)
CHUNKS = [(0, 128), (128, 128), (256, HID - 256)]
KEYS = P + WIN
EPS = 1e-5
QK_SCALE = 8.0
CYCLES = 3
FF = 4 * D
TWO_PI = 6.283185307179586
PI2_A = 6.28125
PI2_B = float(np.float32(0.0019350051879882812))
PI2_C = TWO_PI - PI2_A - PI2_B
ROUND = 12582912.0
PI_IN = float(np.nextafter(np.float32(np.pi), np.float32(0)))

FRONT = {}
_at = 0
for _name, _cols in [("wk", D), ("wv", D), ("wr", D), ("wcr", D), ("wck", FF), ("wcv", FF),
                     ("cn1", 128), ("cn2", 64), ("cn3", 128), ("cn4", 128),
                     ("gc1", 64), ("gc2", 128), ("gc3", 128),
                     ("aq", D), ("ak", D), ("av", D), ("ao", D)]:
    FRONT[_name] = slice(_at, _at + _cols)
    _at += _cols
FRONT_COLS = _at

VEC = {n: i for i, n in enumerate(
    ["ln1_w", "ln1_b", "ln2_w", "ln2_b", "ts", "u", "cn_b1", "cn_b2", "cn_b3", "cn_b4",
     "gc_b1", "gc_b2", "gc_b3", "ar", "wave", "phase", "bq", "bk", "bv", "bo"])}
CST = {n: i for i, n in enumerate(["eps", "eps_sq", "tiny", "ln_1024", "half_pi"])}
DER = {n: i for i, n in enumerate(
    ["neg_ts", "one_plus_ts", "one_minus_ts", "half_gc_b3", "half_cn_b4", "ar7", "ar3",
     "inv_wave", "theta_q0", "theta_k0", "wave_eps"])}
LVEC = {n: i for i, n in enumerate(
    ["qs", "qs_r", "ks", "ks_r", "ln_g", "ln_b", "b1a0", "b1a1", "b1a2", "b1g0", "b1g1", "b1g2", "b2"])}
C_ID, C_TW, C_PAIR, C_HEAD = slice(0, 128), slice(128, 256), slice(256, 384), slice(384, 386)
C_CST = 386
CONST_COLS = C_CST + len(CST)
WQK_COLS = 4 * PAIRS * P
LAYER_COLS = WQK_COLS + INNER + PAIRS * D
MLP_COLS = 2 * HID + len(CHUNKS) * D


class Signal:

    def __init__(self, ctx, nc, name, per, raised=0):
        self.sem = ctx.enter_context(nc.semaphore(name))
        self.per = per
        self.raised = raised

    def at(self, turn, n):
        return turn * self.per + n + self.raised


def build(nc, x_d, front_d, vec_d, layer_d, mlp_d, lvec_d, const_d, table_d, mask_d, out_d):
    ctx = ExitStack()
    with ctx:
        def sb(name, shape, dt=F32):
            return ctx.enter_context(nc.sbuf_tensor(name, shape, dt))

        front = sb("front_w", [P, FRONT_COLS])
        vec = sb("vec", [P, len(VEC)])
        der = sb("derived_vec", [P, len(DER)])
        const = sb("const", [P, CONST_COLS])
        table = sb("rotary_table", [P, 4, T])
        mask = sb("mask", [P, P + 2 * KEYS], BF16)
        layer_w = sb("layer_w", [P, LAYER_COLS])
        mlp_w = sb("mlp_w", [P, MLP_COLS])
        lvec = sb("lvec", [P, len(LVEC)])
        ident = const[:, C_ID]
        twist = const[:, C_TW]
        pair_ones = const[:, C_PAIR]
        head_ones = const[:, C_HEAD]
        ident16 = mask[:, 0:P]
        band_mask, first_mask = mask[:, P:P + KEYS], mask[:, P + KEYS:]

        def w(name, rows=P):
            return front[0:rows, FRONT[name]]

        def v(name, rows=P):
            return vec[0:rows, VEC[name]:VEC[name] + 1]

        def dv(name):
            return der[:, DER[name]:DER[name] + 1]

        def cst(name):
            return const[:, C_CST + CST[name]:C_CST + CST[name] + 1]

        def lv(name, rows=P):
            return lvec[0:rows, LVEC[name]:LVEC[name] + 1]

        x_in = sb("x_in", [P, NT, D])
        x_mid = sb("x_mid", [P, NT, D])
        y = sb("y", [P, T])
        s_att = sb("s_att", [P, T])
        stats = sb("stats", [P, NT, 6])
        mv = sb("mean_var", [P, NT, 2])
        log_a = sb("log_a", [P, NT])
        seed = sb("seed", [P, 5])
        carrier = sb("carrier", [P, 1])
        log_b = sb("log_b", [P, NT])
        rstd = sb("rstd", [P, NT])
        rstd2 = sb("rstd2", [P, NT])
        norm_t = sb("norm_t", [P, NT, D])
        net = norm_t[:, :, :].rearrange("p n d -> p (n d)")
        k_c = sb("k_c", [P, T])
        r_c = sb("r_c", [P, T])
        e_a = sb("e_a", [P, T])
        e_b = sb("e_b", [P, T])
        log_d = sb("log_d", [P, T + 1])
        work = sb("work", [P, 8 * T + 3])
        at = [0]

        def cut(cols):
            at[0] += cols
            return work[:, at[0] - cols:at[0]]

        xn = cut(T)
        xn1 = cut(T)
        z_c = cut(T)
        v_c = cut(T)
        norm2_t = cut(T).rearrange("p (n d) -> p n d", n=NT)
        top = cut(T + 1)
        aa = cut(T + 1)
        h_pad = cut(T + 1)
        at[0] = 0
        rot = cut(4 * T).rearrange("p (i k n) -> p i k n", i=2, k=4)
        squares = cut(2 * T).rearrange("p (i k n) -> p i k n", i=2, k=2)
        k_un = cut(T).rearrange("p (i n) -> p i n", i=2)
        rn_k = cut(T).rearrange("p (i n) -> p i n", i=2)
        at[0] = 0
        o_t = cut(2 * T).rearrange("p (i n d) -> p i n d", i=2, n=NT)
        pt_win = cut(T).rearrange("p (i e c k) -> p i e c k", i=2, e=2, c=2)
        mean_c = sb("mean_c", [P, 1])
        g1 = sb("g1", [P, 1])
        g2 = sb("g2", [P, 1])
        tg = sb("tg", [P, 1])
        c0 = sb("c0", [P, 1])
        big = sb("big", [P, PAIRS * T + PAIRS * (T + WIN)])
        q_rot = big[:, 0:PAIRS * T].rearrange("p (h t) -> p h t", h=PAIRS)
        k_rot = big[:, PAIRS * T:].rearrange("p (h t) -> p h t", h=PAIRS)
        p_att = big[:, 0:NT * T].rearrange("p (k t) -> p k t", k=NT)
        ff = sb("ff", [P, PAIRS, T])
        v_win = sb("v_win", [P, NT, HEADS, DH + 1])
        v_att = ff[:, :, :].rearrange("p h t -> p (h t)")[:, 0:NT * (D + 1)].rearrange("p (n d) -> p n d", n=NT)
        p_win = sb("p_win", [P, 3, 2, 2 * P])
        h_s = sb("h_s", [P, T])
        rn_q = sb("rn_q", [P, PAIRS * NT * 2])
        top_s = sb("top_s", [P, 4, 2])
        neg_top = sb("neg_top", [P, 4, 2])
        rden = sb("rden", [P, 2, 2])
        rden_att = sb("rden_att", [P, NT])

        ps = ctx.enter_context(nc.psum_tensor("ps", [P, 8, HALF], F32))

        def both(n):
            return ps[:, n:n + 2, :]

        def flat(a):
            return a[:, :, :].rearrange("p (c n) d -> p c (n d)", c=2)

        def halves(a):
            return a.rearrange("p (c n) -> p c n", c=2)

        def sig(name, per=1, raised=0):
            return Signal(ctx, nc, name, per, raised)

        w_in = sig("w_in")
        ready0 = sig("setup_done")
        setup = sig("setup_step")
        x_loaded = sig("x_loaded", 16)
        lw_loaded = sig("lw_loaded", 16)
        mlp_loaded = sig("mlp_loaded", 32)
        out_sent = sig("out_sent", 16, raised=1)
        ln0_stats, ln0_mv, ln0_logs, ln0_logd, ln0_rstd = (
            sig("ln0_stats"), sig("ln0_mv"), sig("ln0_logs", 2), sig("ln0_logd"), sig("ln0_rstd", 2))
        xn_t, hn_t = sig("xn_t"), sig("hn_t")
        xn_ps, hn_ps = sig("xn_ps"), sig("hn_ps")
        xn_c, h_c = sig("xn_c"), sig("h_c")
        hpad0 = sig("hpad0")
        mix_a, mixed = sig("mix_a"), sig("mixed")
        k_ps, v_ps, r_ps, k_sb, v_sb = sig("k_ps"), sig("v_ps"), sig("r_ps"), sig("k_sb"), sig("v_sb")
        wkv = sig("wkv_step", 15)
        wkv_exp, wkv_ln, wkv_exp2, wkv_gate = sig("wkv_exp", 2), sig("wkv_ln"), sig("wkv_exp2", 2), sig("wkv_gate", 2)
        x1_ps, ln2_stats, ln2_mv, ln2_log, ln2_rstd = (
            sig("x1_ps"), sig("ln2_stats"), sig("ln2_mv"), sig("ln2_log"), sig("ln2_rstd"))
        h2_t, h2_ps, h2_c = sig("h2_t"), sig("h2_ps"), sig("h2_c")
        mix2 = sig("mix2", 3)
        kc_ps, kc_relu, kc_sq = sig("kc_ps", 4), sig("kc_relu", 4), sig("kc_sq", 4)
        rc_ps, vv_ps, rc_sb, s_mul, s_done = sig("rc_ps"), sig("vv_ps"), sig("rc_sb"), sig("s_mul"), sig("s_done")
        mean_done, gc_ps, gc_sb, gc_c0 = sig("mean_done"), sig("gc_ps", 3), sig("gc_sb", 3), sig("gc_c0")
        cn_ps, cn_sb = sig("cn_ps", 5 * CYCLES), sig("cn_sb", 4 * CYCLES)
        cycle = sig("cycle", 3 * CYCLES)
        gate0, prod0, prod0_ps, x_mid_done = sig("gate0"), sig("prod0", 2), sig("prod0_ps"), sig("x_mid_done", raised=1)
        ln3_stats, ln3_mv, ln3_log, ln3_rstd = sig("ln3_stats"), sig("ln3_mv"), sig("ln3_log"), sig("ln3_rstd")
        y_t, y_ps, y_c = sig("y_t"), sig("y_ps"), sig("y_c")
        qk_ps, theta, reduce_s, reduced = sig("qk_ps", 2), sig("theta", 2), sig("reduce_s", 10), sig("reduced", 2)
        va_ps, va_sb, abs_s, trig = sig("va_ps"), sig("va_sb"), sig("abs_s", 2), sig("trig", 4)
        sim_ps, sim_exp = sig("sim_ps", 2 * NT), sig("sim_exp", 2 * NT)
        pv_ps, pv_r, pv_sb = sig("pv_ps", NT), sig("pv_r", NT), sig("pv_sb", NT)
        at_ps, at_sb, ao_ps, ao_sb = sig("at_ps"), sig("at_sb"), sig("ao_ps"), sig("ao_sb")
        gate1, prod1, prod1_ps, out_done = sig("gate1"), sig("prod1", 2), sig("prod1_ps"), sig("out_done", raised=1)
        JOBS = PAIRS * 2
        STEPS = PAIRS * NT
        shifted = sig("shifted", 2)
        qk4_ps, vw_ps, vw_sb = sig("qk4_ps", 4 * JOBS), sig("vw_ps", NT), sig("vw_sb", NT)
        sq_sb, norm_ps, norm_ln, norm_ex = sig("sq_sb", 2 * JOBS), sig("norm_ps", JOBS), sig("norm_ln", JOBS), sig("norm_ex", JOBS)
        qn_ln, qn_ex, qn_cl = sig("qn_ln"), sig("qn_ex"), sig("qn_cl")
        rotated, q_sum, k_sum, k_done = sig("rotated", 4 * JOBS), sig("q_sum", JOBS), sig("k_sum", JOBS), sig("k_done", JOBS)
        s_ps, s_top, s_neg, p_sb = sig("s_ps", STEPS), sig("s_top", STEPS), sig("s_neg", STEPS), sig("p_sb", STEPS)
        pt_ps = sig("pt_ps", STEPS)
        pt_sb = [sig("pt_sb_act", STEPS // 2), sig("pt_sb_dve", STEPS // 2)]
        o_ps, o_r, o_sb = sig("o_ps", STEPS), sig("o_r", STEPS), sig("o_sb", STEPS)
        ot_ps, ot_sb = sig("ot_ps", 2 * PAIRS), sig("ot_sb", 2 * PAIRS)
        wo_ps, y_mid = sig("wo_ps", raised=1), sig("y_mid")
        shifted2, lnl_tp, lnl_stats, lnl_mv, lnl_log, lnl_rstd = (
            sig("shifted2"), sig("lnl_tp"), sig("lnl_stats"), sig("lnl_mv"), sig("lnl_log"), sig("lnl_rstd"))
        lnl_t, lnl_ps, lnl_c = sig("lnl_t"), sig("lnl_ps"), sig("lnl_c")
        up_ps, gelu_sb, up_sb = sig("up_ps", 3), sig("gelu_sb", 3), sig("up_sb", 3)
        down_ps, y_done = sig("down_ps"), sig("y_done", raised=1)

        block = ctx.enter_context(nc.Block())

        @block.sync
        def _(sp):
            sp.dma_start(front[:, :], front_d).then_inc(w_in.sem, 16)
            sp.dma_start(vec[:, :], vec_d).then_inc(w_in.sem, 16)
            sp.dma_start(const[:, :], const_d).then_inc(w_in.sem, 16)
            sp.dma_start(table[:, :, :], table_d).then_inc(w_in.sem, 16)
            sp.dma_start(work[:, 0:P + 2 * KEYS], mask_d).then_inc(w_in.sem, 16)
            with sp.Fori(0, B) as b:
                sp.wait_ge(x_mid_done.sem, x_mid_done.at(b, 0))
                sp.dma_start(x_in[:, :, :], x_d[b].rearrange("(n p) c -> p n c", p=P)).then_inc(x_loaded.sem, 16)
                with sp.Fori(0, LAYERS) as l:
                    li = b * LAYERS + l
                    sp.wait_ge(wo_ps.sem, wo_ps.at(li, 0))
                    sp.dma_start(layer_w[:, :], layer_d[l]).then_inc(lw_loaded.sem, 16)
                    sp.wait_ge(y_done.sem, y_done.at(li, 0))
                    sp.dma_start(mlp_w[:, :], mlp_d[l]).then_inc(mlp_loaded.sem, 16)
                    sp.dma_start(lvec[:, :], lvec_d[l]).then_inc(mlp_loaded.sem, 16)
                sp.wait_ge(out_done.sem, out_done.at(b, 1))
                sp.dma_start(out_d[b].rearrange("(n p) c -> p n c", p=P), norm_t[:, :, :]).then_inc(out_sent.sem, 16)
            sp.wait_ge(out_sent.sem, out_sent.at(B, 0))

        @block.tensor
        def _(pe):
            mm = nc.tensor.matmul

            def two(bank, lhsT, rhs, rows=P, start=True, stop=True):
                for c in range(2):
                    last = mm(ps[0:rows, bank + c, :], lhsT, rhs[:, c * HALF:(c + 1) * HALF], start=start, stop=stop)
                return last

            def turn8(bank, tiles):
                for i in range(NT):
                    last = nc.tensor.transpose(ps[:, bank + i // 4, (i % 4) * P:(i % 4 + 1) * P], tiles(i), ident)
                return last

            pe.wait_ge(ready0.sem, 1)

            def front_part(b):
                pe.wait_ge(out_done.sem, out_done.at(b, 0))
                pe.wait_ge(hn_t.sem, hn_t.at(b, 1))
                turn8(0, lambda i: norm2_t[:, i, :]).then_inc(hn_ps.sem, 1)
                pe.wait_ge(xn_t.sem, xn_t.at(b, 1))
                turn8(4, lambda i: norm_t[:, i, :]).then_inc(xn_ps.sem, 1)
                pe.wait_ge(mixed.sem, mixed.at(b, 1))
                two(0, w("wk"), z_c[:, :]).then_inc(k_ps.sem, 1)
                two(2, w("wv"), z_c[:, :]).then_inc(v_ps.sem, 1)
                pe.wait_ge(k_sb.sem, k_sb.at(b, 1))
                two(0, w("wr"), z_c[:, :]).then_inc(r_ps.sem, 1)
                pe.wait_ge(mean_done.sem, mean_done.at(b, 1))
                mm(ps[0:64, 6, 0:1], w("gc1"), mean_c[:, :], start=True, stop=True).then_inc(gc_ps.sem, 1)
                pe.wait_ge(gc_sb.sem, gc_sb.at(b, 1))
                mm(ps[:, 6, 1:2], w("gc2", 64), g1[0:64, :], start=True, stop=True).then_inc(gc_ps.sem, 1)
                pe.wait_ge(gc_sb.sem, gc_sb.at(b, 2))
                mm(ps[:, 6, 2:3], w("gc3", 32), g2[0:32, :], start=True, stop=True).then_inc(gc_ps.sem, 1)
                pe.wait_ge(gc_sb.sem, gc_sb.at(b, 3))
                for cy in range(CYCLES):
                    src = xn if cy == 0 else net
                    if cy == 0:
                        pe.wait_ge(xn_c.sem, xn_c.at(b, 1))
                    else:
                        pe.wait_ge(cycle.sem, cycle.at(b, 3 * cy))
                    two(4, w("cn1"), src[:, :]).then_inc(cn_ps.sem, 1)
                    pe.wait_ge(cn_sb.sem, cn_sb.at(b, 4 * cy + 1))
                    two(6, w("cn2"), ff[:, 0, :], rows=64).then_inc(cn_ps.sem, 1)
                    pe.wait_ge(cn_sb.sem, cn_sb.at(b, 4 * cy + 2))
                    two(4, w("cn3", 64), ff[0:64, 1, :]).then_inc(cn_ps.sem, 1)
                    pe.wait_ge(cn_sb.sem, cn_sb.at(b, 4 * cy + 3))
                    two(6, w("cn4", 32), ff[0:32, 2, :]).then_inc(cn_ps.sem, 1)
                    two(4, twist, src[:, :]).then_inc(cn_ps.sem, 1)
                pe.wait_ge(wkv.sem, wkv.at(b, 15))
                pe.wait_ge(wkv_gate.sem, wkv_gate.at(b, 2))
                turn8(0, lambda i: xn1[:, i * P:(i + 1) * P]).then_inc(x1_ps.sem, 1)
                pe.wait_ge(h2_t.sem, h2_t.at(b, 1))
                turn8(2, lambda i: norm2_t[:, i, :]).then_inc(h2_ps.sem, 1)
                pe.wait_ge(mix2.sem, mix2.at(b, 3))
                for j in range(4):
                    if j >= 2:
                        pe.wait_ge(kc_relu.sem, kc_relu.at(b, j - 1))
                    two(2 * (j % 2), w("wck")[:, j * P:(j + 1) * P], z_c[:, :]).then_inc(kc_ps.sem, 1)
                pe.wait_ge(kc_relu.sem, kc_relu.at(b, 3))
                two(0, w("wcr"), z_c[:, :]).then_inc(rc_ps.sem, 1)
                pe.wait_ge(kc_relu.sem, kc_relu.at(b, 4))
                for c in range(2):
                    for j in range(4):
                        pe.wait_ge(kc_sq.sem, kc_sq.at(b, j + 1))
                        last = mm(ps[:, 2 + c, :], w("wcv")[:, j * P:(j + 1) * P], ff[:, j, c * HALF:(c + 1) * HALF],
                                  start=(j == 0), stop=(j == 3))
                last.then_inc(vv_ps.sem, 1)
                pe.wait_ge(prod0.sem, prod0.at(b, 2))
                turn8(0, lambda i: k_c[:, i * P:(i + 1) * P]).then_inc(prod0_ps.sem, 1)
                pe.wait_ge(y_t.sem, y_t.at(b, 1))
                turn8(2, lambda i: norm_t[:, i, :]).then_inc(y_ps.sem, 1)
                pe.wait_ge(y_c.sem, y_c.at(b, 1))
                two(0, w("aq"), y[:, :]).then_inc(qk_ps.sem, 1)
                two(4, w("ak"), y[:, :]).then_inc(qk_ps.sem, 1)
                for i in range(NT):
                    last = mm(ps[:, 6 + i // 4, (i % 4) * P:(i % 4 + 1) * P], y[:, i * P:(i + 1) * P], w("av"),
                              start=True, stop=True)
                last.then_inc(va_ps.sem, 1)
                pe.wait_ge(trig.sem, trig.at(b, 4))
                for n in range(2 * NT):
                    c, kt = n // NT, n % NT
                    if n >= 4:
                        pe.wait_ge(sim_exp.sem, sim_exp.at(b, n - 3))
                    for f, (kf, qf) in enumerate([(e_b, e_a), (v_c, k_c)]):
                        last = mm(ps[:, n % 4, :], kf[:, kt * P:(kt + 1) * P], qf[:, c * HALF:(c + 1) * HALF],
                                  start=(f == 0), stop=(f == 1))
                    last.then_inc(sim_ps.sem, 1)
                pe.wait_ge(va_sb.sem, va_sb.at(b, 1))
                for m in range(NT):
                    pe.wait_ge(sim_exp.sem, sim_exp.at(b, NT if m < NT // 2 else 2 * NT))
                    if m >= 4:
                        pe.wait_ge(pv_sb.sem, pv_sb.at(b, m - 3))
                    for kt in range(NT):
                        last = mm(ps[:, 4 + m % 4, 0:D + 1], p_att[:, kt, m * P:(m + 1) * P], v_att[:, kt, :],
                                  start=(kt == 0), stop=(kt == NT - 1))
                    last.then_inc(pv_ps.sem, 1)
                pe.wait_ge(pv_sb.sem, pv_sb.at(b, NT))
                turn8(0, lambda i: norm2_t[:, i, :]).then_inc(at_ps.sem, 1)
                pe.wait_ge(at_sb.sem, at_sb.at(b, 1))
                two(2, w("ao"), r_c[:, :]).then_inc(ao_ps.sem, 1)

            def layer_part(li):
                wqk = layer_w[:, 0:WQK_COLS].rearrange("p (k h d) -> p k h d", k=4, h=PAIRS)
                wv = layer_w[:, WQK_COLS:WQK_COLS + INNER]
                wo = layer_w[:, WQK_COLS + INNER:].rearrange("p (h d) -> p h d", h=PAIRS)
                w1 = mlp_w[:, 0:2 * HID]
                w2 = mlp_w[:, 2 * HID:].rearrange("p (j d) -> p j d", j=len(CHUNKS))
                pe.wait_ge(lw_loaded.sem, lw_loaded.at(li, 16))
                pe.wait_ge(y_done.sem, y_done.at(li, 0))
                pe.wait_ge(shifted.sem, shifted.at(li, 2))
                for i in range(JOBS):
                    hp, c = i // 2, i % 2
                    cols = h_s[:, c * HALF:(c + 1) * HALF]
                    for kind in range(4):
                        if i and kind % 2:
                            pe.wait_ge(rotated.sem, rotated.at(li, 4 * (i - 1) + kind + 1))
                        elif i:
                            pe.wait_ge(sq_sb.sem, sq_sb.at(li, 2 * (i - 1) + kind // 2 + 1))
                        mm(ps[:, kind, :], wqk[:, kind, hp, :], cols, start=True, stop=True).then_inc(qk4_ps.sem, 1)
                    if i >= 2:
                        pe.wait_ge(vw_sb.sem, vw_sb.at(li, i - 1))
                    mm(ps[:, 4 + i % 2, :], h_s[:, i * P:(i + 1) * P], wv, start=True, stop=True).then_inc(vw_ps.sem, 1)
                    pe.wait_ge(sq_sb.sem, sq_sb.at(li, 2 * i + 2))
                    if i:
                        pe.wait_ge(norm_ln.sem, norm_ln.at(li, i))
                    mm(ps[:, 6, :], pair_ones, squares[:, i % 2, 1, :], start=True, stop=True)
                    for t in range(4):
                        last = mm(ps[:, 7, i * 8 + 2 * t:i * 8 + 2 * t + 2],
                                  squares[:, i % 2, 0, t * P:(t + 1) * P], head_ones, start=True, stop=True)
                    last.then_inc(norm_ps.sem, 1)

                def scores(n):
                    hp, m = n // NT, n % NT
                    bank = 2 * (n % 2)
                    if n >= 2:
                        pe.wait_ge(p_sb.sem, p_sb.at(li, n - 1))
                    for e in range(2):
                        mm(ps[:, bank + e, 0:KEYS], ident16, first_mask if m == 0 else band_mask, start=True, stop=False)
                    for e in range(2):
                        rows = slice(e * DH, (e + 1) * DH)
                        last = mm(ps[:, bank + e, 0:KEYS], q_rot[rows, hp, m * P:(m + 1) * P],
                                  k_rot[rows, hp, m * P:m * P + KEYS], start=False, stop=True)
                    last.then_inc(s_ps.sem, 1)

                def turn_p(n):
                    m = n % NT
                    pe.wait_ge(p_sb.sem, p_sb.at(li, n + 1))
                    if n >= 2:
                        pe.wait_ge(pt_sb[n % 2].sem, pt_sb[n % 2].at(li, n // 2))
                    for e in range(2):
                        for ch in range(2):
                            if m or ch:
                                last = nc.tensor.transpose(ps[:, 4 + n % 2, (2 * e + ch) * P:(2 * e + ch + 1) * P],
                                                           p_win[:, n % 3, e, ch * P:(ch + 1) * P], ident)
                    last.then_inc(pt_ps.sem, 1)

                def values(n):
                    hp, m = n // NT, n % NT
                    pe.wait_ge(pt_sb[n % 2].sem, pt_sb[n % 2].at(li, n // 2 + 1))
                    if n >= 2:
                        pe.wait_ge(o_sb.sem, o_sb.at(li, n - 1))
                    for e in range(2):
                        for ch in range(2):
                            if m or ch:
                                last = mm(ps[:, 6 + n % 2, e * (DH + 1):(e + 1) * (DH + 1)], pt_win[:, n % 2, e, ch, :],
                                          v_win[:, m - 1 + ch, 2 * hp + e, :], start=(ch == 0 or m == 0), stop=(ch == 1))
                    last.then_inc(o_ps.sem, 1)

                def turn_o(hp):
                    pe.wait_ge(o_sb.sem, o_sb.at(li, NT * (hp + 1)))
                    done = min(NT * (hp + 1) + 3, STEPS)
                    for c in range(2):
                        pe.wait_ge(pt_sb[c].sem, pt_sb[c].at(li, (done + 1 - c) // 2))
                        for t in range(4):
                            last = nc.tensor.transpose(ps[:, 4 + c, t * P:(t + 1) * P], o_t[:, hp % 2, 4 * c + t, :], ident)
                        last.then_inc(ot_ps.sem, 1)

                pe.wait_ge(k_done.sem, k_done.at(li, JOBS))
                pe.wait_ge(q_sum.sem, q_sum.at(li, JOBS))
                pe.wait_ge(qn_ln.sem, qn_ln.at(li, 1))
                pe.wait_ge(vw_sb.sem, vw_sb.at(li, NT))
                for n in range(STEPS + 4):
                    if n < STEPS:
                        scores(n)
                    if 1 <= n <= STEPS:
                        if (n - 1) % NT == 3 and n - 1 >= NT:
                            pe.wait_ge(ot_sb.sem, ot_sb.at(li, 2 * ((n - 1) // NT)))
                        turn_p(n - 1)
                    if 2 <= n < STEPS + 2:
                        values(n - 2)
                    if n >= NT + 3 and (n - 3) % NT == 0:
                        turn_o((n - 3) // NT - 1)
                pe.wait_ge(ot_sb.sem, ot_sb.at(li, 2 * PAIRS))
                for c in range(2):
                    for hp in range(PAIRS):
                        last = mm(ps[:, c, :], wo[:, hp, :], ff[:, hp, c * HALF:(c + 1) * HALF],
                                  start=(hp == 0), stop=(hp == PAIRS - 1))
                last.then_inc(wo_ps.sem, 1)
                pe.wait_ge(shifted2.sem, shifted2.at(li, 1))
                turn8(2, lambda i: h_s[:, i * P:(i + 1) * P]).then_inc(lnl_tp.sem, 1)
                pe.wait_ge(lnl_t.sem, lnl_t.at(li, 1))
                turn8(4, lambda i: norm_t[:, i, :]).then_inc(lnl_ps.sem, 1)
                pe.wait_ge(mlp_loaded.sem, mlp_loaded.at(li, 32))
                pe.wait_ge(lnl_c.sem, lnl_c.at(li, 1))
                for j, (lo, n) in enumerate(CHUNKS):
                    if j == 2:
                        pe.wait_ge(up_sb.sem, up_sb.at(li, 1))
                    bank = 4 * (j % 2)
                    two(bank, w1[:, lo:lo + n], k_c[:, :], rows=n)
                    two(bank + 2, w1[:, HID + lo:HID + lo + n], k_c[:, :], rows=n).then_inc(up_ps.sem, 1)
                pe.wait_ge(up_sb.sem, up_sb.at(li, 3))
                for c in range(2):
                    for j, (lo, n) in enumerate(CHUNKS):
                        last = mm(ps[:, 4 + c, :], w2[0:n, j, :], ff[0:n, j, c * HALF:(c + 1) * HALF],
                                  start=(j == 0), stop=(j == len(CHUNKS) - 1))
                last.then_inc(down_ps.sem, 1)

            with pe.Fori(0, B) as b:
                front_part(b)
                with pe.Fori(0, LAYERS) as l:
                    layer_part(b * LAYERS + l)
                pe.wait_ge(prod1.sem, prod1.at(b, 2))
                turn8(0, lambda i: k_c[:, i * P:(i + 1) * P]).then_inc(prod1_ps.sem, 1)

        @block.scalar
        def _(act):
            fn = nc.scalar.activation
            act.wait_ge(ready0.sem, 1)

            def rsqrt_of(turn, have, log, out):
                act.wait_ge(have.sem, have.at(turn, 1))
                fn(log_a[:, :], mv[:, :, 1], ACT.Ln, bias=cst("eps")).then_inc(log.sem, 1)
                act.wait_ge(log.sem, log.at(turn, 1))
                fn(rstd[:, :], log_a[:, :], ACT.Exp, scale=-0.5).then_inc(out.sem, 1)

            def front_part(b):
                act.wait_ge(ln0_mv.sem, ln0_mv.at(b, 1))
                fn(log_a[:, :], mv[:, :, 1], ACT.Ln, bias=cst("eps")).then_inc(ln0_logs.sem, 1)
                fn(log_b[:, :], mv[:, :, 1], ACT.Ln, bias=cst("eps_sq"), scale=1.0 + EPS).then_inc(ln0_logs.sem, 1)
                act.wait_ge(ln0_logs.sem, ln0_logs.at(b, 1))
                fn(rstd[:, :], log_a[:, :], ACT.Exp, scale=-0.5).then_inc(ln0_rstd.sem, 1)
                act.wait_ge(ln0_logd.sem, ln0_logd.at(b, 1))
                fn(rstd2[:, :], log_b[:, :], ACT.Exp, scale=0.5).then_inc(ln0_rstd.sem, 1)
                act.wait_ge(hn_ps.sem, hn_ps.at(b, 1))
                fn(halves(h_pad[:, 1:T + 1]), both(0), ACT.Identity, bias=v("ln1_b"), scale=v("ln1_w")).then_inc(h_c.sem, 1)
                act.wait_ge(k_ps.sem, k_ps.at(b, 1))
                fn(halves(k_c[:, :]), both(0), ACT.Copy).then_inc(k_sb.sem, 1)
                act.wait_ge(v_ps.sem, v_ps.at(b, 1))
                fn(halves(v_c[:, :]), both(2), ACT.Copy).then_inc(v_sb.sem, 1)
                act.wait_ge(wkv.sem, wkv.at(b, 2))
                fn(e_a[:, :], e_a[:, :], ACT.Exp).then_inc(wkv_exp.sem, 1)
                act.wait_ge(wkv.sem, wkv.at(b, 3))
                fn(e_b[:, :], e_b[:, :], ACT.Exp).then_inc(wkv_exp.sem, 1)
                act.wait_ge(wkv.sem, wkv.at(b, 4))
                fn(log_d[:, 1:T + 1], e_a[:, :], ACT.Ln).then_inc(wkv_ln.sem, 1)
                act.wait_ge(wkv.sem, wkv.at(b, 7))
                fn(e_a[:, :], e_a[:, :], ACT.Exp).then_inc(wkv_exp2.sem, 1)
                act.wait_ge(wkv.sem, wkv.at(b, 8))
                fn(e_b[:, :], e_b[:, :], ACT.Exp).then_inc(wkv_exp2.sem, 1)
                fn(log_d[:, 1:T + 1], z_c[:, :], ACT.Sigmoid, bias=v("u")).then_inc(wkv_gate.sem, 1)
                act.wait_ge(r_ps.sem, r_ps.at(b, 1))
                fn(halves(r_c[:, :]), both(0), ACT.Sigmoid).then_inc(wkv_gate.sem, 1)
                act.wait_ge(gc_ps.sem, gc_ps.at(b, 1))
                fn(g1[0:64, :], ps[0:64, 6, 0:1], ACT.Gelu, bias=v("gc_b1", 64), scale=1.0 / T).then_inc(gc_sb.sem, 1)
                act.wait_ge(gc_ps.sem, gc_ps.at(b, 2))
                fn(g2[0:32, :], ps[0:32, 6, 1:2], ACT.Gelu, bias=v("gc_b2", 32)).then_inc(gc_sb.sem, 1)
                act.wait_ge(gc_ps.sem, gc_ps.at(b, 3))
                fn(tg[:, :], ps[:, 6, 2:3], ACT.Tanh, bias=dv("half_gc_b3"), scale=0.5).then_inc(gc_sb.sem, 1)
                for cy in range(CYCLES):
                    act.wait_ge(cn_ps.sem, cn_ps.at(b, 5 * cy + 1))
                    fn(halves(ff[:, 0, :]), both(4), ACT.Gelu, bias=v("cn_b1")).then_inc(cn_sb.sem, 1)
                    act.wait_ge(cn_ps.sem, cn_ps.at(b, 5 * cy + 2))
                    fn(halves(ff[0:64, 1, :]), ps[0:64, 6:8, :], ACT.Gelu, bias=v("cn_b2", 64)).then_inc(cn_sb.sem, 1)
                    act.wait_ge(cn_ps.sem, cn_ps.at(b, 5 * cy + 3))
                    fn(halves(ff[0:32, 2, :]), ps[0:32, 4:6, :], ACT.Gelu, bias=v("cn_b3", 32)).then_inc(cn_sb.sem, 1)
                    act.wait_ge(cn_ps.sem, cn_ps.at(b, 5 * cy + 4))
                    if cy:
                        act.wait_ge(cycle.sem, cycle.at(b, 3 * cy))
                    fn(halves(ff[:, 3, :]), both(6), ACT.Tanh, bias=dv("half_cn_b4"), scale=0.5).then_inc(cn_sb.sem, 1)
                rsqrt_of(b, ln2_mv, ln2_log, ln2_rstd)
                act.wait_ge(h2_ps.sem, h2_ps.at(b, 1))
                fn(halves(h_pad[:, 1:T + 1]), both(2), ACT.Identity, bias=v("ln2_b"), scale=v("ln2_w")).then_inc(h2_c.sem, 1)
                act.wait_ge(cycle.sem, cycle.at(b, 3 * CYCLES))
                for j in range(4):
                    act.wait_ge(kc_ps.sem, kc_ps.at(b, j + 1))
                    fn(halves(ff[:, j, :]), both(2 * (j % 2)), ACT.Relu).then_inc(kc_relu.sem, 1)
                act.wait_ge(rc_ps.sem, rc_ps.at(b, 1))
                fn(halves(r_c[:, :]), both(0), ACT.Sigmoid).then_inc(rc_sb.sem, 1)
                fn(e_b[:, :], net[:, :], ACT.Sigmoid).then_inc(gate0.sem, 1)
                rsqrt_of(b, ln3_mv, ln3_log, ln3_rstd)
                act.wait_ge(y_ps.sem, y_ps.at(b, 1))
                fn(halves(y[:, :]), both(2), ACT.Copy).then_inc(y_c.sem, 1)
                for n, (dst, bank, bias) in enumerate([(k_c, 0, "theta_q0"), (v_c, 4, "theta_k0")]):
                    act.wait_ge(qk_ps.sem, qk_ps.at(b, n + 1))
                    fn(halves(dst[:, :]), both(bank), ACT.Identity, bias=dv(bias), scale=dv("inv_wave")).then_inc(theta.sem, 1)
                act.wait_ge(va_ps.sem, va_ps.at(b, 1))
                fn(v_att[:, :, 0:D].rearrange("p (c n) d -> p c n d", c=2),
                   ps[:, 6:8, :].rearrange("p c (n d) -> p c n d", d=D), ACT.Copy).then_inc(va_sb.sem, 1)
                for n, (r, co) in enumerate([(k_c, e_a), (v_c, e_b)]):
                    act.wait_ge(reduced.sem, reduced.at(b, n + 1))
                    fn(co[:, :], r[:, :], ACT.Abs).then_inc(abs_s.sem, 1)
                    act.wait_ge(abs_s.sem, abs_s.at(b, n + 1))
                    fn(co[:, :], co[:, :], ACT.Sin, bias=cst("half_pi"), scale=-1.0).then_inc(trig.sem, 1)
                    fn(r[:, :], r[:, :], ACT.Sin).then_inc(trig.sem, 1)
                for n in range(2 * NT):
                    c, kt = n // NT, n % NT
                    act.wait_ge(sim_ps.sem, sim_ps.at(b, n + 1))
                    fn(p_att[:, kt, c * HALF:(c + 1) * HALF], ps[:, n % 4, :], ACT.Exp, scale=D ** -0.5).then_inc(sim_exp.sem, 1)
                act.wait_ge(at_ps.sem, at_ps.at(b, 1))
                fn(halves(r_c[:, :]), both(0), ACT.Identity, bias=v("bv")).then_inc(at_sb.sem, 1)
                act.wait_ge(ao_ps.sem, ao_ps.at(b, 1))
                fn(halves(s_att[:, :]), both(2), ACT.Identity, bias=v("bo")).then_inc(ao_sb.sem, 1)

            def layer_part(li, b):
                act.wait_ge(y_c.sem, y_c.at(b, 1))
                act.wait_ge(y_done.sem, y_done.at(li, 0))
                fn(h_s[0:64, :], y[0:64, :], ACT.Copy).then_inc(shifted.sem, 1)
                fn(h_s[64:P, 1:T], y[64:P, 0:T - 1], ACT.Copy).then_inc(shifted.sem, 1)
                for i in range(JOBS):
                    if i >= 2:
                        act.wait_ge(norm_ps.sem, norm_ps.at(li, i - 1))
                    for kind in range(2):
                        act.wait_ge(rotated.sem, rotated.at(li, 4 * i + 2 * kind + 1))
                        fn(squares[:, i % 2, kind, :], ps[:, 2 * kind, :], ACT.Square).then_inc(sq_sb.sem, 1)
                    act.wait_ge(vw_ps.sem, vw_ps.at(li, i + 1))
                    fn(v_win[:, i, :, 0:DH], ps[:, 4 + i % 2, :].rearrange("p (h d) -> p h d", h=HEADS), ACT.Copy).then_inc(vw_sb.sem, 1)
                    act.wait_ge(norm_ps.sem, norm_ps.at(li, i + 1))
                    if i >= 2:
                        act.wait_ge(k_done.sem, k_done.at(li, i - 1))
                    fn(rn_k[:, i % 2, :], ps[:, 6, :], ACT.Ln, bias=cst("tiny"), scale=2.0 ** 20).then_inc(norm_ln.sem, 1)
                    act.wait_ge(norm_ln.sem, norm_ln.at(li, i + 1))
                    fn(rn_k[:, i % 2, :], rn_k[:, i % 2, :], ACT.Exp, bias=cst("ln_1024"), scale=-0.5).then_inc(norm_ex.sem, 1)
                act.wait_ge(norm_ps.sem, norm_ps.at(li, JOBS))
                fn(rn_q[:, :], ps[:, 7, 0:PAIRS * NT * 2], ACT.Ln, bias=cst("tiny"), scale=2.0 ** 20).then_inc(qn_ln.sem, 1)
                act.wait_ge(qn_ln.sem, qn_ln.at(li, 1))
                fn(rn_q[:, :], rn_q[:, :], ACT.Exp, bias=cst("ln_1024"), scale=-0.5).then_inc(qn_ex.sem, 1)

                def exps(n):
                    hp, m = n // NT, n % NT
                    if n >= 3:
                        act.wait_ge(pt_ps.sem, pt_ps.at(li, n - 2))
                    act.wait_ge(s_neg.sem, s_neg.at(li, n + 1))
                    for e in range(2):
                        col = (hp * NT + m) * 2 + e
                        last = fn(p_win[:, n % 3, e, 2 * P - KEYS:], ps[:, 2 * (n % 2) + e, 0:KEYS], ACT.Exp,
                                  bias=neg_top[:, n % 4, e:e + 1], scale=rn_q[:, col:col + 1])
                    last.then_inc(p_sb.sem, 1)

                def copy_pt(n):
                    m = n % NT
                    act.wait_ge(pt_ps.sem, pt_ps.at(li, n + 1))
                    if n >= 2:
                        act.wait_ge(o_ps.sem, o_ps.at(li, n - 1))
                    lo = 0 if m else 1
                    fn(pt_win[:, 0, :, lo:, :], ps[:, 4, :].rearrange("p (e c k) -> p e c k", e=2, c=2)[:, :, lo:, :],
                       ACT.Copy).then_inc(pt_sb[0].sem, 1)

                for n in range(STEPS + 4):
                    if n < STEPS:
                        exps(n)
                    if 1 <= n <= STEPS and n % 2 == 1:
                        copy_pt(n - 1)
                    if n >= NT + 3 and (n - 3) % NT == 0:
                        hp = (n - 3) // NT - 1
                        for c in range(2):
                            act.wait_ge(ot_ps.sem, ot_ps.at(li, 2 * hp + c + 1))
                            fn(ff[:, hp, c * HALF:(c + 1) * HALF], ps[:, 4 + c, :], ACT.Copy).then_inc(ot_sb.sem, 1)
                act.wait_ge(y_mid.sem, y_mid.at(li, 1))
                fn(h_s[0:64, :], y[0:64, :], ACT.Copy)
                fn(h_s[64:P, 1:T], y[64:P, 0:T - 1], ACT.Copy).then_inc(shifted2.sem, 1)
                rsqrt_of(li, lnl_mv, lnl_log, lnl_rstd)
                act.wait_ge(mlp_loaded.sem, mlp_loaded.at(li, 32))
                act.wait_ge(lnl_ps.sem, lnl_ps.at(li, 1))
                fn(halves(k_c[:, :]), both(4), ACT.Identity, bias=lv("ln_b"), scale=lv("ln_g")).then_inc(lnl_c.sem, 1)
                for j, (lo, n) in enumerate(CHUNKS):
                    act.wait_ge(up_ps.sem, up_ps.at(li, j + 1))
                    dst = [e_a, e_b, r_c][j]
                    fn(halves(dst[0:n, :]), ps[0:n, 4 * (j % 2) + 2:4 * (j % 2) + 4, :], ACT.Gelu,
                       bias=lv(f"b1g{j}", n)).then_inc(gelu_sb.sem, 1)

            with act.Fori(0, B) as b:
                front_part(b)
                with act.Fori(0, LAYERS) as l:
                    layer_part(b * LAYERS + l, b)
                act.wait_ge(y_done.sem, y_done.at(b * LAYERS + LAYERS, 0))
                fn(e_a[:, :], y[:, :], ACT.Sigmoid).then_inc(gate1.sem, 1)

        @block.vector
        def _(dve):
            tt, ts_, stt = nc.vector.tensor_tensor, nc.vector.tensor_scalar, nc.vector.scalar_tensor_tensor
            scan = nc.vector.tensor_tensor_scan

            nc.vector.memset(h_s[64:P, 0:1], 0.0)
            for n, s in enumerate((out_sent, x_mid_done, out_done, wo_ps, y_done)):
                nc.vector.memset(seed[:, n:n + 1], 0.0).then_inc(s.sem, 1)
            for h in range(HEADS):
                nc.vector.memset(v_win[:, :, h, DH:DH + 1], 1.0)
            nc.vector.memset(p_win[:, :, :, 0:2 * P - KEYS], 0.0).then_inc(setup.sem, 1)
            dve.wait_ge(w_in.sem, 16 * 5)
            nc.vector.tensor_copy(mask[:, :], work[:, 0:P + 2 * KEYS])
            ts_(dv("neg_ts"), v("ts"), -1.0, None, ALU.mult)
            ts_(dv("one_plus_ts"), v("ts"), 1.0, None, ALU.add)
            ts_(dv("one_minus_ts"), v("ts"), -1.0, 1.0, ALU.mult, ALU.add)
            ts_(dv("half_gc_b3"), v("gc_b3"), 0.5, None, ALU.mult)
            ts_(dv("half_cn_b4"), v("cn_b4"), 0.5, None, ALU.mult)
            ts_(dv("ar7"), v("ar"), 0.7, None, ALU.mult)
            ts_(dv("ar3"), v("ar"), 0.3, None, ALU.mult)
            ts_(dv("wave_eps"), v("wave"), 1e-8, None, ALU.add).then_inc(setup.sem, 1)
            dve.wait_ge(setup.sem, 2)
            nc.vector.reciprocal(dv("inv_wave"), dv("wave_eps")).then_inc(setup.sem, 1)
            dve.wait_ge(setup.sem, 3)
            stt(dv("theta_q0"), v("bq"), dv("inv_wave"), v("phase"), ALU.mult, ALU.add)
            stt(dv("theta_k0"), v("bk"), dv("inv_wave"), v("phase"), ALU.mult, ALU.add).then_inc(setup.sem, 1)
            dve.wait_ge(setup.sem, 4)
            nc.vector.memset(top_s[:, :, :], 0.0).then_inc(ready0.sem, 1)
            dve.wait_ge(ready0.sem, 1)

            def moments(turn, src, have, done):
                for i in range(NT):
                    last = nc.vector.bn_stats(stats[:, i, :], src(i))
                last.then_inc(have.sem, 1)
                dve.wait_ge(have.sem, have.at(turn, 1))
                nc.vector.memset(carrier[:, :], 0.0)
                for i in range(NT):
                    last = nc.vector.bn_aggr(mv[:, i, :], stats[:, i, :])
                last.then_inc(done.sem, 1)

            def normalise(dst, src):
                for i in range(NT):
                    last = ts_(dst[:, i, :], src(i), mv[:, i, 0:1], rstd[:, i:i + 1], ALU.subtract, ALU.mult)
                return last

            def bank_tile(bank):
                return lambda i: ps[:, bank + i // 4, (i % 4) * P:(i % 4 + 1) * P]

            def front_part(b):
                for buf in (top, log_d, aa):
                    nc.vector.memset(buf[:, 0:1], 0.0)
                dve.wait_ge(x_loaded.sem, x_loaded.at(b, 16))
                moments(b, lambda i: x_in[:, i, :], ln0_stats, ln0_mv)
                dve.wait_ge(ln0_logs.sem, ln0_logs.at(b, 2))
                tt(log_b[:, :], log_a[:, :], log_b[:, :], ALU.subtract).then_inc(ln0_logd.sem, 1)
                dve.wait_ge(ln0_rstd.sem, ln0_rstd.at(b, 1))
                dve.wait_ge(out_sent.sem, out_sent.at(b, 0))
                normalise(norm_t, lambda i: x_in[:, i, :]).then_inc(xn_t.sem, 1)
                dve.wait_ge(ln0_rstd.sem, ln0_rstd.at(b, 2))
                dve.wait_ge(xn_t.sem, xn_t.at(b, 1))
                for i in range(NT):
                    last = ts_(norm2_t[:, i, :], norm_t[:, i, :], rstd2[:, i:i + 1], None, ALU.mult)
                last.then_inc(hn_t.sem, 1)
                ts_(h_pad[:, 0:1], v("ts"), 1.0, None, ALU.mult).then_inc(hpad0.sem, 1)
                dve.wait_ge(xn_ps.sem, xn_ps.at(b, 1))
                nc.vector.tensor_copy(halves(xn[:, :]), both(4)).then_inc(xn_c.sem, 1)
                dve.wait_ge(h_c.sem, h_c.at(b, 1))
                dve.wait_ge(hpad0.sem, hpad0.at(b, 1))
                ts_(e_a[:, :], h_pad[:, 0:T], dv("neg_ts"), None, ALU.mult).then_inc(mix_a.sem, 1)
                dve.wait_ge(mix_a.sem, mix_a.at(b, 1))
                stt(z_c[:, :], h_pad[:, 1:T + 1], dv("one_plus_ts"), e_a[:, :], ALU.mult, ALU.add).then_inc(mixed.sem, 1)
                dve.wait_ge(xn_c.sem, xn_c.at(b, 1))
                nc.vector.tensor_reduce(mean_c[:, :], xn[:, :], axis=AX, op=ALU.add).then_inc(mean_done.sem, 1)
                dve.wait_ge(k_sb.sem, k_sb.at(b, 1))
                scan(top[:, 1:T + 1], k_c[:, :], k_c[:, :], 0.0, ALU.max, ALU.max).then_inc(wkv.sem, 1)
                dve.wait_ge(wkv.sem, wkv.at(b, 1))
                tt(e_a[:, :], top[:, 0:T], top[:, 1:T + 1], ALU.subtract).then_inc(wkv.sem, 1)
                tt(e_b[:, :], k_c[:, :], top[:, 1:T + 1], ALU.subtract).then_inc(wkv.sem, 1)
                dve.wait_ge(wkv_exp.sem, wkv_exp.at(b, 2))
                scan(e_a[:, :], e_a[:, :], e_b[:, :], 1.0, ALU.mult, ALU.add).then_inc(wkv.sem, 1)
                dve.wait_ge(wkv_ln.sem, wkv_ln.at(b, 1))
                tt(top[:, 0:T], top[:, 0:T], log_d[:, 0:T], ALU.add).then_inc(wkv.sem, 1)
                dve.wait_ge(wkv.sem, wkv.at(b, 5))
                dve.wait_ge(r_ps.sem, r_ps.at(b, 1))
                tt(z_c[:, :], k_c[:, :], top[:, 0:T], ALU.subtract).then_inc(wkv.sem, 1)
                dve.wait_ge(wkv.sem, wkv.at(b, 6))
                ts_(e_a[:, :], z_c[:, :], -1.0, 0.0, ALU.mult, ALU.min).then_inc(wkv.sem, 1)
                ts_(e_b[:, :], z_c[:, :], 0.0, None, ALU.min).then_inc(wkv.sem, 1)
                dve.wait_ge(wkv_exp2.sem, wkv_exp2.at(b, 2))
                dve.wait_ge(v_sb.sem, v_sb.at(b, 1))
                tt(e_b[:, :], e_b[:, :], v_c[:, :], ALU.mult).then_inc(wkv.sem, 1)
                dve.wait_ge(wkv.sem, wkv.at(b, 9))
                scan(aa[:, 1:T + 1], e_a[:, :], e_b[:, :], 0.0, ALU.mult, ALU.add).then_inc(wkv.sem, 1)
                dve.wait_ge(wkv.sem, wkv.at(b, 10))
                tt(e_a[:, :], v_c[:, :], aa[:, 0:T], ALU.subtract).then_inc(wkv.sem, 1)
                dve.wait_ge(wkv.sem, wkv.at(b, 11))
                dve.wait_ge(wkv_gate.sem, wkv_gate.at(b, 1))
                tt(e_a[:, :], e_a[:, :], log_d[:, 1:T + 1], ALU.mult).then_inc(wkv.sem, 1)
                dve.wait_ge(wkv.sem, wkv.at(b, 12))
                tt(e_a[:, :], e_a[:, :], aa[:, 0:T], ALU.add).then_inc(wkv.sem, 1)
                dve.wait_ge(wkv.sem, wkv.at(b, 13))
                dve.wait_ge(wkv_gate.sem, wkv_gate.at(b, 2))
                tt(e_a[:, :], e_a[:, :], r_c[:, :], ALU.mult).then_inc(wkv.sem, 1)
                dve.wait_ge(wkv.sem, wkv.at(b, 14))
                tt(xn1[:, :], xn[:, :], e_a[:, :], ALU.add).then_inc(wkv.sem, 1)
                dve.wait_ge(gc_sb.sem, gc_sb.at(b, 3))
                ts_(c0[:, :], tg[:, :], dv("ar7"), 0.1, ALU.mult, ALU.add).then_inc(gc_c0.sem, 1)
                dve.wait_ge(gc_c0.sem, gc_c0.at(b, 1))
                dve.wait_ge(xn_ps.sem, xn_ps.at(b, 1))
                for cy in range(CYCLES):
                    src = xn if cy == 0 else net
                    dve.wait_ge(cn_sb.sem, cn_sb.at(b, 4 * cy + 4))
                    ts_(ff[:, 3, :], ff[:, 3, :], dv("ar3"), c0[:, :], ALU.mult, ALU.add).then_inc(cycle.sem, 1)
                    dve.wait_ge(cycle.sem, cycle.at(b, 3 * cy + 1))
                    dve.wait_ge(cn_ps.sem, cn_ps.at(b, 5 * cy + 5))
                    tt(halves(ff[:, 3, :]), halves(ff[:, 3, :]), both(4), ALU.mult).then_inc(cycle.sem, 1)
                    dve.wait_ge(cycle.sem, cycle.at(b, 3 * cy + 2))
                    tt(net[:, :], src[:, :], ff[:, 3, :], ALU.add).then_inc(cycle.sem, 1)
                dve.wait_ge(x1_ps.sem, x1_ps.at(b, 1))
                moments(b, bank_tile(0), ln2_stats, ln2_mv)
                dve.wait_ge(ln2_rstd.sem, ln2_rstd.at(b, 1))
                normalise(norm2_t, bank_tile(0)).then_inc(h2_t.sem, 1)
                dve.wait_ge(h2_c.sem, h2_c.at(b, 1))
                nc.vector.tensor_copy(h_pad[:, 0:1], h_pad[:, T:T + 1]).then_inc(mix2.sem, 1)
                dve.wait_ge(mix2.sem, mix2.at(b, 1))
                ts_(e_a[:, :], h_pad[:, 0:T], v("ts"), None, ALU.mult).then_inc(mix2.sem, 1)
                dve.wait_ge(mix2.sem, mix2.at(b, 2))
                stt(z_c[:, :], h_pad[:, 1:T + 1], dv("one_minus_ts"), e_a[:, :], ALU.mult, ALU.add).then_inc(mix2.sem, 1)
                dve.wait_ge(vv_ps.sem, vv_ps.at(b, 1))
                dve.wait_ge(rc_sb.sem, rc_sb.at(b, 1))
                tt(halves(k_c[:, :]), halves(r_c[:, :]), both(2), ALU.mult).then_inc(s_mul.sem, 1)
                dve.wait_ge(s_mul.sem, s_mul.at(b, 1))
                tt(k_c[:, :], k_c[:, :], xn1[:, :], ALU.add).then_inc(s_done.sem, 1)
                dve.wait_ge(s_done.sem, s_done.at(b, 1))
                tt(k_c[:, :], k_c[:, :], net[:, :], ALU.mult).then_inc(prod0.sem, 1)
                dve.wait_ge(prod0.sem, prod0.at(b, 1))
                dve.wait_ge(gate0.sem, gate0.at(b, 1))
                tt(k_c[:, :], k_c[:, :], e_b[:, :], ALU.mult).then_inc(prod0.sem, 1)
                dve.wait_ge(prod0_ps.sem, prod0_ps.at(b, 1))
                tt(flat(x_mid), flat(x_in), both(0), ALU.add).then_inc(x_mid_done.sem, 1)
                nc.vector.memset(v_att[:, :, D:D + 1], 1.0)
                dve.wait_ge(x_mid_done.sem, x_mid_done.at(b, 1))
                moments(b, lambda i: x_mid[:, i, :], ln3_stats, ln3_mv)
                dve.wait_ge(ln3_rstd.sem, ln3_rstd.at(b, 1))
                normalise(norm_t, lambda i: x_mid[:, i, :]).then_inc(y_t.sem, 1)
                for n, th in enumerate((k_c, v_c)):
                    s0 = 5 * n
                    dve.wait_ge(theta.sem, theta.at(b, n + 1))
                    ts_(z_c[:, :], th[:, :], 1.0 / TWO_PI, ROUND, ALU.mult, ALU.add).then_inc(reduce_s.sem, 1)
                    dve.wait_ge(reduce_s.sem, reduce_s.at(b, s0 + 1))
                    ts_(z_c[:, :], z_c[:, :], ROUND, None, ALU.subtract).then_inc(reduce_s.sem, 1)
                    for k, part in enumerate((PI2_A, PI2_B, PI2_C)):
                        dve.wait_ge(reduce_s.sem, reduce_s.at(b, s0 + 2 + k))
                        stt(th[:, :], z_c[:, :], -part, th[:, :], ALU.mult, ALU.add).then_inc(reduce_s.sem, 1)
                    dve.wait_ge(reduce_s.sem, reduce_s.at(b, s0 + 5))
                    ts_(th[:, :], th[:, :], PI_IN, -PI_IN, ALU.min, ALU.max).then_inc(reduced.sem, 1)
                for m in range(NT):
                    dve.wait_ge(pv_ps.sem, pv_ps.at(b, m + 1))
                    nc.vector.reciprocal(rden_att[:, m:m + 1], ps[:, 4 + m % 4, D:D + 1]).then_inc(pv_r.sem, 1)
                    dve.wait_ge(pv_r.sem, pv_r.at(b, m + 1))
                    ts_(norm2_t[:, m, :], ps[:, 4 + m % 4, 0:D], rden_att[:, m:m + 1], None, ALU.mult).then_inc(pv_sb.sem, 1)

            def layer_part(li):
                dve.wait_ge(mlp_loaded.sem, mlp_loaded.at(li, 32))
                dve.wait_ge(qk4_ps.sem, qk4_ps.at(li, 1))
                nc.vector.memset(k_rot[:, :, 0:WIN], 0.0)

                def normalise_keys(i):
                    hp, c = i // 2, i % 2
                    dve.wait_ge(k_sum.sem, k_sum.at(li, i + 1))
                    dve.wait_ge(norm_ex.sem, norm_ex.at(li, i + 1))
                    stt(k_rot[:, hp, WIN + c * HALF:WIN + (c + 1) * HALF], rn_k[:, i % 2, :], 1e12, k_un[:, i % 2, :],
                        ALU.min, ALU.mult).then_inc(k_done.sem, 1)

                for i in range(JOBS):
                    hp, c = i // 2, i % 2
                    if i >= 2:
                        dve.wait_ge(q_sum.sem, q_sum.at(li, i - 1))
                        dve.wait_ge(k_sum.sem, k_sum.at(li, i - 1))
                    for kind, scale in enumerate(("qs", "qs_r", "ks", "ks_r")):
                        dve.wait_ge(qk4_ps.sem, qk4_ps.at(li, 4 * i + kind + 1))
                        stt(rot[:, i % 2, kind, :], ps[:, kind, :], lv(scale), table[:, kind, c * HALF:(c + 1) * HALF],
                            ALU.mult, ALU.mult).then_inc(rotated.sem, 1)
                    if i:
                        normalise_keys(i - 1)
                normalise_keys(JOBS - 1)
                dve.wait_ge(qn_ex.sem, qn_ex.at(li, 1))
                ts_(rn_q[:, :], rn_q[:, :], 1e12, None, ALU.min).then_inc(qn_cl.sem, 1)
                dve.wait_ge(qn_cl.sem, qn_cl.at(li, 1))

                def tops(n):
                    hp, m = n // NT, n % NT
                    dve.wait_ge(s_ps.sem, s_ps.at(li, n + 1))
                    nc.vector.tensor_reduce(top_s[:, n % 4, :], ps[:, 2 * (n % 2):2 * (n % 2) + 2, 0:KEYS], axis=AX,
                                            op=ALU.max).then_inc(s_top.sem, 1)
                    dve.wait_ge(s_top.sem, s_top.at(li, n + 1))
                    col = (hp * NT + m) * 2
                    stt(neg_top[:, n % 4, :], top_s[:, n % 4, :], -1.0, rn_q[:, col:col + 2], ALU.mult, ALU.mult).then_inc(s_neg.sem, 1)

                def copy_pt(n):
                    dve.wait_ge(pt_ps.sem, pt_ps.at(li, n + 1))
                    if n >= 2:
                        dve.wait_ge(o_ps.sem, o_ps.at(li, n - 1))
                    nc.vector.tensor_copy(pt_win[:, 1, :, :, :],
                                          ps[:, 5, :].rearrange("p (e c k) -> p e c k", e=2, c=2)).then_inc(pt_sb[1].sem, 1)

                def outputs(n):
                    hp, m = n // NT, n % NT
                    dve.wait_ge(o_ps.sem, o_ps.at(li, n + 1))
                    o = ps[:, 6 + n % 2, 0:2 * (DH + 1)].rearrange("p (e d) -> p e d", e=2)
                    nc.vector.reciprocal(rden[:, n % 2, :], o[:, :, DH]).then_inc(o_r.sem, 1)
                    dve.wait_ge(o_r.sem, o_r.at(li, n + 1))
                    if m == 0 and hp >= 2:
                        dve.wait_ge(ot_ps.sem, ot_ps.at(li, 2 * (hp - 1)))
                    tt(o_t[:, hp % 2, m, :].rearrange("p (e d) -> p e d", e=2), o[:, :, 0:DH],
                       rden[:, n % 2, :].rearrange("p (e u) -> p e u", u=1).broadcast_to((P, 2, DH)), ALU.mult).then_inc(o_sb.sem, 1)

                for n in range(STEPS + 2):
                    if n < STEPS:
                        tops(n)
                    if 1 <= n <= STEPS and n % 2 == 0:
                        copy_pt(n - 1)
                    if n >= 2:
                        outputs(n - 2)
                dve.wait_ge(wo_ps.sem, wo_ps.at(li, 1))
                dve.wait_ge(shifted.sem, shifted.at(li, 2))
                tt(halves(y[:, :]), halves(y[:, :]), both(0), ALU.add).then_inc(y_mid.sem, 1)
                dve.wait_ge(lnl_tp.sem, lnl_tp.at(li, 1))
                moments(li, bank_tile(2), lnl_stats, lnl_mv)
                dve.wait_ge(lnl_rstd.sem, lnl_rstd.at(li, 1))
                normalise(norm_t, bank_tile(2)).then_inc(lnl_t.sem, 1)
                for j, (lo, n) in enumerate(CHUNKS):
                    dve.wait_ge(gelu_sb.sem, gelu_sb.at(li, j + 1))
                    g = [e_a, e_b, r_c][j]
                    stt(halves(ff[0:n, j, :]), ps[0:n, 4 * (j % 2):4 * (j % 2) + 2, :], lv(f"b1a{j}", n), halves(g[0:n, :]),
                        ALU.add, ALU.mult).then_inc(up_sb.sem, 1)
                dve.wait_ge(down_ps.sem, down_ps.at(li, 1))
                stt(halves(y[:, :]), both(4), lv("b2"), halves(y[:, :]), ALU.add, ALU.add).then_inc(y_done.sem, 1)

            with dve.Fori(0, B) as b:
                front_part(b)
                with dve.Fori(0, LAYERS) as l:
                    layer_part(b * LAYERS + l)
                dve.wait_ge(y_done.sem, y_done.at(b * LAYERS + LAYERS, 0))
                tt(k_c[:, :], s_att[:, :], y[:, :], ALU.mult).then_inc(prod1.sem, 1)
                dve.wait_ge(prod1.sem, prod1.at(b, 1))
                dve.wait_ge(gate1.sem, gate1.at(b, 1))
                tt(k_c[:, :], k_c[:, :], e_a[:, :], ALU.mult).then_inc(prod1.sem, 1)
                dve.wait_ge(prod1_ps.sem, prod1_ps.at(b, 1))
                tt(flat(norm_t), flat(x_mid), both(0), ALU.add).then_inc(out_done.sem, 1)

        @block.gpsimd
        def _(pool):
            add = nc.gpsimd.tensor_tensor
            with pool.Fori(0, B) as b:
                for j in range(4):
                    pool.wait_ge(kc_relu.sem, kc_relu.at(b, j + 1))
                    add(ff[:, j, :], ff[:, j, :], ff[:, j, :], ALU.mult).then_inc(kc_sq.sem, 1)
                with pool.Fori(0, LAYERS) as l:
                    li = b * LAYERS + l
                    for i in range(JOBS):
                        hp, c = i // 2, i % 2
                        pool.wait_ge(rotated.sem, rotated.at(li, 4 * i + 2))
                        add(q_rot[:, hp, c * HALF:(c + 1) * HALF], rot[:, i % 2, 0, :], rot[:, i % 2, 1, :], ALU.add).then_inc(q_sum.sem, 1)
                        pool.wait_ge(rotated.sem, rotated.at(li, 4 * i + 4))
                        if i >= 2:
                            pool.wait_ge(k_done.sem, k_done.at(li, i - 1))
                        add(k_un[:, i % 2, :], rot[:, i % 2, 2, :], rot[:, i % 2, 3, :], ALU.add).then_inc(k_sum.sem, 1)


def _pad_rows(a, rows=P, cols=None):
    a = np.asarray(a, np.float32)
    if a.ndim == 1:
        return _pad_rows(a[:, None], rows)[:, 0]
    out = np.zeros((rows, cols or a.shape[1]), np.float32)
    out[:a.shape[0], :a.shape[1]] = a
    return out


def _column(a, repeat=False):
    a = np.asarray(a, np.float32).reshape(-1)
    return np.repeat(a, P) if repeat else _pad_rows(a)


def _by_chunk(a):
    a = _pad_rows(a, -(-a.shape[0] // P) * P)
    return a.reshape(-1, P, a.shape[1]).transpose(1, 0, 2).reshape(P, -1)


def _constants():
    const = np.zeros((P, CONST_COLS), np.float32)
    const[:, C_ID] = np.eye(P)
    quarter = np.arange(P // 4)
    twist = np.zeros((P, P), np.float32)
    for to, frm, sign in [(0, 64, 1), (32, 96, -1), (64, 0, -1), (96, 32, 1)]:
        twist[frm + quarter, to + quarter] = sign
    const[:, C_TW] = twist
    head = np.arange(P) // DH
    const[:, C_PAIR] = head[:, None] == head[None, :]
    const[:, C_HEAD] = head[:, None] == np.arange(2)[None, :]
    for name, value in [("eps", EPS), ("eps_sq", EPS * EPS), ("tiny", 2.0 ** -64), ("ln_1024", np.log(1024.0)),
                        ("half_pi", np.pi / 2)]:
        const[:, C_CST + CST[name]] = value
    f = np.float32
    half = np.arange(0, DH, 2, dtype=f)
    freq = (f(1.0) / f(10000.0) ** (half / f(DH))).astype(f)
    t = np.arange(T, dtype=f)
    angle = (t[None, :] * freq[:, None]).astype(f)
    base = (half + f(0.4 * DH)) / f(1.4 * DH)
    scale = base[:, None].astype(f) ** ((t - T // 2) / f(WIN // 2))[None, :]
    cos, sin = np.cos(angle), np.sin(angle)
    sign_rows = lambda a: np.concatenate([-a, a, -a, a])
    table = np.stack([np.tile(cos * scale, (4, 1)) * f(QK_SCALE), sign_rows(sin * scale) * f(QK_SCALE),
                      np.tile(cos / scale, (4, 1)), sign_rows(sin / scale)], axis=1).astype(f)
    q, k = np.arange(P)[:, None], np.arange(KEYS)[None, :]
    band = (k >= q) & (k <= q + WIN)
    mask = np.concatenate([np.eye(P), np.where(band, 0.0, -1e30), np.where(band & (k >= WIN), 0.0, -1e30)], axis=1)
    return const, np.ascontiguousarray(table), mask.astype(f)


def _layout(i):
    f = lambda n: np.asarray(i[n], np.float32)
    A, G, C, W = "L0_attn_", "L0_ffn_", "L1_attn_", "L1_ffn_"
    wide = lambda a: np.repeat(a, P, axis=1)
    front = np.concatenate([
        f(A + "Wk").T, f(A + "Wv").T, f(A + "Wr").T, f(A + "Wcr").T, f(A + "Wck").T, _by_chunk(f(A + "Wcv").T),
        f(G + "cn_w1"), f(G + "cn_w2"), _pad_rows(f(G + "cn_w3"), cols=P), _pad_rows(wide(f(G + "cn_w4"))),
        f(G + "gc_w1"), _pad_rows(f(G + "gc_w2"), cols=P), _pad_rows(wide(f(G + "gc_w3"))),
        f(C + "Wq").T, f(C + "Wk").T, f(C + "Wv").T, f(C + "Wo").T], axis=1)
    vec = np.stack([_column(f(n), repeat=n.endswith(("cn_b4", "gc_b3", "range"))) for n in
                    [A + "ln1_w", A + "ln1_b", A + "ln2_w", A + "ln2_b", A + "time_shift", A + "time_first",
                     G + "cn_b1", G + "cn_b2", G + "cn_b3", G + "cn_b4", G + "gc_b1", G + "gc_b2", G + "gc_b3",
                     G + "adaptive_range", C + "wavelengths", C + "phase_bias", C + "bq", C + "bk", C + "bv", C + "bo"]], axis=1)
    swap = (np.arange(DH) + DH // 2) % DH
    layers, mlps, lvecs = [], [], []
    for l in range(LAYERS):
        wqkv = f(W + "wqkv")[l].reshape(D, 3, PAIRS, 2, DH)
        q, k, v = wqkv[:, 0], wqkv[:, 1], wqkv[:, 2]
        wqk = np.stack([q, q[..., swap], k, k[..., swap]], axis=1)
        layers.append(np.concatenate([wqk.reshape(D, -1), v.reshape(D, -1), _by_chunk(f(W + "wo")[l])], axis=1))
        mlps.append(np.concatenate([f(W + "w1")[l], _by_chunk(f(W + "w2")[l])], axis=1))
        qs, ks, b1 = f(W + "q_scale")[l], f(W + "k_scale")[l], f(W + "b1")[l]
        two = lambda a: np.concatenate([a, a])
        lvecs.append(np.stack(
            [two(qs), two(qs[swap]), two(ks), two(ks[swap]), f(W + "ln_g")[l], f(W + "ln_b")[l]]
            + [_column(b1[o + lo:o + lo + n]) for o in (0, HID) for lo, n in CHUNKS] + [f(W + "b2")[l]], axis=1))
    return front, vec, np.stack(layers), np.stack(mlps), np.stack(lvecs)


def kernel(**inputs):
    import concourse.bacc as bacc
    from concourse.bass_utils import run_bass_kernel_spmd

    front, vec, layers, mlps, lvecs = _layout(inputs)
    const, table, mask = _constants()
    arrays = {"x": np.asarray(inputs["L0_attn_x"]), "front": front, "vec": vec, "layers": layers, "mlps": mlps,
              "lvecs": lvecs, "const": const, "table": table, "mask": mask}
    arrays = {"in_" + n: np.ascontiguousarray(a) for n, a in arrays.items()}
    nc = bacc.Bacc("TRN2", target_bir_lowering=False, num_devices=1)
    args = [nc.dram_tensor(n, a.shape, mybir.dt.from_np(a.dtype), kind="ExternalInput").ap() for n, a in arrays.items()]
    out = nc.dram_tensor("out", (B, T, D), F32, kind="ExternalOutput").ap()
    build(nc, *args, out)
    r = run_bass_kernel_spmd(nc, [arrays], core_ids=[0])
    return r.results[0]["out"]
```

```python
from contextlib import ExitStack

import numpy as np
import concourse.bass as bass
from concourse import mybir
from concourse.alu_op_type import AluOpType as ALU

F32 = mybir.dt.float32
BF16 = mybir.dt.bfloat16
ACT = mybir.ActivationFunctionType
AX = mybir.AxisListType.X

B, T, D = 8, 1024, 128
P = 128
NT = T // P
HALF = 512
LAYERS = 2
HEADS, DH, WIN = 8, 64, 64
INNER = HEADS * DH
PAIRS = HEADS // 2
HID = int(D * 4 * 2 / 3)
CHUNKS = [(0, 128), (128, 128), (256, HID - 256)]
KEYS = P + WIN
EPS = 1e-5
QK_SCALE = 8.0
CYCLES = 3
FF = 4 * D
TWO_PI = 6.283185307179586
PI2_A = 6.28125
PI2_B = float(np.float32(0.0019350051879882812))
PI2_C = TWO_PI - PI2_A - PI2_B
ROUND = 12582912.0
PI_IN = float(np.nextafter(np.float32(np.pi), np.float32(0)))

FRONT = {}
_at = 0
for _name, _cols in [("wk", D), ("wv", D), ("wr", D), ("wcr", D), ("wck", FF), ("wcv", FF),
                     ("cn1", 128), ("cn2", 64), ("cn3", 128), ("cn4", 128),
                     ("gc1", 64), ("gc2", 128), ("gc3", 128),
                     ("aq", D), ("ak", D), ("av", D), ("ao", D)]:
    FRONT[_name] = slice(_at, _at + _cols)
    _at += _cols
FRONT_COLS = _at

VEC = {n: i for i, n in enumerate(
    ["ln1_w", "ln1_b", "ln2_w", "ln2_b", "ts", "u", "cn_b1", "cn_b2", "cn_b3", "cn_b4",
     "gc_b1", "gc_b2", "gc_b3", "ar", "wave", "phase", "bq", "bk", "bv", "bo"])}
CST = {n: i for i, n in enumerate(["eps", "eps_sq", "tiny", "ln_1024", "half_pi"])}
DER = {n: i for i, n in enumerate(
    ["neg_ts", "one_plus_ts", "one_minus_ts", "half_gc_b3", "half_cn_b4", "ar7", "ar3",
     "inv_wave", "theta_q0", "theta_k0", "wave_eps", "half_u"])}
LVEC = {n: i for i, n in enumerate(
    ["qs", "qs_r", "ks", "ks_r", "ln_g", "ln_b", "b1a0", "b1a1", "b1a2", "b1g0", "b1g1", "b1g2", "b2"])}
C_ID, C_TW, C_PAIR, C_HEAD = slice(0, 128), slice(128, 256), slice(256, 384), slice(384, 386)
C_CST = 386
CONST_COLS = C_CST + len(CST)
WQK_COLS = 4 * PAIRS * P
LAYER_COLS = WQK_COLS + INNER + PAIRS * D
MLP_COLS = 2 * HID + len(CHUNKS) * D


class Signal:

    def __init__(self, ctx, nc, name, per, raised=0):
        self.sem = ctx.enter_context(nc.semaphore(name))
        self.per = per
        self.raised = raised

    def at(self, turn, n):
        return turn * self.per + n + self.raised


def build(nc, x_d, front_d, vec_d, layer_d, mlp_d, lvec_d, const_d, table_d, mask_d, out_d):
    ctx = ExitStack()
    with ctx:
        def sb(name, shape, dt=F32):
            return ctx.enter_context(nc.sbuf_tensor(name, shape, dt))

        front = sb("front_w", [P, FRONT_COLS])
        vec = sb("vec", [P, len(VEC)])
        der = sb("derived_vec", [P, len(DER)])
        const = sb("const", [P, CONST_COLS])
        table = sb("rotary_table", [P, 4, T])
        mask = sb("mask", [P, P + 2 * KEYS], BF16)
        layer_w = sb("layer_w", [P, LAYER_COLS])
        mlp_w = sb("mlp_w", [P, MLP_COLS])
        lvec = sb("lvec", [P, len(LVEC)])
        ident = const[:, C_ID]
        twist = const[:, C_TW]
        pair_ones = const[:, C_PAIR]
        head_ones = const[:, C_HEAD]
        ident16 = mask[:, 0:P]
        band_mask, first_mask = mask[:, P:P + KEYS], mask[:, P + KEYS:]

        def w(name, rows=P):
            return front[0:rows, FRONT[name]]

        def v(name, rows=P):
            return vec[0:rows, VEC[name]:VEC[name] + 1]

        def dv(name):
            return der[:, DER[name]:DER[name] + 1]

        def cst(name):
            return const[:, C_CST + CST[name]:C_CST + CST[name] + 1]

        def lv(name, rows=P):
            return lvec[0:rows, LVEC[name]:LVEC[name] + 1]

        x_in = sb("x_in", [P, NT, D])
        x_mid = sb("x_mid", [P, NT, D])
        y = sb("y", [P, T])
        s_att = sb("s_att", [P, T])
        stats = sb("stats", [P, 2, NT, 6])
        mv = sb("mean_var", [P, 2, NT, 2])
        log_a = sb("log_a", [P, 2, NT])
        seed = sb("seed", [P, 5])
        carrier = sb("carrier", [P, 2])
        log_b = sb("log_b", [P, NT])
        rstd = sb("rstd", [P, 2, NT])
        rstd2 = sb("rstd2", [P, NT])
        xn = sb("xn", [P, T])
        xn1 = sb("xn1", [P, T])
        k_c = sb("k_c", [P, T])
        v_c = sb("v_c", [P, T])
        r_c = sb("r_c", [P, T])
        z_c = sb("z_c", [P, T])
        e_a = sb("e_a", [P, T])
        e_b = sb("e_b", [P, T])
        top = sb("top", [P, T + 1])
        aa = sb("aa", [P, T + 1])
        h_pad = sb("h_pad", [P, T + 1])

        def as_t(a):
            return a[:, 0:T].rearrange("p (n d) -> p n d", n=NT)

        xn_tt, hn_tt, y_tt, o_tt, out_tt = as_t(top), as_t(e_b), as_t(z_c), as_t(h_pad), as_t(top)
        relus = [k_c, v_c, aa, top]
        work = sb("work", [P, 5 * T])
        at = [0]

        def cut(cols):
            at[0] += cols
            return work[:, at[0] - cols:at[0]]

        rot = cut(4 * T).rearrange("p (i k n) -> p i k n", i=2, k=4)
        rn_k = cut(T).rearrange("p (i n) -> p i n", i=2)
        at[0] = 0
        o_t = cut(2 * T).rearrange("p (i n d) -> p i n d", i=2, n=NT)
        pt_win = cut(3 * HALF).rearrange("p (i e c k) -> p i e c k", i=3, e=2, c=2)
        mean_c = sb("mean_c", [P, 1])
        g1 = sb("g1", [P, 1])
        g2 = sb("g2", [P, 1])
        tg = sb("tg", [P, 1])
        c0 = sb("c0", [P, 1])
        big = sb("big", [P, PAIRS * T + PAIRS * (T + WIN)])
        q_rot = big[:, 0:PAIRS * T].rearrange("p (h t) -> p h t", h=PAIRS)
        k_rot = big[:, PAIRS * T:].rearrange("p (h t) -> p h t", h=PAIRS)
        p_att = big[:, 0:NT * T].rearrange("p (k t) -> p k t", k=NT)
        ln_t = as_t(big)
        ln_c = big[:, T:2 * T]
        gelus = big[:, 2 * T:2 * T + 3 * HALF].rearrange("p (i n) -> p i n", i=3)
        ff = sb("ff", [P, PAIRS, T])
        v_win = sb("v_win", [P, NT, HEADS, DH + 1])
        squares = ff[:, :, :].rearrange("p h t -> p (h t)")[:, 0:2 * T].rearrange("p (i k n) -> p i k n", i=2, k=2)
        v_att = ff[:, :, :].rearrange("p h t -> p (h t)")[:, 0:NT * (D + 1)].rearrange("p (n d) -> p n d", n=NT)
        p_win = sb("p_win", [P, 2, 2, 2 * P])
        h_s = sb("h_s", [P, T])
        rn_q = sb("rn_q", [P, PAIRS * NT * 2])
        top_s = sb("top_s", [P, 4, 2])
        neg_top = sb("neg_top", [P, 4, 2])
        rden = sb("rden", [P, 2, 2])
        rden_att = sb("rden_att", [P, NT])

        ps = ctx.enter_context(nc.psum_tensor("ps", [P, 8, HALF], F32))

        def both(n):
            return ps[:, n:n + 2, :]

        def flat(a):
            return a[:, :, :].rearrange("p (c n) d -> p c (n d)", c=2)

        def halves(a):
            return a.rearrange("p (c n) -> p c n", c=2)

        def sig(name, per=1, raised=0):
            return Signal(ctx, nc, name, per, raised)

        w_in = sig("w_in")
        ready0 = sig("setup_done")
        setup = sig("setup_step")
        x_loaded = sig("x_loaded", 16)
        lw_loaded = sig("lw_loaded", 16)
        mlp_loaded = sig("mlp_loaded", 32)
        out_sent = sig("out_sent", 16, raised=1)
        ln0_stats, ln0_mv, ln0_logs, ln0_logd, ln0_rstd = (
            sig("ln0_stats"), sig("ln0_mv"), sig("ln0_logs", 2), sig("ln0_logd"), sig("ln0_rstd", 2))
        xn_t, hn_t = sig("xn_t"), sig("hn_t")
        xn_ps, hn_ps = sig("xn_ps"), sig("hn_ps")
        xn_c, h_c = sig("xn_c"), sig("h_c")
        hpad0 = sig("hpad0")
        mix_a, mixed = sig("mix_a"), sig("mixed")
        k_ps, v_ps, r_ps, k_sb, v_sb = sig("k_ps"), sig("v_ps"), sig("r_ps"), sig("k_sb"), sig("v_sb")
        wkv = sig("wkv_step", 15)
        wkv_exp, wkv_ln, wkv_exp2, wkv_gate, r_sb = (
            sig("wkv_exp", 2), sig("wkv_ln"), sig("wkv_exp2", 2), sig("wkv_gate"), sig("r_sb"))
        x1_ps, ln2_stats, ln2_mv, ln2_log, ln2_rstd = (
            sig("x1_ps"), sig("ln2_stats"), sig("ln2_mv"), sig("ln2_log"), sig("ln2_rstd"))
        h2_t, h2_ps, h2_c = sig("h2_t"), sig("h2_ps"), sig("h2_c")
        mix2 = sig("mix2", 3)
        kc_ps, kc_relu, kc_sq = sig("kc_ps", 4), sig("kc_relu", 4), sig("kc_sq", 4)
        rc_ps, vv_ps, rc_sb, s_mul, s_done = sig("rc_ps"), sig("vv_ps"), sig("rc_sb"), sig("s_mul"), sig("s_done")

        mean_done, gc_ps, gc_sb, gc_c0 = sig("mean_done"), sig("gc_ps", 3), sig("gc_sb", 3), sig("gc_c0")
        cn_ps, cn_sb = sig("cn_ps", 5 * CYCLES), sig("cn_sb", 4 * CYCLES)
        cycle = sig("cycle", 3 * CYCLES)
        gate0, prod0, prod0_ps, x_mid_done = sig("gate0"), sig("prod0", 2), sig("prod0_ps"), sig("x_mid_done", raised=1)
        ln3_stats, ln3_mv, ln3_log, ln3_rstd = sig("ln3_stats"), sig("ln3_mv"), sig("ln3_log"), sig("ln3_rstd")
        y_t, y_ps, y_c = sig("y_t"), sig("y_ps"), sig("y_c")
        qk_ps, theta, reduce_s, reduced = sig("qk_ps", 2), sig("theta", 2), sig("reduce_s", 10), sig("reduced", 2)
        va_ps, va_sb, abs_s, trig = sig("va_ps"), sig("va_sb"), sig("abs_s", 2), sig("trig", 4)
        sim_ps, sim_exp = sig("sim_ps", 2 * NT), sig("sim_exp", 2 * NT)
        pv_ps, pv_r, pv_sb = sig("pv_ps", NT), sig("pv_r", NT), sig("pv_sb", NT)
        at_ps, at_sb, ao_ps, ao_sb = sig("at_ps"), sig("at_sb"), sig("ao_ps"), sig("ao_sb")
        gate1, prod1, prod1_ps, out_done = sig("gate1"), sig("prod1", 2), sig("prod1_ps"), sig("out_done", raised=1)
        JOBS = PAIRS * 2
        STEPS = PAIRS * NT
        shifted = sig("shifted", 2)
        qk4_ps, vw_ps, vw_sb = sig("qk4_ps", 4 * JOBS), sig("vw_ps", NT), sig("vw_sb", NT)
        sq_sb, norm_ps, norm_ln, norm_ex = sig("sq_sb", 2 * JOBS), sig("norm_ps", JOBS), sig("norm_ln", JOBS), sig("norm_ex", JOBS)
        qn_ln, qn_ex, qn_cl = sig("qn_ln", JOBS), sig("qn_ex"), sig("qn_cl")
        rotated, q_sum, k_sum, k_done = sig("rotated", 4 * JOBS), sig("q_sum", JOBS), sig("k_sum", JOBS), sig("k_done", JOBS)
        s_ps, s_top, s_neg, p_sb = sig("s_ps", STEPS), sig("s_top", STEPS), sig("s_neg", STEPS), sig("p_sb", STEPS)
        pt_ps = sig("pt_ps", STEPS)
        pt_sb = [sig("pt_sb_act", STEPS // 2), sig("pt_sb_dve", STEPS // 2)]
        o_ps, o_r, o_sb = sig("o_ps", STEPS), sig("o_r", STEPS), sig("o_sb", STEPS)
        ot_ps, ot_sb = sig("ot_ps", 2 * PAIRS), sig("ot_sb", 2 * PAIRS)
        wo_ps, y_mid = sig("wo_ps", raised=1), sig("y_mid")
        shifted2, lnl_tp, lnl_stats, lnl_mv, lnl_log, lnl_rstd = (
            sig("shifted2"), sig("lnl_tp"), sig("lnl_stats"), sig("lnl_mv"), sig("lnl_log"), sig("lnl_rstd"))
        lnl_t, lnl_ps, lnl_c = sig("lnl_t"), sig("lnl_ps"), sig("lnl_c")
        UNITS = 2 * len(CHUNKS)
        up_ps, gelu_sb, up_sb = sig("up_ps", UNITS), sig("gelu_sb", UNITS), sig("up_sb", UNITS)
        down_ps, y_done = sig("down_ps"), sig("y_done", raised=1)

        block = ctx.enter_context(nc.Block())

        @block.sync
        def _(sp):
            sp.dma_start(front[:, :], front_d).then_inc(w_in.sem, 16)
            sp.dma_start(vec[:, :], vec_d).then_inc(w_in.sem, 16)
            sp.dma_start(const[:, :], const_d).then_inc(w_in.sem, 16)
            sp.dma_start(table[:, :, :], table_d).then_inc(w_in.sem, 16)
            sp.dma_start(work[:, 0:P + 2 * KEYS], mask_d).then_inc(w_in.sem, 16)
            def tokens(a, b):
                return a[b].rearrange("(n p) c -> p n c", p=P)

            def batch(b, more):
                if more:
                    sp.wait_ge(x_mid_done.sem, x_mid_done.at(b, 1))
                    sp.dma_start(x_in[:, :, :], tokens(x_d, b + 1)).then_inc(x_loaded.sem, 16)
                for l in range(LAYERS):
                    li = b * LAYERS + l
                    sp.wait_ge(wo_ps.sem, wo_ps.at(li, 0))
                    sp.dma_start(layer_w[:, :], layer_d[l]).then_inc(lw_loaded.sem, 16)
                    sp.wait_ge(y_done.sem, y_done.at(li, 0))
                    sp.dma_start(mlp_w[:, :], mlp_d[l]).then_inc(mlp_loaded.sem, 16)
                    sp.dma_start(lvec[:, :], lvec_d[l]).then_inc(mlp_loaded.sem, 16)
                sp.wait_ge(out_done.sem, out_done.at(b, 1))
                sp.dma_start(tokens(out_d, b), out_tt).then_inc(out_sent.sem, 16)

            sp.dma_start(x_in[:, :, :], tokens(x_d, 0)).then_inc(x_loaded.sem, 16)
            with sp.Fori(0, B - 1) as b:
                batch(b, True)
            batch(B - 1, False)
            sp.wait_ge(out_sent.sem, out_sent.at(B, 0))

        @block.tensor
        def _(pe):
            mm = nc.tensor.matmul

            def two(bank, lhsT, rhs, rows=P, start=True, stop=True):
                for c in range(2):
                    last = mm(ps[0:rows, bank + c, :], lhsT, rhs[:, c * HALF:(c + 1) * HALF], start=start, stop=stop)
                return last

            def turn8(bank, tiles):
                for i in range(NT):
                    last = nc.tensor.transpose(ps[:, bank + i // 4, (i % 4) * P:(i % 4 + 1) * P], tiles(i), ident)
                return last

            pe.wait_ge(ready0.sem, 1)

            def block0(b):
                for _ in range(6):
                    yield
                pe.wait_ge(hn_t.sem, hn_t.at(b, 1))
                turn8(6, lambda i: hn_tt[:, i, :]).then_inc(hn_ps.sem, 1)
                yield
                yield
                pe.wait_ge(h_c.sem, h_c.at(b, 1))
                turn8(6, lambda i: xn_tt[:, i, :]).then_inc(xn_ps.sem, 1)
                yield
                yield
                yield
                pe.wait_ge(mixed.sem, mixed.at(b, 1))
                pe.wait_ge(xn_c.sem, xn_c.at(b, 1))
                two(6, w("wk"), z_c[:, :]).then_inc(k_ps.sem, 1)
                yield
                yield
                pe.wait_ge(k_sb.sem, k_sb.at(b, 1))
                two(6, w("wv"), z_c[:, :]).then_inc(v_ps.sem, 1)
                yield
                yield
                pe.wait_ge(v_sb.sem, v_sb.at(b, 1))
                two(6, w("wr"), z_c[:, :]).then_inc(r_ps.sem, 1)
                yield
                yield
                pe.wait_ge(r_sb.sem, r_sb.at(b, 1))
                pe.wait_ge(mean_done.sem, mean_done.at(b, 1))
                mm(ps[0:64, 6, 0:1], w("gc1"), mean_c[:, :], start=True, stop=True).then_inc(gc_ps.sem, 1)
                yield
                yield
                pe.wait_ge(gc_sb.sem, gc_sb.at(b, 1))
                mm(ps[:, 6, 1:2], w("gc2", 64), g1[0:64, :], start=True, stop=True).then_inc(gc_ps.sem, 1)
                yield
                yield
                pe.wait_ge(gc_sb.sem, gc_sb.at(b, 2))
                mm(ps[:, 6, 2:3], w("gc3", 32), g2[0:32, :], start=True, stop=True).then_inc(gc_ps.sem, 1)
                for _ in range(10):
                    yield
                pe.wait_ge(gc_sb.sem, gc_sb.at(b, 3))
                pe.wait_ge(wkv.sem, wkv.at(b, 15))
                for cy in range(CYCLES):
                    if cy:
                        pe.wait_ge(cycle.sem, cycle.at(b, 3 * cy))
                    two(6, w("cn1"), xn[:, :]).then_inc(cn_ps.sem, 1)
                    yield
                    yield
                    pe.wait_ge(cn_sb.sem, cn_sb.at(b, 4 * cy + 1))
                    two(6, w("cn2"), k_c[:, :], rows=64).then_inc(cn_ps.sem, 1)
                    yield
                    yield
                    pe.wait_ge(cn_sb.sem, cn_sb.at(b, 4 * cy + 2))
                    two(6, w("cn3", 64), v_c[0:64, :]).then_inc(cn_ps.sem, 1)
                    yield
                    yield
                    pe.wait_ge(cn_sb.sem, cn_sb.at(b, 4 * cy + 3))
                    two(6, w("cn4", 32), aa[0:32, 0:T]).then_inc(cn_ps.sem, 1)
                    yield
                    yield
                    pe.wait_ge(cn_sb.sem, cn_sb.at(b, 4 * cy + 4))
                    two(6, twist, xn[:, :]).then_inc(cn_ps.sem, 1)
                    yield
                    yield
                pe.wait_ge(cycle.sem, cycle.at(b, 3 * CYCLES))
                turn8(6, lambda i: xn1[:, i * P:(i + 1) * P]).then_inc(x1_ps.sem, 1)
                for _ in range(4):
                    yield
                pe.wait_ge(h2_t.sem, h2_t.at(b, 1))
                turn8(6, lambda i: e_b[:, i * P:(i + 1) * P]).then_inc(h2_ps.sem, 1)
                for _ in range(4):
                    yield
                pe.wait_ge(mix2.sem, mix2.at(b, 3))
                for j in range(4):
                    if j:
                        pe.wait_ge(kc_relu.sem, kc_relu.at(b, j))
                    two(6, w("wck")[:, j * P:(j + 1) * P], z_c[:, :]).then_inc(kc_ps.sem, 1)
                    yield
                    yield
                pe.wait_ge(kc_relu.sem, kc_relu.at(b, 4))
                two(6, w("wcr"), z_c[:, :]).then_inc(rc_ps.sem, 1)
                yield
                yield
                pe.wait_ge(rc_sb.sem, rc_sb.at(b, 1))
                for c in range(2):
                    for j in range(4):
                        pe.wait_ge(kc_sq.sem, kc_sq.at(b, j + 1))
                        last = mm(ps[:, 6 + c, :], w("wcv")[:, j * P:(j + 1) * P], relus[j][:, c * HALF:(c + 1) * HALF],
                                  start=(j == 0), stop=(j == 3))
                last.then_inc(vv_ps.sem, 1)
                yield

            def middle_part(b):
                pe.wait_ge(out_done.sem, out_done.at(b, 0))
                pe.wait_ge(prod0.sem, prod0.at(b, 2))
                turn8(0, lambda i: e_a[:, i * P:(i + 1) * P]).then_inc(prod0_ps.sem, 1)
                pe.wait_ge(y_t.sem, y_t.at(b, 1))
                turn8(2, lambda i: y_tt[:, i, :]).then_inc(y_ps.sem, 1)
                pe.wait_ge(y_c.sem, y_c.at(b, 1))
                two(0, w("aq"), y[:, :]).then_inc(qk_ps.sem, 1)
                two(4, w("ak"), y[:, :]).then_inc(qk_ps.sem, 1)
                for i in range(NT):
                    last = mm(ps[:, 6 + i // 4, (i % 4) * P:(i % 4 + 1) * P], y[:, i * P:(i + 1) * P], w("av"),
                              start=True, stop=True)
                last.then_inc(va_ps.sem, 1)
                pe.wait_ge(trig.sem, trig.at(b, 4))
                for n in range(2 * NT):
                    c, kt = n // NT, n % NT
                    if n >= 4:
                        pe.wait_ge(sim_exp.sem, sim_exp.at(b, n - 3))
                    for f, (kf, qf) in enumerate([(e_b, e_a), (v_c, k_c)]):
                        last = mm(ps[:, n % 4, :], kf[:, kt * P:(kt + 1) * P], qf[:, c * HALF:(c + 1) * HALF],
                                  start=(f == 0), stop=(f == 1))
                    last.then_inc(sim_ps.sem, 1)
                pe.wait_ge(va_sb.sem, va_sb.at(b, 1))
                for m in range(NT):
                    pe.wait_ge(sim_exp.sem, sim_exp.at(b, NT if m < NT // 2 else 2 * NT))
                    if m >= 4:
                        pe.wait_ge(pv_sb.sem, pv_sb.at(b, m - 3))
                    for kt in range(NT):
                        last = mm(ps[:, 4 + m % 4, 0:D + 1], p_att[:, kt, m * P:(m + 1) * P], v_att[:, kt, :],
                                  start=(kt == 0), stop=(kt == NT - 1))
                    last.then_inc(pv_ps.sem, 1)
                pe.wait_ge(pv_sb.sem, pv_sb.at(b, NT))
                turn8(0, lambda i: o_tt[:, i, :]).then_inc(at_ps.sem, 1)
                pe.wait_ge(at_sb.sem, at_sb.at(b, 1))
                two(2, w("ao"), r_c[:, :]).then_inc(ao_ps.sem, 1)

            def layer_part(li, aside):
                wqk = layer_w[:, 0:WQK_COLS].rearrange("p (k h d) -> p k h d", k=4, h=PAIRS)
                wv = layer_w[:, WQK_COLS:WQK_COLS + INNER]
                wo = layer_w[:, WQK_COLS + INNER:].rearrange("p (h d) -> p h d", h=PAIRS)
                w1 = mlp_w[:, 0:2 * HID]
                w2 = mlp_w[:, 2 * HID:].rearrange("p (j d) -> p j d", j=len(CHUNKS))
                pe.wait_ge(lw_loaded.sem, lw_loaded.at(li, 16))
                pe.wait_ge(y_done.sem, y_done.at(li, 0))
                pe.wait_ge(shifted.sem, shifted.at(li, 2))
                for i in range(JOBS + 1):
                    hp, c = i // 2, i % 2
                    if i < JOBS:
                        if i >= 2:
                            pe.wait_ge(qn_ln.sem, qn_ln.at(li, i - 1))
                        if i == 1:
                            pe.wait_ge(vw_sb.sem, vw_sb.at(li, 1))
                        mm(ps[:, 4, :], h_s[:, i * P:(i + 1) * P], wv, start=True, stop=True).then_inc(vw_ps.sem, 1)
                        cols = h_s[:, c * HALF:(c + 1) * HALF]
                        for kind in range(4):
                            if i and kind % 2:
                                pe.wait_ge(rotated.sem, rotated.at(li, 4 * (i - 1) + kind + 1))
                            elif i:
                                pe.wait_ge(sq_sb.sem, sq_sb.at(li, 2 * (i - 1) + kind // 2 + 1))
                            mm(ps[:, kind, :], wqk[:, kind, hp, :], cols, start=True, stop=True).then_inc(qk4_ps.sem, 1)
                        next(aside, None)
                    if i:
                        pe.wait_ge(sq_sb.sem, sq_sb.at(li, 2 * i))
                        if i >= 2:
                            pe.wait_ge(norm_ln.sem, norm_ln.at(li, i - 1))
                        mm(ps[:, 5, :], pair_ones, squares[:, (i - 1) % 2, 1, :], start=True, stop=True)
                        pe.wait_ge(vw_sb.sem, vw_sb.at(li, min(i + 1, JOBS)))
                        if i == JOBS:
                            pe.wait_ge(qn_ln.sem, qn_ln.at(li, i - 1))
                        for t in range(4):
                            last = mm(ps[:, 4, 2 * t:2 * t + 2], squares[:, (i - 1) % 2, 0, t * P:(t + 1) * P], head_ones,
                                      start=True, stop=True)
                        last.then_inc(norm_ps.sem, 1)
                        next(aside, None)

                def scores(n):
                    hp, m = n // NT, n % NT
                    bank = 2 * (n % 2)
                    if n >= 2:
                        pe.wait_ge(p_sb.sem, p_sb.at(li, n - 1))
                    for e in range(2):
                        mm(ps[:, bank + e, 0:KEYS], ident16, first_mask if m == 0 else band_mask, start=True, stop=False)
                    for e in range(2):
                        rows = slice(e * DH, (e + 1) * DH)
                        last = mm(ps[:, bank + e, 0:KEYS], q_rot[rows, hp, m * P:(m + 1) * P],
                                  k_rot[rows, hp, m * P:m * P + KEYS], start=False, stop=True)
                    last.then_inc(s_ps.sem, 1)

                def turn_p(n):
                    m = n % NT
                    pe.wait_ge(p_sb.sem, p_sb.at(li, n + 1))
                    if n:
                        pe.wait_ge(pt_sb[(n - 1) % 2].sem, pt_sb[(n - 1) % 2].at(li, (n - 1) // 2 + 1))
                    for e in range(2):
                        for ch in range(2):
                            if m or ch:
                                last = nc.tensor.transpose(ps[:, 4, (2 * e + ch) * P:(2 * e + ch + 1) * P],
                                                           p_win[:, n % 2, e, ch * P:(ch + 1) * P], ident)
                    last.then_inc(pt_ps.sem, 1)

                def values(n):
                    hp, m = n // NT, n % NT
                    pe.wait_ge(pt_sb[n % 2].sem, pt_sb[n % 2].at(li, n // 2 + 1))
                    if n:
                        pe.wait_ge(o_sb.sem, o_sb.at(li, n))
                    for e in range(2):
                        for ch in range(2):
                            if m or ch:
                                last = mm(ps[:, 5, e * (DH + 1):(e + 1) * (DH + 1)], pt_win[:, n % 3, e, ch, :],
                                          v_win[:, m - 1 + ch, 2 * hp + e, :], start=(ch == 0 or m == 0), stop=(ch == 1))
                    last.then_inc(o_ps.sem, 1)

                def turn_o(n):
                    hp = (n - 3) // NT
                    pe.wait_ge(o_sb.sem, o_sb.at(li, n - 2))
                    for t in range(4):
                        last = nc.tensor.transpose(ps[:, 5, t * P:(t + 1) * P], o_t[:, hp % 2, t, :], ident)
                    last.then_inc(ot_ps.sem, 1)
                    turned = min(n, STEPS)
                    pe.wait_ge(pt_sb[(turned - 1) % 2].sem, pt_sb[(turned - 1) % 2].at(li, (turned - 1) // 2 + 1))
                    for t in range(4):
                        last = nc.tensor.transpose(ps[:, 4, t * P:(t + 1) * P], o_t[:, hp % 2, 4 + t, :], ident)
                    last.then_inc(ot_ps.sem, 1)

                pe.wait_ge(k_done.sem, k_done.at(li, JOBS))
                pe.wait_ge(q_sum.sem, q_sum.at(li, JOBS))
                pe.wait_ge(qn_ln.sem, qn_ln.at(li, JOBS))
                pe.wait_ge(norm_ln.sem, norm_ln.at(li, JOBS))
                for n in range(STEPS + 3):
                    if n < STEPS:
                        scores(n)
                    if n > NT + 2 and (n - 3) % NT == 0:
                        pe.wait_ge(ot_sb.sem, ot_sb.at(li, 2 * ((n - 3) // NT)))
                    if 1 <= n <= STEPS:
                        turn_p(n - 1)
                    if n >= 3:
                        values(n - 3)
                    if n >= 3 and (n - 3) % NT == NT - 1:
                        turn_o(n)
                    next(aside, None)
                pe.wait_ge(ot_sb.sem, ot_sb.at(li, 2 * PAIRS))
                for c in range(2):
                    for hp in range(PAIRS):
                        last = mm(ps[:, c, :], wo[:, hp, :], ff[:, hp, c * HALF:(c + 1) * HALF],
                                  start=(hp == 0), stop=(hp == PAIRS - 1))
                last.then_inc(wo_ps.sem, 1)
                next(aside, None)
                pe.wait_ge(shifted2.sem, shifted2.at(li, 1))
                turn8(2, lambda i: h_s[:, i * P:(i + 1) * P]).then_inc(lnl_tp.sem, 1)
                pe.wait_ge(lnl_t.sem, lnl_t.at(li, 1))
                turn8(4, lambda i: ln_t[:, i, :]).then_inc(lnl_ps.sem, 1)
                pe.wait_ge(mlp_loaded.sem, mlp_loaded.at(li, 32))
                pe.wait_ge(lnl_c.sem, lnl_c.at(li, 1))
                for u in range(UNITS):
                    j, c = u // 2, u % 2
                    lo, n = CHUNKS[j]
                    if u >= 3:
                        pe.wait_ge(up_sb.sem, up_sb.at(li, u - 2))
                    for k, o in enumerate((lo, HID + lo)):
                        last = mm(ps[0:n, 2 * (u % 3) + k, :], w1[:, o:o + n], ln_c[:, c * HALF:(c + 1) * HALF], start=True, stop=True)
                    last.then_inc(up_ps.sem, 1)
                    next(aside, None)
                pe.wait_ge(up_sb.sem, up_sb.at(li, UNITS))
                for c in range(2):
                    for j, (lo, n) in enumerate(CHUNKS):
                        last = mm(ps[:, c, :], w2[0:n, j, :], ff[0:n, j, c * HALF:(c + 1) * HALF],
                                  start=(j == 0), stop=(j == len(CHUNKS) - 1))
                last.then_inc(down_ps.sem, 1)
                next(aside, None)

            def batch(b, aside):
                middle_part(b)
                for l in range(LAYERS):
                    layer_part(b * LAYERS + l, aside)
                for _ in aside:
                    pass
                pe.wait_ge(prod1.sem, prod1.at(b, 2))
                turn8(0, lambda i: s_att[:, i * P:(i + 1) * P]).then_inc(prod1_ps.sem, 1)

            for _ in block0(0):
                pass
            with pe.Fori(0, B - 1) as b:
                batch(b, block0(b + 1))
            batch(B - 1, iter(()))

        @block.scalar
        def _(act):
            fn = nc.scalar.activation
            act.wait_ge(ready0.sem, 1)

            def rsqrt_of(k, turn, have, log, out):
                act.wait_ge(have.sem, have.at(turn, 1))
                fn(log_a[:, k, :], mv[:, k, :, 1], ACT.Ln, bias=cst("eps")).then_inc(log.sem, 1)
                act.wait_ge(log.sem, log.at(turn, 1))
                fn(rstd[:, k, :], log_a[:, k, :], ACT.Exp, scale=-0.5).then_inc(out.sem, 1)

            def block0(b):
                yield
                act.wait_ge(ln0_mv.sem, ln0_mv.at(b, 1))
                fn(log_a[:, 0, :], mv[:, 0, :, 1], ACT.Ln, bias=cst("eps")).then_inc(ln0_logs.sem, 1)
                fn(log_b[:, :], mv[:, 0, :, 1], ACT.Ln, bias=cst("eps_sq"), scale=1.0 + EPS).then_inc(ln0_logs.sem, 1)
                act.wait_ge(ln0_logs.sem, ln0_logs.at(b, 1))
                fn(rstd[:, 0, :], log_a[:, 0, :], ACT.Exp, scale=-0.5).then_inc(ln0_rstd.sem, 1)
                yield
                yield
                act.wait_ge(ln0_logd.sem, ln0_logd.at(b, 1))
                fn(rstd2[:, :], log_b[:, :], ACT.Exp, scale=0.5).then_inc(ln0_rstd.sem, 1)
                for _ in range(4):
                    yield
                act.wait_ge(hn_ps.sem, hn_ps.at(b, 1))
                fn(halves(h_pad[:, 1:T + 1]), both(6), ACT.Identity, bias=v("ln1_b"), scale=v("ln1_w")).then_inc(h_c.sem, 1)
                for _ in range(5):
                    yield
                act.wait_ge(k_ps.sem, k_ps.at(b, 1))
                fn(halves(k_c[:, :]), both(6), ACT.Copy).then_inc(k_sb.sem, 1)
                yield
                yield
                act.wait_ge(v_ps.sem, v_ps.at(b, 1))
                fn(halves(v_c[:, :]), both(6), ACT.Copy).then_inc(v_sb.sem, 1)
                yield
                yield
                act.wait_ge(r_ps.sem, r_ps.at(b, 1))
                fn(halves(r_c[:, :]), both(6), ACT.Tanh, scale=0.5).then_inc(r_sb.sem, 1)
                yield
                act.wait_ge(wkv.sem, wkv.at(b, 2))
                fn(e_a[:, :], e_a[:, :], ACT.Exp).then_inc(wkv_exp.sem, 1)
                act.wait_ge(wkv.sem, wkv.at(b, 3))
                fn(e_b[:, :], e_b[:, :], ACT.Exp).then_inc(wkv_exp.sem, 1)
                yield
                act.wait_ge(gc_ps.sem, gc_ps.at(b, 1))
                fn(g1[0:64, :], ps[0:64, 6, 0:1], ACT.Gelu, bias=v("gc_b1", 64), scale=1.0 / T).then_inc(gc_sb.sem, 1)
                yield
                act.wait_ge(wkv.sem, wkv.at(b, 4))
                act.wait_ge(mixed.sem, mixed.at(b, 1))
                fn(h_pad[:, 1:T + 1], e_a[:, :], ACT.Ln).then_inc(wkv_ln.sem, 1)
                yield
                act.wait_ge(gc_ps.sem, gc_ps.at(b, 2))
                fn(g2[0:32, :], ps[0:32, 6, 1:2], ACT.Gelu, bias=v("gc_b2", 32)).then_inc(gc_sb.sem, 1)
                yield
                yield
                act.wait_ge(gc_ps.sem, gc_ps.at(b, 3))
                fn(tg[:, :], ps[:, 6, 2:3], ACT.Tanh, bias=dv("half_gc_b3"), scale=0.5).then_inc(gc_sb.sem, 1)
                yield
                act.wait_ge(wkv.sem, wkv.at(b, 7))
                fn(e_a[:, :], e_a[:, :], ACT.Exp).then_inc(wkv_exp2.sem, 1)
                act.wait_ge(wkv.sem, wkv.at(b, 8))
                fn(e_b[:, :], e_b[:, :], ACT.Exp).then_inc(wkv_exp2.sem, 1)
                yield
                fn(z_c[:, :], z_c[:, :], ACT.Tanh, bias=dv("half_u"), scale=0.5).then_inc(wkv_gate.sem, 1)
                for _ in range(7):
                    yield
                for cy in range(CYCLES):
                    yield
                    act.wait_ge(cn_ps.sem, cn_ps.at(b, 5 * cy + 1))
                    fn(halves(k_c[:, :]), both(6), ACT.Gelu, bias=v("cn_b1")).then_inc(cn_sb.sem, 1)
                    yield
                    yield
                    act.wait_ge(cn_ps.sem, cn_ps.at(b, 5 * cy + 2))
                    fn(halves(v_c[0:64, :]), ps[0:64, 6:8, :], ACT.Gelu, bias=v("cn_b2", 64)).then_inc(cn_sb.sem, 1)
                    yield
                    yield
                    act.wait_ge(cn_ps.sem, cn_ps.at(b, 5 * cy + 3))
                    fn(halves(aa[0:32, 0:T]), ps[0:32, 6:8, :], ACT.Gelu, bias=v("cn_b3", 32)).then_inc(cn_sb.sem, 1)
                    yield
                    yield
                    act.wait_ge(cn_ps.sem, cn_ps.at(b, 5 * cy + 4))
                    if cy:
                        act.wait_ge(cycle.sem, cycle.at(b, 3 * cy))
                    fn(halves(e_a[:, :]), both(6), ACT.Tanh, bias=dv("half_cn_b4"), scale=0.5).then_inc(cn_sb.sem, 1)
                    yield
                    yield
                    yield
                yield
                yield
                rsqrt_of(0, b, ln2_mv, ln2_log, ln2_rstd)
                yield
                yield
                yield
                act.wait_ge(h2_ps.sem, h2_ps.at(b, 1))
                fn(halves(h_pad[:, 1:T + 1]), both(6), ACT.Identity, bias=v("ln2_b"), scale=v("ln2_w")).then_inc(h2_c.sem, 1)
                for _ in range(3):
                    yield
                for j in range(4):
                    yield
                    act.wait_ge(kc_ps.sem, kc_ps.at(b, j + 1))
                    fn(halves(relus[j][:, 0:T]), both(6), ACT.Relu).then_inc(kc_relu.sem, 1)
                    yield
                yield
                act.wait_ge(rc_ps.sem, rc_ps.at(b, 1))
                fn(halves(r_c[:, :]), both(6), ACT.Tanh, scale=0.5).then_inc(rc_sb.sem, 1)
                fn(e_b[:, :], xn[:, :], ACT.Tanh, scale=0.5).then_inc(gate0.sem, 1)
                yield

            def middle_part(b):
                rsqrt_of(1, b, ln3_mv, ln3_log, ln3_rstd)
                act.wait_ge(y_ps.sem, y_ps.at(b, 1))
                fn(halves(y[:, :]), both(2), ACT.Copy).then_inc(y_c.sem, 1)
                for n, (dst, bank, bias) in enumerate([(k_c, 0, "theta_q0"), (v_c, 4, "theta_k0")]):
                    act.wait_ge(qk_ps.sem, qk_ps.at(b, n + 1))
                    fn(halves(dst[:, :]), both(bank), ACT.Identity, bias=dv(bias), scale=dv("inv_wave")).then_inc(theta.sem, 1)
                act.wait_ge(va_ps.sem, va_ps.at(b, 1))
                fn(v_att[:, :, 0:D].rearrange("p (c n) d -> p c n d", c=2),
                   ps[:, 6:8, :].rearrange("p c (n d) -> p c n d", d=D), ACT.Copy).then_inc(va_sb.sem, 1)
                for n, (r, co) in enumerate([(k_c, e_a), (v_c, e_b)]):
                    act.wait_ge(reduced.sem, reduced.at(b, n + 1))
                    fn(co[:, :], r[:, :], ACT.Abs).then_inc(abs_s.sem, 1)
                    act.wait_ge(abs_s.sem, abs_s.at(b, n + 1))
                    fn(co[:, :], co[:, :], ACT.Sin, bias=cst("half_pi"), scale=-1.0).then_inc(trig.sem, 1)
                    fn(r[:, :], r[:, :], ACT.Sin).then_inc(trig.sem, 1)
                for n in range(2 * NT):
                    c, kt = n // NT, n % NT
                    act.wait_ge(sim_ps.sem, sim_ps.at(b, n + 1))
                    fn(p_att[:, kt, c * HALF:(c + 1) * HALF], ps[:, n % 4, :], ACT.Exp, scale=D ** -0.5).then_inc(sim_exp.sem, 1)
                act.wait_ge(at_ps.sem, at_ps.at(b, 1))
                fn(halves(r_c[:, :]), both(0), ACT.Identity, bias=v("bv")).then_inc(at_sb.sem, 1)
                act.wait_ge(ao_ps.sem, ao_ps.at(b, 1))
                fn(halves(s_att[:, :]), both(2), ACT.Identity, bias=v("bo")).then_inc(ao_sb.sem, 1)

            def layer_part(li, b, aside):
                act.wait_ge(y_c.sem, y_c.at(b, 1))
                act.wait_ge(y_done.sem, y_done.at(li, 0))
                fn(h_s[0:64, :], y[0:64, :], ACT.Copy).then_inc(shifted.sem, 1)
                fn(h_s[64:P, 1:T], y[64:P, 0:T - 1], ACT.Copy).then_inc(shifted.sem, 1)
                for i in range(JOBS + 1):
                    if i < JOBS:
                        act.wait_ge(vw_ps.sem, vw_ps.at(li, i + 1))
                        fn(v_win[:, i, :, 0:DH], ps[:, 4, :].rearrange("p (h d) -> p h d", h=HEADS), ACT.Copy).then_inc(vw_sb.sem, 1)
                        if i >= 2:
                            act.wait_ge(norm_ps.sem, norm_ps.at(li, i - 1))
                        for kind in range(2):
                            act.wait_ge(rotated.sem, rotated.at(li, 4 * i + 2 * kind + 1))
                            fn(squares[:, i % 2, kind, :], ps[:, 2 * kind, :], ACT.Square).then_inc(sq_sb.sem, 1)
                        next(aside, None)
                    if i:
                        act.wait_ge(norm_ps.sem, norm_ps.at(li, i))
                        if i >= 3:
                            act.wait_ge(k_done.sem, k_done.at(li, i - 2))
                        fn(rn_k[:, (i - 1) % 2, :], ps[:, 5, :], ACT.Ln, bias=cst("tiny"), scale=2.0 ** 20).then_inc(norm_ln.sem, 1)
                        fn(rn_q[:, 8 * (i - 1):8 * i], ps[:, 4, 0:8], ACT.Ln, bias=cst("tiny"), scale=2.0 ** 20).then_inc(qn_ln.sem, 1)
                        act.wait_ge(norm_ln.sem, norm_ln.at(li, i))
                        fn(rn_k[:, (i - 1) % 2, :], rn_k[:, (i - 1) % 2, :], ACT.Exp, bias=cst("ln_1024"), scale=-0.5).then_inc(norm_ex.sem, 1)
                        next(aside, None)
                act.wait_ge(qn_ln.sem, qn_ln.at(li, JOBS))
                fn(rn_q[:, :], rn_q[:, :], ACT.Exp, bias=cst("ln_1024"), scale=-0.5).then_inc(qn_ex.sem, 1)

                def exps(n):
                    hp, m = n // NT, n % NT
                    if n >= 2:
                        act.wait_ge(pt_ps.sem, pt_ps.at(li, n - 1))
                    act.wait_ge(s_neg.sem, s_neg.at(li, n + 1))
                    for e in range(2):
                        col = (hp * NT + m) * 2 + e
                        last = fn(p_win[:, n % 2, e, 2 * P - KEYS:], ps[:, 2 * (n % 2) + e, 0:KEYS], ACT.Exp,
                                  bias=neg_top[:, n % 4, e:e + 1], scale=rn_q[:, col:col + 1])
                    last.then_inc(p_sb.sem, 1)

                def copy_pt(n):
                    act.wait_ge(pt_ps.sem, pt_ps.at(li, n + 1))
                    if n >= 3:
                        act.wait_ge(o_ps.sem, o_ps.at(li, n - 2))
                    lo = 0 if n % NT else 1
                    fn(pt_win[:, n % 3, :, lo:, :], ps[:, 4, :].rearrange("p (e c k) -> p e c k", e=2, c=2)[:, :, lo:, :],
                       ACT.Copy).then_inc(pt_sb[0].sem, 1)

                for n in range(STEPS + 3):
                    if n < STEPS:
                        exps(n)
                    if 1 <= n <= STEPS and n % 2 == 1:
                        copy_pt(n - 1)
                    if n >= 3 and (n - 3) % NT == NT - 1:
                        hp = (n - 3) // NT
                        for c in range(2):
                            act.wait_ge(ot_ps.sem, ot_ps.at(li, 2 * hp + c + 1))
                            fn(ff[:, hp, c * HALF:(c + 1) * HALF], ps[:, 5 - c, :], ACT.Copy).then_inc(ot_sb.sem, 1)
                    next(aside, None)
                next(aside, None)
                act.wait_ge(y_mid.sem, y_mid.at(li, 1))
                fn(h_s[0:64, :], y[0:64, :], ACT.Copy)
                fn(h_s[64:P, 1:T], y[64:P, 0:T - 1], ACT.Copy).then_inc(shifted2.sem, 1)
                rsqrt_of(1, li, lnl_mv, lnl_log, lnl_rstd)
                act.wait_ge(mlp_loaded.sem, mlp_loaded.at(li, 32))
                act.wait_ge(lnl_ps.sem, lnl_ps.at(li, 1))
                fn(halves(ln_c), both(4), ACT.Identity, bias=lv("ln_b"), scale=lv("ln_g")).then_inc(lnl_c.sem, 1)
                for u in range(UNITS):
                    n = CHUNKS[u // 2][1]
                    act.wait_ge(up_ps.sem, up_ps.at(li, u + 1))
                    if u >= 3:
                        act.wait_ge(up_sb.sem, up_sb.at(li, u - 2))
                    fn(gelus[0:n, u % 3, :], ps[0:n, 2 * (u % 3) + 1, :], ACT.Gelu, bias=lv(f"b1g{u // 2}", n)).then_inc(gelu_sb.sem, 1)
                    next(aside, None)
                next(aside, None)

            def batch(b, aside):
                middle_part(b)
                for l in range(LAYERS):
                    layer_part(b * LAYERS + l, b, aside)
                for _ in aside:
                    pass
                act.wait_ge(y_done.sem, y_done.at(b * LAYERS + LAYERS, 0))
                fn(e_b[:, :], y[:, :], ACT.Tanh, scale=0.5).then_inc(gate1.sem, 1)

            for _ in block0(0):
                pass
            with act.Fori(0, B - 1) as b:
                batch(b, block0(b + 1))
            batch(B - 1, iter(()))

        @block.vector
        def _(dve):
            tt, ts_, stt = nc.vector.tensor_tensor, nc.vector.tensor_scalar, nc.vector.scalar_tensor_tensor
            scan = nc.vector.tensor_tensor_scan

            nc.vector.memset(h_s[64:P, 0:1], 0.0)
            for n, s in enumerate((out_sent, x_mid_done, out_done, wo_ps, y_done)):
                nc.vector.memset(seed[:, n:n + 1], 0.0).then_inc(s.sem, 1)
            for h in range(HEADS):
                nc.vector.memset(v_win[:, :, h, DH:DH + 1], 1.0)
            nc.vector.memset(p_win[:, :, :, 0:2 * P - KEYS], 0.0).then_inc(setup.sem, 1)
            dve.wait_ge(w_in.sem, 16 * 5)
            nc.vector.tensor_copy(mask[:, :], work[:, 0:P + 2 * KEYS])
            ts_(dv("neg_ts"), v("ts"), -1.0, None, ALU.mult)
            ts_(dv("one_plus_ts"), v("ts"), 1.0, None, ALU.add)
            ts_(dv("one_minus_ts"), v("ts"), -1.0, 1.0, ALU.mult, ALU.add)
            ts_(dv("half_gc_b3"), v("gc_b3"), 0.5, None, ALU.mult)
            ts_(dv("half_cn_b4"), v("cn_b4"), 0.5, None, ALU.mult)
            ts_(dv("half_u"), v("u"), 0.5, None, ALU.mult)
            ts_(dv("ar7"), v("ar"), 0.7, None, ALU.mult)
            ts_(dv("ar3"), v("ar"), 0.3, None, ALU.mult)
            ts_(dv("wave_eps"), v("wave"), 1e-8, None, ALU.add).then_inc(setup.sem, 1)
            dve.wait_ge(setup.sem, 2)
            nc.vector.reciprocal(dv("inv_wave"), dv("wave_eps")).then_inc(setup.sem, 1)
            dve.wait_ge(setup.sem, 3)
            stt(dv("theta_q0"), v("bq"), dv("inv_wave"), v("phase"), ALU.mult, ALU.add)
            stt(dv("theta_k0"), v("bk"), dv("inv_wave"), v("phase"), ALU.mult, ALU.add).then_inc(setup.sem, 1)
            dve.wait_ge(setup.sem, 4)
            nc.vector.memset(top_s[:, :, :], 0.0).then_inc(ready0.sem, 1)
            dve.wait_ge(ready0.sem, 1)

            def moments(k, turn, src, have, done):
                for i in range(NT):
                    last = nc.vector.bn_stats(stats[:, k, i, :], src(i))
                last.then_inc(have.sem, 1)
                dve.wait_ge(have.sem, have.at(turn, 1))
                nc.vector.memset(carrier[:, k:k + 1], 0.0)
                for i in range(NT):
                    last = nc.vector.bn_aggr(mv[:, k, i, :], stats[:, k, i, :])
                last.then_inc(done.sem, 1)

            def normalise(k, dst, src):
                for i in range(NT):
                    last = ts_(dst[:, i, :], src(i), mv[:, k, i, 0:1], rstd[:, k, i:i + 1], ALU.subtract, ALU.mult)
                return last

            def bank_tile(bank):
                return lambda i: ps[:, bank + i // 4, (i % 4) * P:(i % 4 + 1) * P]

            def block0(b):
                dve.wait_ge(x_loaded.sem, x_loaded.at(b, 16))
                moments(0, b, lambda i: x_in[:, i, :], ln0_stats, ln0_mv)
                yield
                yield
                dve.wait_ge(ln0_logs.sem, ln0_logs.at(b, 2))
                tt(log_b[:, :], log_a[:, 0, :], log_b[:, :], ALU.subtract).then_inc(ln0_logd.sem, 1)
                yield
                yield
                dve.wait_ge(ln0_rstd.sem, ln0_rstd.at(b, 1))
                normalise(0, xn_tt, lambda i: x_in[:, i, :]).then_inc(xn_t.sem, 1)
                nc.vector.tensor_copy(h_pad[:, 0:1], v("ts")).then_inc(hpad0.sem, 1)
                yield
                dve.wait_ge(ln0_rstd.sem, ln0_rstd.at(b, 2))
                dve.wait_ge(xn_t.sem, xn_t.at(b, 1))
                for i in range(NT):
                    last = ts_(hn_tt[:, i, :], xn_tt[:, i, :], rstd2[:, i:i + 1], None, ALU.mult)
                last.then_inc(hn_t.sem, 1)
                yield
                yield
                yield
                dve.wait_ge(h_c.sem, h_c.at(b, 1))
                dve.wait_ge(hpad0.sem, hpad0.at(b, 1))
                ts_(e_a[:, :], h_pad[:, 0:T], dv("neg_ts"), None, ALU.mult).then_inc(mix_a.sem, 1)
                yield
                dve.wait_ge(xn_ps.sem, xn_ps.at(b, 1))
                nc.vector.tensor_copy(halves(xn[:, :]), both(6)).then_inc(xn_c.sem, 1)
                yield
                dve.wait_ge(mix_a.sem, mix_a.at(b, 1))
                stt(z_c[:, :], h_pad[:, 1:T + 1], dv("one_plus_ts"), e_a[:, :], ALU.mult, ALU.add).then_inc(mixed.sem, 1)
                yield
                dve.wait_ge(xn_c.sem, xn_c.at(b, 1))
                nc.vector.tensor_reduce(mean_c[:, :], xn[:, :], axis=AX, op=ALU.add).then_inc(mean_done.sem, 1)
                dve.wait_ge(mixed.sem, mixed.at(b, 1))
                for buf in (top, h_pad, aa):
                    nc.vector.memset(buf[:, 0:1], 0.0)
                yield
                yield
                dve.wait_ge(k_sb.sem, k_sb.at(b, 1))
                scan(top[:, 1:T + 1], k_c[:, :], k_c[:, :], 0.0, ALU.max, ALU.max).then_inc(wkv.sem, 1)
                yield
                dve.wait_ge(wkv.sem, wkv.at(b, 1))
                tt(e_a[:, :], top[:, 0:T], top[:, 1:T + 1], ALU.subtract).then_inc(wkv.sem, 1)
                yield
                tt(e_b[:, :], k_c[:, :], top[:, 1:T + 1], ALU.subtract).then_inc(wkv.sem, 1)
                yield
                yield
                yield
                dve.wait_ge(wkv_exp.sem, wkv_exp.at(b, 2))
                scan(e_a[:, :], e_a[:, :], e_b[:, :], 1.0, ALU.mult, ALU.add).then_inc(wkv.sem, 1)
                yield
                yield
                dve.wait_ge(wkv_ln.sem, wkv_ln.at(b, 1))
                tt(top[:, 0:T], top[:, 0:T], h_pad[:, 0:T], ALU.add).then_inc(wkv.sem, 1)
                yield
                dve.wait_ge(wkv.sem, wkv.at(b, 5))
                dve.wait_ge(r_ps.sem, r_ps.at(b, 1))
                tt(z_c[:, :], k_c[:, :], top[:, 0:T], ALU.subtract).then_inc(wkv.sem, 1)
                yield
                dve.wait_ge(wkv.sem, wkv.at(b, 6))
                ts_(e_a[:, :], z_c[:, :], -1.0, 0.0, ALU.mult, ALU.min).then_inc(wkv.sem, 1)
                ts_(e_b[:, :], z_c[:, :], 0.0, None, ALU.min).then_inc(wkv.sem, 1)
                yield
                dve.wait_ge(gc_sb.sem, gc_sb.at(b, 3))
                ts_(c0[:, :], tg[:, :], dv("ar7"), 0.1, ALU.mult, ALU.add).then_inc(gc_c0.sem, 1)
                yield
                dve.wait_ge(wkv_exp2.sem, wkv_exp2.at(b, 2))
                tt(e_b[:, :], e_b[:, :], v_c[:, :], ALU.mult).then_inc(wkv.sem, 1)
                yield
                dve.wait_ge(wkv.sem, wkv.at(b, 9))
                scan(aa[:, 1:T + 1], e_a[:, :], e_b[:, :], 0.0, ALU.mult, ALU.add).then_inc(wkv.sem, 1)
                yield
                dve.wait_ge(wkv.sem, wkv.at(b, 10))
                tt(e_a[:, :], v_c[:, :], aa[:, 0:T], ALU.subtract).then_inc(wkv.sem, 1)
                yield
                dve.wait_ge(wkv.sem, wkv.at(b, 11))
                dve.wait_ge(wkv_gate.sem, wkv_gate.at(b, 1))
                stt(e_a[:, :], z_c[:, :], 1.0, e_a[:, :], ALU.add, ALU.mult).then_inc(wkv.sem, 1)
                yield
                dve.wait_ge(wkv.sem, wkv.at(b, 12))
                stt(e_a[:, :], e_a[:, :], 0.5, aa[:, 0:T], ALU.mult, ALU.add).then_inc(wkv.sem, 1)
                yield
                dve.wait_ge(wkv.sem, wkv.at(b, 13))
                dve.wait_ge(r_sb.sem, r_sb.at(b, 1))
                stt(e_a[:, :], r_c[:, :], 1.0, e_a[:, :], ALU.add, ALU.mult).then_inc(wkv.sem, 1)
                yield
                dve.wait_ge(wkv.sem, wkv.at(b, 14))
                stt(xn1[:, :], e_a[:, :], 0.5, xn[:, :], ALU.mult, ALU.add).then_inc(wkv.sem, 1)
                yield
                dve.wait_ge(gc_c0.sem, gc_c0.at(b, 1))
                for cy in range(CYCLES):
                    for _ in range(8):
                        yield
                    dve.wait_ge(cn_sb.sem, cn_sb.at(b, 4 * cy + 4))
                    ts_(e_a[:, :], e_a[:, :], dv("ar3"), c0[:, :], ALU.mult, ALU.add).then_inc(cycle.sem, 1)
                    yield
                    dve.wait_ge(cycle.sem, cycle.at(b, 3 * cy + 1))
                    dve.wait_ge(cn_ps.sem, cn_ps.at(b, 5 * cy + 5))
                    tt(halves(e_a[:, :]), halves(e_a[:, :]), both(6), ALU.mult).then_inc(cycle.sem, 1)
                    dve.wait_ge(cycle.sem, cycle.at(b, 3 * cy + 2))
                    tt(xn[:, :], xn[:, :], e_a[:, :], ALU.add).then_inc(cycle.sem, 1)
                    yield
                yield
                dve.wait_ge(x1_ps.sem, x1_ps.at(b, 1))
                moments(0, b, bank_tile(6), ln2_stats, ln2_mv)
                yield
                yield
                dve.wait_ge(ln2_rstd.sem, ln2_rstd.at(b, 1))
                normalise(0, hn_tt, bank_tile(6)).then_inc(h2_t.sem, 1)
                yield
                yield
                yield
                dve.wait_ge(h2_c.sem, h2_c.at(b, 1))
                nc.vector.tensor_copy(h_pad[:, 0:1], h_pad[:, T:T + 1]).then_inc(mix2.sem, 1)
                dve.wait_ge(mix2.sem, mix2.at(b, 1))
                ts_(e_a[:, :], h_pad[:, 0:T], v("ts"), None, ALU.mult).then_inc(mix2.sem, 1)
                yield
                dve.wait_ge(mix2.sem, mix2.at(b, 2))
                stt(z_c[:, :], h_pad[:, 1:T + 1], dv("one_minus_ts"), e_a[:, :], ALU.mult, ALU.add).then_inc(mix2.sem, 1)
                yield
                for _ in range(11):
                    yield
                dve.wait_ge(vv_ps.sem, vv_ps.at(b, 1))
                dve.wait_ge(rc_sb.sem, rc_sb.at(b, 1))
                stt(halves(e_a[:, :]), halves(r_c[:, :]), 1.0, both(6), ALU.add, ALU.mult).then_inc(s_mul.sem, 1)
                yield
                dve.wait_ge(s_mul.sem, s_mul.at(b, 1))
                stt(e_a[:, :], e_a[:, :], 0.5, xn1[:, :], ALU.mult, ALU.add).then_inc(s_done.sem, 1)
                yield
                dve.wait_ge(s_done.sem, s_done.at(b, 1))
                tt(e_a[:, :], e_a[:, :], xn[:, :], ALU.mult).then_inc(prod0.sem, 1)
                yield
                dve.wait_ge(prod0.sem, prod0.at(b, 1))
                dve.wait_ge(gate0.sem, gate0.at(b, 1))
                stt(e_a[:, :], e_b[:, :], 1.0, e_a[:, :], ALU.add, ALU.mult).then_inc(prod0.sem, 1)
                yield

            def middle_part(b):
                dve.wait_ge(out_sent.sem, out_sent.at(b, 0))
                dve.wait_ge(prod0_ps.sem, prod0_ps.at(b, 1))
                stt(flat(x_mid), both(0), 0.5, flat(x_in), ALU.mult, ALU.add).then_inc(x_mid_done.sem, 1)
                nc.vector.memset(v_att[:, :, D:D + 1], 1.0)
                dve.wait_ge(x_mid_done.sem, x_mid_done.at(b, 1))
                moments(1, b, lambda i: x_mid[:, i, :], ln3_stats, ln3_mv)
                dve.wait_ge(ln3_rstd.sem, ln3_rstd.at(b, 1))
                normalise(1, y_tt, lambda i: x_mid[:, i, :]).then_inc(y_t.sem, 1)
                for n, th in enumerate((k_c, v_c)):
                    s0 = 5 * n
                    dve.wait_ge(theta.sem, theta.at(b, n + 1))
                    ts_(z_c[:, :], th[:, :], 1.0 / TWO_PI, ROUND, ALU.mult, ALU.add).then_inc(reduce_s.sem, 1)
                    dve.wait_ge(reduce_s.sem, reduce_s.at(b, s0 + 1))
                    ts_(z_c[:, :], z_c[:, :], ROUND, None, ALU.subtract).then_inc(reduce_s.sem, 1)
                    for k, part in enumerate((PI2_A, PI2_B, PI2_C)):
                        dve.wait_ge(reduce_s.sem, reduce_s.at(b, s0 + 2 + k))
                        stt(th[:, :], z_c[:, :], -part, th[:, :], ALU.mult, ALU.add).then_inc(reduce_s.sem, 1)
                    dve.wait_ge(reduce_s.sem, reduce_s.at(b, s0 + 5))
                    ts_(th[:, :], th[:, :], PI_IN, -PI_IN, ALU.min, ALU.max).then_inc(reduced.sem, 1)
                for m in range(NT):
                    dve.wait_ge(pv_ps.sem, pv_ps.at(b, m + 1))
                    nc.vector.reciprocal(rden_att[:, m:m + 1], ps[:, 4 + m % 4, D:D + 1]).then_inc(pv_r.sem, 1)
                    dve.wait_ge(pv_r.sem, pv_r.at(b, m + 1))
                    ts_(o_tt[:, m, :], ps[:, 4 + m % 4, 0:D], rden_att[:, m:m + 1], None, ALU.mult).then_inc(pv_sb.sem, 1)

            def layer_part(li, aside):
                dve.wait_ge(mlp_loaded.sem, mlp_loaded.at(li, 32))
                dve.wait_ge(qk4_ps.sem, qk4_ps.at(li, 1))
                nc.vector.memset(k_rot[:, :, 0:WIN], 0.0)

                for i in range(JOBS + 2):
                    if i >= 2:
                        hp, c, slot = (i - 2) // 2, i % 2, i % 2
                        dve.wait_ge(k_sum.sem, k_sum.at(li, i - 1))
                        dve.wait_ge(q_sum.sem, q_sum.at(li, i - 1))
                        dve.wait_ge(norm_ex.sem, norm_ex.at(li, i - 1))
                        stt(k_rot[:, hp, WIN + c * HALF:WIN + (c + 1) * HALF], rn_k[:, slot, :], 1e12, rot[:, slot, 2, :],
                            ALU.min, ALU.mult).then_inc(k_done.sem, 1)
                        dve.wait_ge(k_done.sem, k_done.at(li, i - 1))
                    if i < JOBS:
                        hp, c = i // 2, i % 2
                        for kind, scale in enumerate(("qs", "qs_r", "ks", "ks_r")):
                            dve.wait_ge(qk4_ps.sem, qk4_ps.at(li, 4 * i + kind + 1))
                            stt(rot[:, i % 2, kind, :], ps[:, kind, :], lv(scale), table[:, kind, c * HALF:(c + 1) * HALF],
                                ALU.mult, ALU.mult).then_inc(rotated.sem, 1)
                        next(aside, None)
                    if 1 <= i <= JOBS:
                        next(aside, None)
                dve.wait_ge(qn_ex.sem, qn_ex.at(li, 1))
                ts_(rn_q[:, :], rn_q[:, :], 1e12, None, ALU.min).then_inc(qn_cl.sem, 1)
                dve.wait_ge(qn_cl.sem, qn_cl.at(li, 1))

                def tops(n):
                    hp, m = n // NT, n % NT
                    dve.wait_ge(s_ps.sem, s_ps.at(li, n + 1))
                    nc.vector.tensor_reduce(top_s[:, n % 4, :], ps[:, 2 * (n % 2):2 * (n % 2) + 2, 0:KEYS], axis=AX,
                                            op=ALU.max).then_inc(s_top.sem, 1)
                    dve.wait_ge(s_top.sem, s_top.at(li, n + 1))
                    col = (hp * NT + m) * 2
                    stt(neg_top[:, n % 4, :], top_s[:, n % 4, :], -1.0, rn_q[:, col:col + 2], ALU.mult, ALU.mult).then_inc(s_neg.sem, 1)

                def copy_pt(n):
                    dve.wait_ge(pt_ps.sem, pt_ps.at(li, n + 1))
                    if n >= 3:
                        dve.wait_ge(o_ps.sem, o_ps.at(li, n - 2))
                    nc.vector.tensor_copy(pt_win[:, n % 3, :, :, :],
                                          ps[:, 4, :].rearrange("p (e c k) -> p e c k", e=2, c=2)).then_inc(pt_sb[1].sem, 1)

                def outputs(n):
                    hp, m = n // NT, n % NT
                    dve.wait_ge(o_ps.sem, o_ps.at(li, n + 1))
                    o = ps[:, 5, 0:2 * (DH + 1)].rearrange("p (e d) -> p e d", e=2)
                    nc.vector.reciprocal(rden[:, n % 2, :], o[:, :, DH]).then_inc(o_r.sem, 1)
                    dve.wait_ge(o_r.sem, o_r.at(li, n + 1))
                    if m == 0 and hp >= 2:
                        dve.wait_ge(ot_ps.sem, ot_ps.at(li, 2 * (hp - 1)))
                    tt(o_t[:, hp % 2, m, :].rearrange("p (e d) -> p e d", e=2), o[:, :, 0:DH],
                       rden[:, n % 2, :].rearrange("p (e u) -> p e u", u=1).broadcast_to((P, 2, DH)), ALU.mult).then_inc(o_sb.sem, 1)

                for n in range(STEPS + 3):
                    if n < STEPS:
                        tops(n)
                    if 1 <= n <= STEPS and n % 2 == 0:
                        copy_pt(n - 1)
                    if n >= 3:
                        outputs(n - 3)
                    next(aside, None)
                next(aside, None)
                dve.wait_ge(wo_ps.sem, wo_ps.at(li, 1))
                dve.wait_ge(shifted.sem, shifted.at(li, 2))
                tt(halves(y[:, :]), halves(y[:, :]), both(0), ALU.add).then_inc(y_mid.sem, 1)
                dve.wait_ge(lnl_tp.sem, lnl_tp.at(li, 1))
                moments(1, li, bank_tile(2), lnl_stats, lnl_mv)
                dve.wait_ge(lnl_rstd.sem, lnl_rstd.at(li, 1))
                normalise(1, ln_t, bank_tile(2)).then_inc(lnl_t.sem, 1)
                for u in range(UNITS):
                    j, c = u // 2, u % 2
                    n = CHUNKS[j][1]
                    dve.wait_ge(gelu_sb.sem, gelu_sb.at(li, u + 1))
                    stt(ff[0:n, j, c * HALF:(c + 1) * HALF], ps[0:n, 2 * (u % 3), :], lv(f"b1a{j}", n), gelus[0:n, u % 3, :],
                        ALU.add, ALU.mult).then_inc(up_sb.sem, 1)
                    next(aside, None)
                dve.wait_ge(down_ps.sem, down_ps.at(li, 1))
                stt(halves(y[:, :]), both(0), lv("b2"), halves(y[:, :]), ALU.add, ALU.add).then_inc(y_done.sem, 1)
                next(aside, None)

            def batch(b, aside):
                middle_part(b)
                for l in range(LAYERS):
                    layer_part(b * LAYERS + l, aside)
                for _ in aside:
                    pass
                dve.wait_ge(y_done.sem, y_done.at(b * LAYERS + LAYERS, 0))
                dve.wait_ge(ao_sb.sem, ao_sb.at(b, 1))
                tt(s_att[:, :], s_att[:, :], y[:, :], ALU.mult).then_inc(prod1.sem, 1)
                dve.wait_ge(prod1.sem, prod1.at(b, 1))
                dve.wait_ge(gate1.sem, gate1.at(b, 1))
                stt(s_att[:, :], e_b[:, :], 1.0, s_att[:, :], ALU.add, ALU.mult).then_inc(prod1.sem, 1)
                dve.wait_ge(prod1_ps.sem, prod1_ps.at(b, 1))
                stt(halves(top[:, 0:T]), both(0), 0.5, flat(x_mid), ALU.mult, ALU.add).then_inc(out_done.sem, 1)

            for _ in block0(0):
                pass
            with dve.Fori(0, B - 1) as b:
                batch(b, block0(b + 1))
            batch(B - 1, iter(()))

        @block.gpsimd
        def _(pool):
            add = nc.gpsimd.tensor_tensor

            def squares_of_relu(b):
                for j in range(4):
                    pool.wait_ge(kc_relu.sem, kc_relu.at(b, j + 1))
                    add(relus[j][:, 0:T], relus[j][:, 0:T], relus[j][:, 0:T], ALU.mult).then_inc(kc_sq.sem, 1)

            def sums(li):
                for i in range(JOBS):
                    hp, c = i // 2, i % 2
                    pool.wait_ge(rotated.sem, rotated.at(li, 4 * i + 2))
                    add(q_rot[:, hp, c * HALF:(c + 1) * HALF], rot[:, i % 2, 0, :], rot[:, i % 2, 1, :], ALU.add).then_inc(q_sum.sem, 1)
                    pool.wait_ge(rotated.sem, rotated.at(li, 4 * i + 4))
                    add(rot[:, i % 2, 2, :], rot[:, i % 2, 2, :], rot[:, i % 2, 3, :], ALU.add).then_inc(k_sum.sem, 1)

            squares_of_relu(0)
            with pool.Fori(0, B - 1) as b:
                sums(b * LAYERS)
                sums(b * LAYERS + 1)
                squares_of_relu(b + 1)
            for l in range(LAYERS):
                sums((B - 1) * LAYERS + l)


def _pad_rows(a, rows=P, cols=None):
    a = np.asarray(a, np.float32)
    if a.ndim == 1:
        return _pad_rows(a[:, None], rows)[:, 0]
    out = np.zeros((rows, cols or a.shape[1]), np.float32)
    out[:a.shape[0], :a.shape[1]] = a
    return out


def _column(a, repeat=False):
    a = np.asarray(a, np.float32).reshape(-1)
    return np.repeat(a, P) if repeat else _pad_rows(a)


def _by_chunk(a):
    a = _pad_rows(a, -(-a.shape[0] // P) * P)
    return a.reshape(-1, P, a.shape[1]).transpose(1, 0, 2).reshape(P, -1)


def _constants():
    const = np.zeros((P, CONST_COLS), np.float32)
    const[:, C_ID] = np.eye(P)
    quarter = np.arange(P // 4)
    twist = np.zeros((P, P), np.float32)
    for to, frm, sign in [(0, 64, 1), (32, 96, -1), (64, 0, -1), (96, 32, 1)]:
        twist[frm + quarter, to + quarter] = sign
    const[:, C_TW] = twist
    head = np.arange(P) // DH
    const[:, C_PAIR] = head[:, None] == head[None, :]
    const[:, C_HEAD] = head[:, None] == np.arange(2)[None, :]
    for name, value in [("eps", EPS), ("eps_sq", EPS * EPS), ("tiny", 2.0 ** -64), ("ln_1024", np.log(1024.0)),
                        ("half_pi", np.pi / 2)]:
        const[:, C_CST + CST[name]] = value
    f = np.float32
    half = np.arange(0, DH, 2, dtype=f)
    freq = (f(1.0) / f(10000.0) ** (half / f(DH))).astype(f)
    t = np.arange(T, dtype=f)
    angle = (t[None, :] * freq[:, None]).astype(f)
    base = (half + f(0.4 * DH)) / f(1.4 * DH)
    scale = base[:, None].astype(f) ** ((t - T // 2) / f(WIN // 2))[None, :]
    cos, sin = np.cos(angle), np.sin(angle)
    sign_rows = lambda a: np.concatenate([-a, a, -a, a])
    table = np.stack([np.tile(cos * scale, (4, 1)) * f(QK_SCALE), sign_rows(sin * scale) * f(QK_SCALE),
                      np.tile(cos / scale, (4, 1)), sign_rows(sin / scale)], axis=1).astype(f)
    q, k = np.arange(P)[:, None], np.arange(KEYS)[None, :]
    band = (k >= q) & (k <= q + WIN)
    mask = np.concatenate([np.eye(P), np.where(band, 0.0, -1e30), np.where(band & (k >= WIN), 0.0, -1e30)], axis=1)
    return const, np.ascontiguousarray(table), mask.astype(f)


def _layout(i):
    f = lambda n: np.asarray(i[n], np.float32)
    A, G, C, W = "L0_attn_", "L0_ffn_", "L1_attn_", "L1_ffn_"
    wide = lambda a: np.repeat(a, P, axis=1)
    front = np.concatenate([
        f(A + "Wk").T, f(A + "Wv").T, f(A + "Wr").T, f(A + "Wcr").T, f(A + "Wck").T, _by_chunk(f(A + "Wcv").T),
        f(G + "cn_w1"), f(G + "cn_w2"), _pad_rows(f(G + "cn_w3"), cols=P), _pad_rows(wide(f(G + "cn_w4"))),
        f(G + "gc_w1"), _pad_rows(f(G + "gc_w2"), cols=P), _pad_rows(wide(f(G + "gc_w3"))),
        f(C + "Wq").T, f(C + "Wk").T, f(C + "Wv").T, f(C + "Wo").T], axis=1)
    vec = np.stack([_column(f(n), repeat=n.endswith(("cn_b4", "gc_b3", "range"))) for n in
                    [A + "ln1_w", A + "ln1_b", A + "ln2_w", A + "ln2_b", A + "time_shift", A + "time_first",
                     G + "cn_b1", G + "cn_b2", G + "cn_b3", G + "cn_b4", G + "gc_b1", G + "gc_b2", G + "gc_b3",
                     G + "adaptive_range", C + "wavelengths", C + "phase_bias", C + "bq", C + "bk", C + "bv", C + "bo"]], axis=1)
    swap = (np.arange(DH) + DH // 2) % DH
    layers, mlps, lvecs = [], [], []
    for l in range(LAYERS):
        wqkv = f(W + "wqkv")[l].reshape(D, 3, PAIRS, 2, DH)
        q, k, v = wqkv[:, 0], wqkv[:, 1], wqkv[:, 2]
        wqk = np.stack([q, q[..., swap], k, k[..., swap]], axis=1)
        layers.append(np.concatenate([wqk.reshape(D, -1), v.reshape(D, -1), _by_chunk(f(W + "wo")[l])], axis=1))
        mlps.append(np.concatenate([f(W + "w1")[l], _by_chunk(f(W + "w2")[l])], axis=1))
        qs, ks, b1 = f(W + "q_scale")[l], f(W + "k_scale")[l], f(W + "b1")[l]
        two = lambda a: np.concatenate([a, a])
        lvecs.append(np.stack(
            [two(qs), two(qs[swap]), two(ks), two(ks[swap]), f(W + "ln_g")[l], f(W + "ln_b")[l]]
            + [_column(b1[o + lo:o + lo + n]) for o in (0, HID) for lo, n in CHUNKS] + [f(W + "b2")[l]], axis=1))
    return front, vec, np.stack(layers), np.stack(mlps), np.stack(lvecs)


def kernel(**inputs):
    import concourse.bacc as bacc
    from concourse.bass_utils import run_bass_kernel_spmd

    front, vec, layers, mlps, lvecs = _layout(inputs)
    const, table, mask = _constants()
    arrays = {"x": np.asarray(inputs["L0_attn_x"]), "front": front, "vec": vec, "layers": layers, "mlps": mlps,
              "lvecs": lvecs, "const": const, "table": table, "mask": mask}
    arrays = {"in_" + n: np.ascontiguousarray(a) for n, a in arrays.items()}
    nc = bacc.Bacc("TRN2", target_bir_lowering=False, num_devices=1)
    args = [nc.dram_tensor(n, a.shape, mybir.dt.from_np(a.dtype), kind="ExternalInput").ap() for n, a in arrays.items()]
    out = nc.dram_tensor("out", (B, T, D), F32, kind="ExternalOutput").ap()
    build(nc, *args, out)
    r = run_bass_kernel_spmd(nc, [arrays], core_ids=[0])
    return r.results[0]["out"]
```

```python
from contextlib import ExitStack

import numpy as np
import concourse.bass as bass
from concourse import mybir
from concourse.alu_op_type import AluOpType as ALU

F32 = mybir.dt.float32
BF16 = mybir.dt.bfloat16
ACT = mybir.ActivationFunctionType
AX = mybir.AxisListType.X

B, T, D = 8, 1024, 128
P = 128
NT = T // P
HALF = 512
LAYERS = 2
HEADS, DH, WIN = 8, 64, 64
INNER = HEADS * DH
PAIRS = HEADS // 2
HID = int(D * 4 * 2 / 3)
CHUNKS = [(0, 128), (128, 128), (256, HID - 256)]
KEYS = P + WIN
EPS = 1e-5
QK_SCALE = 8.0
CYCLES = 3
FF = 4 * D
TWO_PI = 6.283185307179586
PI2_A = 6.28125
PI2_B = float(np.float32(0.0019350051879882812))
PI2_C = TWO_PI - PI2_A - PI2_B
ROUND = 12582912.0
PI_IN = float(np.nextafter(np.float32(np.pi), np.float32(0)))

FRONT = {}
_at = 0
for _name, _cols in [("wk", D), ("wv", D), ("wr", D), ("wcr", D), ("wck", FF), ("wcv", FF),
                     ("cn1", 128), ("cn2", 64), ("cn3", 128), ("cn4", 128),
                     ("gc1", 64), ("gc2", 128), ("gc3", 128),
                     ("aq", D), ("ak", D), ("av", D), ("ao", D)]:
    FRONT[_name] = slice(_at, _at + _cols)
    _at += _cols
FRONT_COLS = _at

VEC = {n: i for i, n in enumerate(
    ["ln1_w", "ln1_b", "ln2_w", "ln2_b", "ts", "u", "cn_b1", "cn_b2", "cn_b3", "cn_b4",
     "gc_b1", "gc_b2", "gc_b3", "ar", "wave", "phase", "bq", "bk", "bv", "bo"])}
CST = {n: i for i, n in enumerate(["eps", "eps_sq", "tiny", "ln_1024", "half_pi"])}
DER = {n: i for i, n in enumerate(
    ["neg_ts", "one_plus_ts", "one_minus_ts", "half_gc_b3", "half_cn_b4", "ar7", "ar3",
     "inv_wave", "theta_q0", "theta_k0", "wave_eps", "half_u"])}
LVEC = {n: i for i, n in enumerate(
    ["qs", "qs_r", "ks", "ks_r", "ln_g", "ln_b", "b1a0", "b1a1", "b1a2", "b1g0", "b1g1", "b1g2", "b2"])}
C_ID, C_TW, C_PAIR, C_HEAD = slice(0, 128), slice(128, 256), slice(256, 384), slice(384, 386)
C_CST = 386
CONST_COLS = C_CST + len(CST)
WQK_COLS = 4 * PAIRS * P
LAYER_COLS = WQK_COLS + INNER + PAIRS * D
MLP_COLS = 2 * HID + len(CHUNKS) * D


class Signal:

    def __init__(self, ctx, nc, name, per, raised=0):
        self.sem = ctx.enter_context(nc.semaphore(name))
        self.per = per
        self.raised = raised

    def at(self, turn, n):
        return turn * self.per + n + self.raised


def build(nc, x_d, front_d, vec_d, layer_d, mlp_d, lvec_d, const_d, table_d, mask_d, out_d):
    ctx = ExitStack()
    with ctx:
        def sb(name, shape, dt=F32):
            return ctx.enter_context(nc.sbuf_tensor(name, shape, dt))

        front = sb("front_w", [P, FRONT_COLS])
        vec = sb("vec", [P, len(VEC)])
        der = sb("derived_vec", [P, len(DER)])
        const = sb("const", [P, CONST_COLS])
        table = sb("rotary_table", [P, 4, T])
        mask = sb("mask", [P, P + 2 * KEYS], BF16)
        layer_w = sb("layer_w", [P, LAYER_COLS])
        mlp_w = sb("mlp_w", [P, MLP_COLS])
        lvec = sb("lvec", [P, len(LVEC)])
        ident = const[:, C_ID]
        twist = const[:, C_TW]
        pair_ones = const[:, C_PAIR]
        head_ones = const[:, C_HEAD]
        ident16 = mask[:, 0:P]
        band_mask, first_mask = mask[:, P:P + KEYS], mask[:, P + KEYS:]

        def w(name, rows=P):
            return front[0:rows, FRONT[name]]

        def v(name, rows=P):
            return vec[0:rows, VEC[name]:VEC[name] + 1]

        def dv(name):
            return der[:, DER[name]:DER[name] + 1]

        def cst(name):
            return const[:, C_CST + CST[name]:C_CST + CST[name] + 1]

        def lv(name, rows=P):
            return lvec[0:rows, LVEC[name]:LVEC[name] + 1]

        x_in = sb("x_in", [P, NT, D])
        x_mid = sb("x_mid", [P, NT, D])
        y = sb("y", [P, T])
        s_att = sb("s_att", [P, T])
        stats = sb("stats", [P, 2, NT, 6])
        mv = sb("mean_var", [P, 2, NT, 2])
        log_a = sb("log_a", [P, 2, NT])
        seed = sb("seed", [P, 4])
        carrier = sb("carrier", [P, 2])
        log_b = sb("log_b", [P, NT])
        rstd = sb("rstd", [P, 2, NT])
        rstd2 = sb("rstd2", [P, NT])
        xn = sb("xn", [P, T])
        xn1 = sb("xn1", [P, T])
        k_c = sb("k_c", [P, T])
        v_c = sb("v_c", [P, T])
        r_c = sb("r_c", [P, T])
        z_c = sb("z_c", [P, T])
        e_a = sb("e_a", [P, T])
        e_b = sb("e_b", [P, T])
        top = sb("top", [P, T + 1])
        aa = sb("aa", [P, T + 1])
        h_pad = sb("h_pad", [P, T + 1])

        def as_t(a):
            return a[:, 0:T].rearrange("p (n d) -> p n d", n=NT)

        xn_tt, hn_tt, y_tt = as_t(top), as_t(e_b), as_t(z_c)
        relus = [k_c, v_c, aa, top]
        work = sb("work", [P, 4 * T])
        at = [0]

        def cut(cols):
            at[0] += cols
            return work[:, at[0] - cols:at[0]]

        rot = cut(4 * T).rearrange("p (i k n) -> p i k n", i=2, k=4)
        out_tt, gate_c, o_tt = as_t(work[:, 0:T]), work[:, T:2 * T], as_t(work[:, 2 * T:3 * T])
        att_c = work[:, 3 * T:4 * T]
        at[0] = 0
        pt_win = cut(3 * HALF).rearrange("p (i e c k) -> p i e c k", i=3, e=2, c=2)
        mean_c = sb("mean_c", [P, 1])
        g1 = sb("g1", [P, 1])
        g2 = sb("g2", [P, 1])
        tg = sb("tg", [P, 1])
        c0 = sb("c0", [P, 1])
        big = sb("big", [P, PAIRS * T + PAIRS * (T + WIN)])
        q_rot = big[:, 0:PAIRS * T].rearrange("p (h t) -> p h t", h=PAIRS)
        k_rot = big[:, PAIRS * T:].rearrange("p (h t) -> p h t", h=PAIRS)
        p_att = big[:, 0:NT * T].rearrange("p (k t) -> p k t", k=NT)
        ln_t = as_t(big)
        ln_c = big[:, T:2 * T]
        gelus = big[:, 2 * T:2 * T + 3 * HALF].rearrange("p (i n) -> p i n", i=3)
        ff = sb("ff", [P, PAIRS, T])
        v_win = sb("v_win", [P, NT, HEADS, DH])
        squares = ff[:, 0:2, :].rearrange("p i (k n) -> p i k n", k=2)
        rn_k = ff[:, 2, :].rearrange("p (i n) -> p i n", i=2)
        v_att = sb("v_att", [P, NT, D + 1])
        p_win = sb("p_win", [P, 4, 2, 2 * P])
        h_s = sb("h_s", [P, T])
        rn_q = sb("rn_q", [P, PAIRS * NT * 2])
        top_s = sb("top_s", [P, 4, 2])
        neg_top = sb("neg_top", [P, 4, 2])
        den = sb("den", [P, 4, 2])
        rden = sb("rden", [P, 4, 2])
        rden_att = sb("rden_att", [P, NT])

        ps = ctx.enter_context(nc.psum_tensor("ps", [P, 8, HALF], F32))

        def both(n):
            return ps[:, n:n + 2, :]

        def flat(a):
            return a[:, :, :].rearrange("p (c n) d -> p c (n d)", c=2)

        def halves(a):
            return a.rearrange("p (c n) -> p c n", c=2)

        def sig(name, per=1, raised=0):
            return Signal(ctx, nc, name, per, raised)

        w_in = sig("w_in")
        ready0 = sig("setup_done")
        setup = sig("setup_step")
        x_loaded = sig("x_loaded", 16)
        lw_loaded = sig("lw_loaded", 16)
        mlp_loaded = sig("mlp_loaded", 32)
        out_sent = sig("out_sent", 16, raised=1)
        ln0_stats, ln0_mv, ln0_logs, ln0_logd, ln0_rstd = (
            sig("ln0_stats"), sig("ln0_mv"), sig("ln0_logs", 2), sig("ln0_logd"), sig("ln0_rstd", 2))
        xn_t, hn_t = sig("xn_t"), sig("hn_t")
        xn_ps, hn_ps = sig("xn_ps"), sig("hn_ps")
        xn_c, h_c = sig("xn_c"), sig("h_c")
        hpad0 = sig("hpad0")
        mix_a, mixed = sig("mix_a"), sig("mixed")
        k_ps, v_ps, r_ps, k_sb, v_sb = sig("k_ps"), sig("v_ps"), sig("r_ps"), sig("k_sb"), sig("v_sb")
        wkv = sig("wkv_step", 15)
        wkv_exp, wkv_ln, wkv_exp2, wkv_gate, r_sb = (
            sig("wkv_exp", 2), sig("wkv_ln"), sig("wkv_exp2", 2), sig("wkv_gate"), sig("r_sb"))
        x1_ps, ln2_stats, ln2_mv, ln2_log, ln2_rstd = (
            sig("x1_ps"), sig("ln2_stats"), sig("ln2_mv"), sig("ln2_log"), sig("ln2_rstd"))
        h2_t, h2_ps, h2_c = sig("h2_t"), sig("h2_ps"), sig("h2_c")
        mix2 = sig("mix2", 3)
        kc_ps, kc_relu, kc_sq = sig("kc_ps", 4), sig("kc_relu", 4), sig("kc_sq", 4)
        rc_ps, vv_ps, rc_sb, s_mul, s_done = sig("rc_ps"), sig("vv_ps"), sig("rc_sb"), sig("s_mul"), sig("s_done")

        mean_done, gc_ps, gc_sb, gc_c0 = sig("mean_done"), sig("gc_ps", 3), sig("gc_sb", 3), sig("gc_c0")
        cn_ps, cn_sb = sig("cn_ps", 5 * CYCLES), sig("cn_sb", 4 * CYCLES)
        cycle = sig("cycle", 3 * CYCLES)
        gate0, prod0, prod0_ps, x_new = sig("gate0"), sig("prod0", 2), sig("prod0_ps"), sig("x_new")
        y_in, x_mid_done = sig("y_in"), sig("x_mid_done")
        ln3_stats, ln3_mv, ln3_log, ln3_rstd = sig("ln3_stats"), sig("ln3_mv"), sig("ln3_log"), sig("ln3_rstd")
        y_t, y_ps, y_c = sig("y_t"), sig("y_ps"), sig("y_c")
        qk_ps, theta, reduce_s, reduced = sig("qk_ps", 2), sig("theta", 2), sig("reduce_s", 10), sig("reduced", 2)
        va_ps, va_sb, abs_s, trig = sig("va_ps"), sig("va_sb"), sig("abs_s", 2), sig("trig", 4)
        sim_ps, sim_exp = sig("sim_ps", 2 * NT), sig("sim_exp", 2 * NT)
        pv_ps, pv_r, pv_sb = sig("pv_ps", NT), sig("pv_r", NT), sig("pv_sb", NT)
        at_ps, at_sb, ao_ps, ao_sb = sig("at_ps"), sig("at_sb"), sig("ao_ps"), sig("ao_sb")
        gate1, prod1, prod1_ps, out_done = sig("gate1"), sig("prod1", 2), sig("prod1_ps"), sig("out_done", raised=1)
        UNITS = 2 * len(CHUNKS)
        JOBS = PAIRS * 2
        STEPS = PAIRS * NT
        TURN = 2
        LAG = TURN + 1
        STEP_SLOTS = (0, 2, 4, 6)
        TAIL_SLOTS = 4 + UNITS
        shifted, copied, copied2 = sig("shifted"), sig("copied"), sig("copied2")
        qk4_ps, vw_ps, vw_sb = sig("qk4_ps", 4 * JOBS), sig("vw_ps", NT), sig("vw_sb", NT)
        sq_sb, norm_ps, norm_ln, norm_ex = sig("sq_sb", 2 * JOBS), sig("norm_ps", JOBS), sig("norm_ln", JOBS), sig("norm_ex", JOBS)
        qn_ln, qn_ex, qn_cl = sig("qn_ln", JOBS), sig("qn_ex"), sig("qn_cl")
        rotated, q_sum, k_sum, k_done = sig("rotated", 4 * JOBS), sig("q_sum", JOBS), sig("k_sum", JOBS), sig("k_done", JOBS)
        s_ps, s_top, s_neg, p_sb = sig("s_ps", STEPS), sig("s_top", STEPS), sig("s_neg", STEPS), sig("p_sb", STEPS)
        pt_ps = sig("pt_ps", STEPS)
        pt_sb = [sig("pt_sb_act", STEPS // 2), sig("pt_sb_dve", STEPS // 2)]
        p_den, p_norm = sig("p_den", STEPS), sig("p_norm", STEPS)
        o_ps, o_sb = sig("o_ps", STEPS), sig("o_sb", STEPS)
        wo_half, wo_ps, y_mid = sig("wo_half"), sig("wo_ps", raised=1), sig("y_mid")
        shifted2, lnl_tp, lnl_stats, lnl_mv, lnl_log, lnl_rstd = (
            sig("shifted2"), sig("lnl_tp"), sig("lnl_stats"), sig("lnl_mv"), sig("lnl_log"), sig("lnl_rstd"))
        lnl_t, lnl_ps, lnl_c = sig("lnl_t", 2), sig("lnl_ps", 2), sig("lnl_c", 2)
        up_ps, gelu_sb, up_sb = sig("up_ps", UNITS), sig("gelu_sb", UNITS), sig("up_sb", UNITS)
        down_ps, y_done = sig("down_ps", 2), sig("y_done", raised=1)

        block = ctx.enter_context(nc.Block())

        @block.sync
        def _(sp):
            sp.dma_start(front[:, :], front_d).then_inc(w_in.sem, 16)
            sp.dma_start(vec[:, :], vec_d).then_inc(w_in.sem, 16)
            sp.dma_start(const[:, :], const_d).then_inc(w_in.sem, 16)
            sp.dma_start(table[:, :, :], table_d).then_inc(w_in.sem, 16)
            sp.dma_start(work[:, 0:P + 2 * KEYS], mask_d).then_inc(w_in.sem, 16)
            def tokens(a, b):
                return a[b].rearrange("(n p) c -> p n c", p=P)

            def batch(b, more):
                if more:
                    sp.wait_ge(x_mid_done.sem, x_mid_done.at(b, 1))
                    sp.dma_start(x_in[:, :, :], tokens(x_d, b + 1)).then_inc(x_loaded.sem, 16)
                for l in range(LAYERS):
                    li = b * LAYERS + l
                    sp.wait_ge(wo_ps.sem, wo_ps.at(li, 0))
                    sp.dma_start(layer_w[:, :], layer_d[l]).then_inc(lw_loaded.sem, 16)
                    sp.wait_ge(y_done.sem, y_done.at(li, 0))
                    sp.dma_start(mlp_w[:, :], mlp_d[l]).then_inc(mlp_loaded.sem, 16)
                    sp.dma_start(lvec[:, :], lvec_d[l]).then_inc(mlp_loaded.sem, 16)
                sp.wait_ge(out_done.sem, out_done.at(b, 1))
                sp.dma_start(tokens(out_d, b), out_tt).then_inc(out_sent.sem, 16)

            sp.dma_start(x_in[:, :, :], tokens(x_d, 0)).then_inc(x_loaded.sem, 16)
            with sp.Fori(0, B - 1) as b:
                batch(b, True)
            batch(B - 1, False)
            sp.wait_ge(out_sent.sem, out_sent.at(B, 0))

        @block.tensor
        def _(pe):
            mm = nc.tensor.matmul

            def two(bank, lhsT, rhs, rows=P, start=True, stop=True):
                for c in range(2):
                    last = mm(ps[0:rows, bank + c, :], lhsT, rhs[:, c * HALF:(c + 1) * HALF], start=start, stop=stop)
                return last

            def turn8(bank, tiles):
                for i in range(NT):
                    last = nc.tensor.transpose(ps[:, bank + i // 4, (i % 4) * P:(i % 4 + 1) * P], tiles(i), ident)
                return last

            pe.wait_ge(ready0.sem, 1)

            def block0(b):
                for _ in range(6):
                    yield
                pe.wait_ge(hn_t.sem, hn_t.at(b, 1))
                turn8(6, lambda i: hn_tt[:, i, :]).then_inc(hn_ps.sem, 1)
                yield
                yield
                pe.wait_ge(h_c.sem, h_c.at(b, 1))
                turn8(6, lambda i: xn_tt[:, i, :]).then_inc(xn_ps.sem, 1)
                yield
                yield
                yield
                pe.wait_ge(mixed.sem, mixed.at(b, 1))
                pe.wait_ge(xn_c.sem, xn_c.at(b, 1))
                two(6, w("wk"), z_c[:, :]).then_inc(k_ps.sem, 1)
                yield
                yield
                pe.wait_ge(k_sb.sem, k_sb.at(b, 1))
                two(6, w("wv"), z_c[:, :]).then_inc(v_ps.sem, 1)
                yield
                yield
                pe.wait_ge(v_sb.sem, v_sb.at(b, 1))
                two(6, w("wr"), z_c[:, :]).then_inc(r_ps.sem, 1)
                yield
                yield
                pe.wait_ge(r_sb.sem, r_sb.at(b, 1))
                pe.wait_ge(mean_done.sem, mean_done.at(b, 1))
                mm(ps[0:64, 6, 0:1], w("gc1"), mean_c[:, :], start=True, stop=True).then_inc(gc_ps.sem, 1)
                yield
                yield
                pe.wait_ge(gc_sb.sem, gc_sb.at(b, 1))
                mm(ps[:, 6, 1:2], w("gc2", 64), g1[0:64, :], start=True, stop=True).then_inc(gc_ps.sem, 1)
                yield
                yield
                pe.wait_ge(gc_sb.sem, gc_sb.at(b, 2))
                mm(ps[:, 6, 2:3], w("gc3", 32), g2[0:32, :], start=True, stop=True).then_inc(gc_ps.sem, 1)
                for _ in range(10):
                    yield
                pe.wait_ge(gc_sb.sem, gc_sb.at(b, 3))
                pe.wait_ge(wkv.sem, wkv.at(b, 15))
                for cy in range(CYCLES):
                    if cy:
                        pe.wait_ge(cycle.sem, cycle.at(b, 3 * cy))
                    two(6, w("cn1"), xn[:, :]).then_inc(cn_ps.sem, 1)
                    yield
                    yield
                    pe.wait_ge(cn_sb.sem, cn_sb.at(b, 4 * cy + 1))
                    two(6, w("cn2"), k_c[:, :], rows=64).then_inc(cn_ps.sem, 1)
                    yield
                    yield
                    pe.wait_ge(cn_sb.sem, cn_sb.at(b, 4 * cy + 2))
                    two(6, w("cn3", 64), v_c[0:64, :]).then_inc(cn_ps.sem, 1)
                    yield
                    yield
                    pe.wait_ge(cn_sb.sem, cn_sb.at(b, 4 * cy + 3))
                    two(6, w("cn4", 32), aa[0:32, 0:T]).then_inc(cn_ps.sem, 1)
                    yield
                    yield
                    pe.wait_ge(cn_sb.sem, cn_sb.at(b, 4 * cy + 4))
                    two(6, twist, xn[:, :]).then_inc(cn_ps.sem, 1)
                    yield
                    yield
                pe.wait_ge(cycle.sem, cycle.at(b, 3 * CYCLES))
                turn8(6, lambda i: xn1[:, i * P:(i + 1) * P]).then_inc(x1_ps.sem, 1)
                for _ in range(4):
                    yield
                pe.wait_ge(h2_t.sem, h2_t.at(b, 1))
                turn8(6, lambda i: e_b[:, i * P:(i + 1) * P]).then_inc(h2_ps.sem, 1)
                for _ in range(4):
                    yield
                pe.wait_ge(mix2.sem, mix2.at(b, 3))
                for j in range(4):
                    if j:
                        pe.wait_ge(kc_relu.sem, kc_relu.at(b, j))
                    two(6, w("wck")[:, j * P:(j + 1) * P], z_c[:, :]).then_inc(kc_ps.sem, 1)
                    yield
                    yield
                pe.wait_ge(kc_relu.sem, kc_relu.at(b, 4))
                two(6, w("wcr"), z_c[:, :]).then_inc(rc_ps.sem, 1)
                yield
                yield
                pe.wait_ge(rc_sb.sem, rc_sb.at(b, 1))
                for c in range(2):
                    for j in range(4):
                        pe.wait_ge(kc_sq.sem, kc_sq.at(b, j + 1))
                        last = mm(ps[:, 6 + c, :], w("wcv")[:, j * P:(j + 1) * P], relus[j][:, c * HALF:(c + 1) * HALF],
                                  start=(j == 0), stop=(j == 3))
                last.then_inc(vv_ps.sem, 1)
                for _ in range(5):
                    yield
                pe.wait_ge(prod0.sem, prod0.at(b, 2))
                turn8(6, lambda i: e_a[:, i * P:(i + 1) * P]).then_inc(prod0_ps.sem, 1)
                for _ in range(4):
                    yield
                pe.wait_ge(y_t.sem, y_t.at(b, 1))
                turn8(6, lambda i: y_tt[:, i, :]).then_inc(y_ps.sem, 1)
                yield
                yield
                pe.wait_ge(y_c.sem, y_c.at(b, 1))
                two(6, w("aq"), xn1[:, :]).then_inc(qk_ps.sem, 1)
                yield
                yield
                pe.wait_ge(theta.sem, theta.at(b, 1))
                two(6, w("ak"), xn1[:, :]).then_inc(qk_ps.sem, 1)
                yield
                yield
                pe.wait_ge(theta.sem, theta.at(b, 2))
                for i in range(NT):
                    last = mm(ps[:, 6 + i // 4, (i % 4) * P:(i % 4 + 1) * P], xn1[:, i * P:(i + 1) * P], w("av"),
                              start=True, stop=True)
                last.then_inc(va_ps.sem, 1)
                yield

            def finish(bn):
                pe.wait_ge(prod1.sem, prod1.at(bn, 0))
                turn8(4, lambda i: s_att[:, i * P:(i + 1) * P]).then_inc(prod1_ps.sem, 1)

            def similarities(b, after):
                pe.wait_ge(trig.sem, trig.at(b, 4))
                for n in range(2 * NT):
                    c, kt = n // NT, n % NT
                    if n == 2:
                        pe.wait_ge(y_done.sem, y_done.at(b * LAYERS, 0))
                    if n == NT and after:
                        finish(b)
                    if n >= 4:
                        pe.wait_ge(sim_exp.sem, sim_exp.at(b, n - 3))
                    for f, (kf, qf) in enumerate([(e_b, e_a), (v_c, k_c)]):
                        last = mm(ps[:, (n + 2) % 4, :], kf[:, kt * P:(kt + 1) * P], qf[:, c * HALF:(c + 1) * HALF],
                                  start=(f == 0), stop=(f == 1))
                    last.then_inc(sim_ps.sem, 1)

            def middle_part(b, aside):
                pe.wait_ge(va_sb.sem, va_sb.at(b, 1))
                pe.wait_ge(out_done.sem, out_done.at(b, 0))
                for m in range(NT):
                    pe.wait_ge(sim_exp.sem, sim_exp.at(b, NT if m < NT // 2 else 2 * NT))
                    if m >= 2:
                        pe.wait_ge(pv_sb.sem, pv_sb.at(b, m - 1))
                    for kt in range(NT):
                        last = mm(ps[:, 4 + m % 2, 0:D + 1], p_att[:, kt, m * P:(m + 1) * P], v_att[:, kt, :],
                                  start=(kt == 0), stop=(kt == NT - 1))
                    last.then_inc(pv_ps.sem, 1)
                    next(aside, None)
                pe.wait_ge(pv_sb.sem, pv_sb.at(b, NT))
                turn8(0, lambda i: o_tt[:, i, :]).then_inc(at_ps.sem, 1)
                pe.wait_ge(at_sb.sem, at_sb.at(b, 1))
                two(4, w("ao"), att_c).then_inc(ao_ps.sem, 1)

            def layer_part(li, b, l, aside):
                wqk = layer_w[:, 0:WQK_COLS].rearrange("p (k h d) -> p k h d", k=4, h=PAIRS)
                wv = layer_w[:, WQK_COLS:WQK_COLS + INNER]
                wo = layer_w[:, WQK_COLS + INNER:].rearrange("p (h d) -> p h d", h=PAIRS)
                w1 = mlp_w[:, 0:2 * HID]
                w2 = mlp_w[:, 2 * HID:].rearrange("p (j d) -> p j d", j=len(CHUNKS))
                pe.wait_ge(lw_loaded.sem, lw_loaded.at(li, 16))
                pe.wait_ge(y_done.sem, y_done.at(li, 0))
                pe.wait_ge(shifted.sem, shifted.at(li, 1))
                pe.wait_ge(copied.sem, copied.at(li, 1))
                for i in range(JOBS + 1):
                    hp, c = i // 2, i % 2
                    if i < JOBS:
                        cols = h_s[:, c * HALF:(c + 1) * HALF]
                        for kind in range(4):
                            if kind == 3:
                                if i >= 2:
                                    pe.wait_ge(qn_ln.sem, qn_ln.at(li, i - 1))
                                if i == 1:
                                    pe.wait_ge(vw_sb.sem, vw_sb.at(li, 1))
                                if i == 0 and l == 0:
                                    pe.wait_ge(ao_sb.sem, ao_sb.at(b, 1))
                                mm(ps[:, 4, :], h_s[:, i * P:(i + 1) * P], wv, start=True, stop=True).then_inc(vw_ps.sem, 1)
                            if i and kind % 2:
                                pe.wait_ge(rotated.sem, rotated.at(li, 4 * (i - 1) + kind + 1))
                            elif i:
                                pe.wait_ge(sq_sb.sem, sq_sb.at(li, 2 * (i - 1) + kind // 2 + 1))
                            mm(ps[:, kind, :], wqk[:, kind, hp, :], cols, start=True, stop=True).then_inc(qk4_ps.sem, 1)
                        next(aside, None)
                    if i:
                        pe.wait_ge(sq_sb.sem, sq_sb.at(li, 2 * i))
                        if i >= 2:
                            pe.wait_ge(norm_ln.sem, norm_ln.at(li, i - 1))
                        mm(ps[:, 5, :], pair_ones, squares[:, (i - 1) % 2, 1, :], start=True, stop=True)
                        pe.wait_ge(vw_sb.sem, vw_sb.at(li, min(i + 1, JOBS)))
                        if i == JOBS:
                            pe.wait_ge(qn_ln.sem, qn_ln.at(li, i - 1))
                        for t in range(4):
                            last = mm(ps[:, 4, 2 * t:2 * t + 2], squares[:, (i - 1) % 2, 0, t * P:(t + 1) * P], head_ones,
                                      start=True, stop=True)
                        last.then_inc(norm_ps.sem, 1)
                        next(aside, None)

                def scores(n):
                    hp, m = n // NT, n % NT
                    bank = 2 * (n % 2)
                    if m == 0:
                        pe.wait_ge(k_done.sem, k_done.at(li, 2 * hp + 2))
                        pe.wait_ge(q_sum.sem, q_sum.at(li, 2 * hp + 2))
                    if n == 0:
                        pe.wait_ge(sq_sb.sem, sq_sb.at(li, 2 * JOBS))
                        pe.wait_ge(rotated.sem, rotated.at(li, 4 * JOBS))
                    if n >= 2:
                        pe.wait_ge(p_sb.sem, p_sb.at(li, n - 1))
                    for e in range(2):
                        mm(ps[:, bank + e, 0:KEYS], ident16, first_mask if m == 0 else band_mask, start=True, stop=False)
                    for e in range(2):
                        rows = slice(e * DH, (e + 1) * DH)
                        last = mm(ps[:, bank + e, 0:KEYS], q_rot[rows, hp, m * P:(m + 1) * P],
                                  k_rot[rows, hp, m * P:m * P + KEYS], start=False, stop=True)
                    last.then_inc(s_ps.sem, 1)

                def turn_p(n):
                    m = n % NT
                    if n == 0:
                        pe.wait_ge(qn_ln.sem, qn_ln.at(li, JOBS))
                        pe.wait_ge(norm_ln.sem, norm_ln.at(li, JOBS))
                    pe.wait_ge(p_norm.sem, p_norm.at(li, n + 1))
                    if n:
                        pe.wait_ge(pt_sb[(n - 1) % 2].sem, pt_sb[(n - 1) % 2].at(li, (n - 1) // 2 + 1))
                    for e in range(2):
                        for ch in range(2):
                            if m or ch:
                                last = nc.tensor.transpose(ps[:, 4, (2 * e + ch) * P:(2 * e + ch + 1) * P],
                                                           p_win[:, n % 4, e, ch * P:(ch + 1) * P], ident)
                    last.then_inc(pt_ps.sem, 1)

                def values(n):
                    hp, m = n // NT, n % NT
                    pe.wait_ge(pt_sb[n % 2].sem, pt_sb[n % 2].at(li, n // 2 + 1))
                    if n:
                        pe.wait_ge(o_sb.sem, o_sb.at(li, n))
                    for e in range(2):
                        for ch in range(2):
                            if m or ch:
                                last = mm(ps[e * DH:(e + 1) * DH, 5, 0:P], v_win[:, m - 1 + ch, 2 * hp + e, :],
                                          pt_win[:, n % 3, e, ch, :], start=(ch == 0 or m == 0), stop=(ch == 1))
                    last.then_inc(o_ps.sem, 1)

                for n in range(STEPS + LAG):
                    if n < STEPS:
                        scores(n)
                    if TURN <= n < STEPS + TURN:
                        turn_p(n - TURN)
                    if n >= LAG:
                        values(n - LAG)
                    if n % 8 in STEP_SLOTS:
                        next(aside, None)
                pe.wait_ge(o_sb.sem, o_sb.at(li, STEPS))
                for c in range(2):
                    for hp in range(PAIRS):
                        last = mm(ps[:, c, :], wo[:, hp, :], ff[:, hp, c * HALF:(c + 1) * HALF],
                                  start=(hp == 0), stop=(hp == PAIRS - 1))
                    if c == 0:
                        last.then_inc(wo_half.sem, 1)
                last.then_inc(wo_ps.sem, 1)
                next(aside, None)
                pe.wait_ge(shifted2.sem, shifted2.at(li, 1))
                pe.wait_ge(copied2.sem, copied2.at(li, 1))
                turn8(2, lambda i: h_s[:, i * P:(i + 1) * P]).then_inc(lnl_tp.sem, 1)
                next(aside, None)
                for c in range(2):
                    pe.wait_ge(lnl_t.sem, lnl_t.at(li, c + 1))
                    for t in range(4):
                        last = nc.tensor.transpose(ps[:, 4 + c, t * P:(t + 1) * P], ln_t[:, 4 * c + t, :], ident)
                    last.then_inc(lnl_ps.sem, 1)
                next(aside, None)
                pe.wait_ge(mlp_loaded.sem, mlp_loaded.at(li, 32))
                for u in range(UNITS):
                    j, c = u // 2, u % 2
                    lo, n = CHUNKS[j]
                    if u < 2:
                        pe.wait_ge(lnl_c.sem, lnl_c.at(li, c + 1))
                    if u >= 3:
                        pe.wait_ge(up_sb.sem, up_sb.at(li, u - 2))
                    for k, o in enumerate((lo, HID + lo)):
                        last = mm(ps[0:n, 2 * (u % 3) + k, :], w1[:, o:o + n], ln_c[:, c * HALF:(c + 1) * HALF], start=True, stop=True)
                    last.then_inc(up_ps.sem, 1)
                    next(aside, None)
                pe.wait_ge(up_sb.sem, up_sb.at(li, UNITS))
                for c in range(2):
                    for j, (lo, n) in enumerate(CHUNKS):
                        last = mm(ps[:, c, :], w2[0:n, j, :], ff[0:n, j, c * HALF:(c + 1) * HALF],
                                  start=(j == 0), stop=(j == len(CHUNKS) - 1))
                    last.then_inc(down_ps.sem, 1)
                next(aside, None)

            def batch(b, aside):
                middle_part(b, aside)
                for l in range(LAYERS):
                    layer_part(b * LAYERS + l, b, l, aside)
                for _ in aside:
                    pass

            for _ in block0(0):
                pass
            similarities(0, after=False)
            with pe.Fori(0, B - 1) as b:
                batch(b, block0(b + 1))
                similarities(b + 1, after=True)
            batch(B - 1, iter(()))
            finish(B)

        @block.scalar
        def _(act):
            fn = nc.scalar.activation
            act.wait_ge(ready0.sem, 1)

            def rsqrt_of(k, turn, have, log, out):
                act.wait_ge(have.sem, have.at(turn, 1))
                fn(log_a[:, k, :], mv[:, k, :, 1], ACT.Ln, bias=cst("eps")).then_inc(log.sem, 1)
                act.wait_ge(log.sem, log.at(turn, 1))
                fn(rstd[:, k, :], log_a[:, k, :], ACT.Exp, scale=-0.5).then_inc(out.sem, 1)

            def block0(b):
                yield
                act.wait_ge(ln0_mv.sem, ln0_mv.at(b, 1))
                fn(log_a[:, 0, :], mv[:, 0, :, 1], ACT.Ln, bias=cst("eps")).then_inc(ln0_logs.sem, 1)
                fn(log_b[:, :], mv[:, 0, :, 1], ACT.Ln, bias=cst("eps_sq"), scale=1.0 + EPS).then_inc(ln0_logs.sem, 1)
                act.wait_ge(ln0_logs.sem, ln0_logs.at(b, 1))
                fn(rstd[:, 0, :], log_a[:, 0, :], ACT.Exp, scale=-0.5).then_inc(ln0_rstd.sem, 1)
                yield
                yield
                act.wait_ge(ln0_logd.sem, ln0_logd.at(b, 1))
                fn(rstd2[:, :], log_b[:, :], ACT.Exp, scale=0.5).then_inc(ln0_rstd.sem, 1)
                for _ in range(4):
                    yield
                act.wait_ge(hn_ps.sem, hn_ps.at(b, 1))
                fn(halves(h_pad[:, 1:T + 1]), both(6), ACT.Identity, bias=v("ln1_b"), scale=v("ln1_w")).then_inc(h_c.sem, 1)
                for _ in range(5):
                    yield
                act.wait_ge(k_ps.sem, k_ps.at(b, 1))
                fn(halves(k_c[:, :]), both(6), ACT.Copy).then_inc(k_sb.sem, 1)
                yield
                yield
                act.wait_ge(v_ps.sem, v_ps.at(b, 1))
                fn(halves(v_c[:, :]), both(6), ACT.Copy).then_inc(v_sb.sem, 1)
                yield
                yield
                act.wait_ge(r_ps.sem, r_ps.at(b, 1))
                fn(halves(r_c[:, :]), both(6), ACT.Tanh, scale=0.5).then_inc(r_sb.sem, 1)
                yield
                act.wait_ge(wkv.sem, wkv.at(b, 2))
                fn(e_a[:, :], e_a[:, :], ACT.Exp).then_inc(wkv_exp.sem, 1)
                act.wait_ge(wkv.sem, wkv.at(b, 3))
                fn(e_b[:, :], e_b[:, :], ACT.Exp).then_inc(wkv_exp.sem, 1)
                yield
                act.wait_ge(gc_ps.sem, gc_ps.at(b, 1))
                fn(g1[0:64, :], ps[0:64, 6, 0:1], ACT.Gelu, bias=v("gc_b1", 64), scale=1.0 / T).then_inc(gc_sb.sem, 1)
                yield
                act.wait_ge(wkv.sem, wkv.at(b, 4))
                act.wait_ge(mixed.sem, mixed.at(b, 1))
                fn(h_pad[:, 1:T + 1], e_a[:, :], ACT.Ln).then_inc(wkv_ln.sem, 1)
                yield
                act.wait_ge(gc_ps.sem, gc_ps.at(b, 2))
                fn(g2[0:32, :], ps[0:32, 6, 1:2], ACT.Gelu, bias=v("gc_b2", 32)).then_inc(gc_sb.sem, 1)
                yield
                yield
                act.wait_ge(gc_ps.sem, gc_ps.at(b, 3))
                fn(tg[:, :], ps[:, 6, 2:3], ACT.Tanh, bias=dv("half_gc_b3"), scale=0.5).then_inc(gc_sb.sem, 1)
                yield
                act.wait_ge(wkv.sem, wkv.at(b, 7))
                fn(e_a[:, :], e_a[:, :], ACT.Exp).then_inc(wkv_exp2.sem, 1)
                act.wait_ge(wkv.sem, wkv.at(b, 8))
                fn(e_b[:, :], e_b[:, :], ACT.Exp).then_inc(wkv_exp2.sem, 1)
                yield
                fn(z_c[:, :], z_c[:, :], ACT.Tanh, bias=dv("half_u"), scale=0.5).then_inc(wkv_gate.sem, 1)
                for _ in range(7):
                    yield
                for cy in range(CYCLES):
                    yield
                    act.wait_ge(cn_ps.sem, cn_ps.at(b, 5 * cy + 1))
                    fn(halves(k_c[:, :]), both(6), ACT.Gelu, bias=v("cn_b1")).then_inc(cn_sb.sem, 1)
                    yield
                    yield
                    act.wait_ge(cn_ps.sem, cn_ps.at(b, 5 * cy + 2))
                    fn(halves(v_c[0:64, :]), ps[0:64, 6:8, :], ACT.Gelu, bias=v("cn_b2", 64)).then_inc(cn_sb.sem, 1)
                    yield
                    yield
                    act.wait_ge(cn_ps.sem, cn_ps.at(b, 5 * cy + 3))
                    fn(halves(aa[0:32, 0:T]), ps[0:32, 6:8, :], ACT.Gelu, bias=v("cn_b3", 32)).then_inc(cn_sb.sem, 1)
                    yield
                    yield
                    act.wait_ge(cn_ps.sem, cn_ps.at(b, 5 * cy + 4))
                    if cy:
                        act.wait_ge(cycle.sem, cycle.at(b, 3 * cy))
                    fn(halves(e_a[:, :]), both(6), ACT.Tanh, bias=dv("half_cn_b4"), scale=0.5).then_inc(cn_sb.sem, 1)
                    yield
                    yield
                    yield
                yield
                yield
                rsqrt_of(0, b, ln2_mv, ln2_log, ln2_rstd)
                yield
                yield
                yield
                act.wait_ge(h2_ps.sem, h2_ps.at(b, 1))
                fn(halves(h_pad[:, 1:T + 1]), both(6), ACT.Identity, bias=v("ln2_b"), scale=v("ln2_w")).then_inc(h2_c.sem, 1)
                for _ in range(3):
                    yield
                for j in range(4):
                    yield
                    act.wait_ge(kc_ps.sem, kc_ps.at(b, j + 1))
                    fn(halves(relus[j][:, 0:T]), both(6), ACT.Relu).then_inc(kc_relu.sem, 1)
                    yield
                yield
                act.wait_ge(rc_ps.sem, rc_ps.at(b, 1))
                fn(halves(r_c[:, :]), both(6), ACT.Tanh, scale=0.5).then_inc(rc_sb.sem, 1)
                fn(e_b[:, :], xn[:, :], ACT.Tanh, scale=0.5).then_inc(gate0.sem, 1)
                yield

                for _ in range(7):
                    yield
                rsqrt_of(0, b, ln3_mv, ln3_log, ln3_rstd)
                for _ in range(3):
                    yield
                act.wait_ge(y_ps.sem, y_ps.at(b, 1))
                fn(halves(xn1[:, :]), both(6), ACT.Copy).then_inc(y_c.sem, 1)
                for n, (dst, bias) in enumerate([(k_c, "theta_q0"), (v_c, "theta_k0")]):
                    yield
                    yield
                    act.wait_ge(qk_ps.sem, qk_ps.at(b, n + 1))
                    fn(halves(dst[:, :]), both(6), ACT.Identity, bias=dv(bias), scale=dv("inv_wave")).then_inc(theta.sem, 1)
                yield
                yield
                act.wait_ge(va_ps.sem, va_ps.at(b, 1))
                fn(v_att[:, :, 0:D].rearrange("p (c n) d -> p c n d", c=2),
                   ps[:, 6:8, :].rearrange("p c (n d) -> p c n d", d=D), ACT.Copy).then_inc(va_sb.sem, 1)
                yield
                for n, (r, co) in enumerate([(k_c, e_a), (v_c, e_b)]):
                    act.wait_ge(reduced.sem, reduced.at(b, n + 1))
                    fn(co[:, :], r[:, :], ACT.Abs).then_inc(abs_s.sem, 1)
                    act.wait_ge(abs_s.sem, abs_s.at(b, n + 1))
                    fn(co[:, :], co[:, :], ACT.Sin, bias=cst("half_pi"), scale=-1.0).then_inc(trig.sem, 1)
                    fn(r[:, :], r[:, :], ACT.Sin).then_inc(trig.sem, 1)
                    yield
                    yield

            def finish(bn):
                act.wait_ge(y_done.sem, y_done.at(bn * LAYERS, 0))
                fn(gate_c, y[:, :], ACT.Tanh, scale=0.5).then_inc(gate1.sem, 1)

            def similarities(b, after):
                if after:
                    finish(b)
                for n in range(2 * NT):
                    c, kt = n // NT, n % NT
                    act.wait_ge(sim_ps.sem, sim_ps.at(b, n + 1))
                    fn(p_att[:, kt, c * HALF:(c + 1) * HALF], ps[:, (n + 2) % 4, :], ACT.Exp, scale=D ** -0.5).then_inc(sim_exp.sem, 1)

            def shift(li, b):
                act.wait_ge(y_in.sem, y_in.at(b, 1))
                act.wait_ge(y_done.sem, y_done.at(li, 0))
                fn(h_s[64:P, 1:T], y[64:P, 0:T - 1], ACT.Copy).then_inc(shifted.sem, 1)

            def middle_part(b, aside):
                shift(b * LAYERS, b)
                for m in range(NT):
                    next(aside, None)
                act.wait_ge(at_ps.sem, at_ps.at(b, 1))
                fn(halves(att_c), both(0), ACT.Identity, bias=v("bv")).then_inc(at_sb.sem, 1)
                act.wait_ge(ao_ps.sem, ao_ps.at(b, 1))
                fn(halves(s_att[:, :]), both(4), ACT.Identity, bias=v("bo")).then_inc(ao_sb.sem, 1)

            def layer_part(li, aside):
                for i in range(JOBS + 1):
                    if i < JOBS:
                        if i >= 2:
                            act.wait_ge(norm_ps.sem, norm_ps.at(li, i - 1))
                        for kind in range(2):
                            act.wait_ge(rotated.sem, rotated.at(li, 4 * i + 2 * kind + 1))
                            fn(squares[:, i % 2, kind, :], ps[:, 2 * kind, :], ACT.Square).then_inc(sq_sb.sem, 1)
                        next(aside, None)
                    if i:
                        act.wait_ge(norm_ps.sem, norm_ps.at(li, i))
                        if i >= 3:
                            act.wait_ge(k_done.sem, k_done.at(li, i - 2))
                        fn(rn_k[:, (i - 1) % 2, :], ps[:, 5, :], ACT.Ln, bias=cst("tiny"), scale=2.0 ** 20).then_inc(norm_ln.sem, 1)
                        fn(rn_q[:, 8 * (i - 1):8 * i], ps[:, 4, 0:8], ACT.Ln, bias=cst("tiny"), scale=2.0 ** 20).then_inc(qn_ln.sem, 1)
                        act.wait_ge(norm_ln.sem, norm_ln.at(li, i))
                        fn(rn_k[:, (i - 1) % 2, :], rn_k[:, (i - 1) % 2, :], ACT.Exp, bias=cst("ln_1024"), scale=-0.5).then_inc(norm_ex.sem, 1)
                        next(aside, None)
                act.wait_ge(qn_ln.sem, qn_ln.at(li, JOBS))
                fn(rn_q[:, :], rn_q[:, :], ACT.Exp, bias=cst("ln_1024"), scale=-0.5).then_inc(qn_ex.sem, 1)

                def exps(n):
                    hp, m = n // NT, n % NT
                    if n >= 4:
                        act.wait_ge(pt_ps.sem, pt_ps.at(li, n - 3))
                    act.wait_ge(s_neg.sem, s_neg.at(li, n + 1))
                    for e in range(2):
                        col = (hp * NT + m) * 2 + e
                        last = fn(p_win[:, n % 4, e, 2 * P - KEYS:], ps[:, 2 * (n % 2) + e, 0:KEYS], ACT.Exp,
                                  bias=neg_top[:, n % 4, e:e + 1], scale=rn_q[:, col:col + 1],
                                  accum_out=den[:, n % 4, e:e + 1])
                    last.then_inc(p_sb.sem, 1)

                def copy_pt(n):
                    act.wait_ge(pt_ps.sem, pt_ps.at(li, n + 1))
                    if n >= 3:
                        act.wait_ge(o_ps.sem, o_ps.at(li, n - 2))
                    lo = 0 if n % NT else 1
                    fn(pt_win[:, n % 3, :, lo:, :], ps[:, 4, :].rearrange("p (e c k) -> p e c k", e=2, c=2)[:, :, lo:, :],
                       ACT.Copy).then_inc(pt_sb[0].sem, 1)

                for n in range(STEPS + LAG):
                    if n < STEPS:
                        exps(n)
                    if TURN <= n < STEPS + TURN and (n - TURN) % 2 == 0:
                        copy_pt(n - TURN)
                    if n % 8 in STEP_SLOTS:
                        next(aside, None)
                next(aside, None)
                act.wait_ge(y_mid.sem, y_mid.at(li, 1))
                fn(h_s[64:P, 1:T], y[64:P, 0:T - 1], ACT.Copy).then_inc(shifted2.sem, 1)
                rsqrt_of(1, li, lnl_mv, lnl_log, lnl_rstd)
                next(aside, None)
                act.wait_ge(mlp_loaded.sem, mlp_loaded.at(li, 32))
                for c in range(2):
                    act.wait_ge(lnl_ps.sem, lnl_ps.at(li, c + 1))
                    fn(ln_c[:, c * HALF:(c + 1) * HALF], ps[:, 4 + c, :], ACT.Identity, bias=lv("ln_b"), scale=lv("ln_g")).then_inc(lnl_c.sem, 1)
                next(aside, None)
                for u in range(UNITS):
                    n = CHUNKS[u // 2][1]
                    act.wait_ge(up_ps.sem, up_ps.at(li, u + 1))
                    if u >= 3:
                        act.wait_ge(up_sb.sem, up_sb.at(li, u - 2))
                    fn(gelus[0:n, u % 3, :], ps[0:n, 2 * (u % 3) + 1, :], ACT.Gelu, bias=lv(f"b1g{u // 2}", n)).then_inc(gelu_sb.sem, 1)
                    next(aside, None)
                next(aside, None)

            def batch(b, aside):
                middle_part(b, aside)
                for l in range(LAYERS):
                    if l:
                        shift(b * LAYERS + l, b)
                    layer_part(b * LAYERS + l, aside)
                for _ in aside:
                    pass

            for _ in block0(0):
                pass
            similarities(0, after=False)
            with act.Fori(0, B - 1) as b:
                batch(b, block0(b + 1))
                similarities(b + 1, after=True)
            batch(B - 1, iter(()))
            finish(B)

        @block.vector
        def _(dve):
            tt, ts_, stt = nc.vector.tensor_tensor, nc.vector.tensor_scalar, nc.vector.scalar_tensor_tensor
            scan = nc.vector.tensor_tensor_scan

            nc.vector.memset(h_s[64:P, 0:1], 0.0)
            for n, s in enumerate((out_sent, out_done, wo_ps, y_done)):
                nc.vector.memset(seed[:, n:n + 1], 0.0).then_inc(s.sem, 1)
            nc.vector.memset(v_att[:, :, D:D + 1], 1.0)
            nc.vector.memset(p_win[:, :, :, 0:2 * P - KEYS], 0.0).then_inc(setup.sem, 1)
            dve.wait_ge(w_in.sem, 16 * 5)
            nc.vector.tensor_copy(mask[:, :], work[:, 0:P + 2 * KEYS])
            ts_(dv("neg_ts"), v("ts"), -1.0, None, ALU.mult)
            ts_(dv("one_plus_ts"), v("ts"), 1.0, None, ALU.add)
            ts_(dv("one_minus_ts"), v("ts"), -1.0, 1.0, ALU.mult, ALU.add)
            ts_(dv("half_gc_b3"), v("gc_b3"), 0.5, None, ALU.mult)
            ts_(dv("half_cn_b4"), v("cn_b4"), 0.5, None, ALU.mult)
            ts_(dv("half_u"), v("u"), 0.5, None, ALU.mult)
            ts_(dv("ar7"), v("ar"), 0.7, None, ALU.mult)
            ts_(dv("ar3"), v("ar"), 0.3, None, ALU.mult)
            ts_(dv("wave_eps"), v("wave"), 1e-8, None, ALU.add).then_inc(setup.sem, 1)
            dve.wait_ge(setup.sem, 2)
            nc.vector.reciprocal(dv("inv_wave"), dv("wave_eps")).then_inc(setup.sem, 1)
            dve.wait_ge(setup.sem, 3)
            stt(dv("theta_q0"), v("bq"), dv("inv_wave"), v("phase"), ALU.mult, ALU.add)
            stt(dv("theta_k0"), v("bk"), dv("inv_wave"), v("phase"), ALU.mult, ALU.add).then_inc(setup.sem, 1)
            dve.wait_ge(setup.sem, 4)
            nc.vector.memset(top_s[:, :, :], 0.0).then_inc(ready0.sem, 1)
            dve.wait_ge(ready0.sem, 1)

            def moments(k, turn, src, have, done):
                for i in range(NT):
                    last = nc.vector.bn_stats(stats[:, k, i, :], src(i))
                last.then_inc(have.sem, 1)
                dve.wait_ge(have.sem, have.at(turn, 1))
                nc.vector.memset(carrier[:, k:k + 1], 0.0)
                for i in range(NT):
                    last = nc.vector.bn_aggr(mv[:, k, i, :], stats[:, k, i, :])
                last.then_inc(done.sem, 1)

            def normalise(k, dst, src):
                for i in range(NT):
                    last = ts_(dst[:, i, :], src(i), mv[:, k, i, 0:1], rstd[:, k, i:i + 1], ALU.subtract, ALU.mult)
                return last

            def bank_tile(bank):
                return lambda i: ps[:, bank + i // 4, (i % 4) * P:(i % 4 + 1) * P]

            def block0(b):
                dve.wait_ge(x_loaded.sem, x_loaded.at(b, 16))
                moments(0, b, lambda i: x_in[:, i, :], ln0_stats, ln0_mv)
                yield
                yield
                dve.wait_ge(ln0_logs.sem, ln0_logs.at(b, 2))
                tt(log_b[:, :], log_a[:, 0, :], log_b[:, :], ALU.subtract).then_inc(ln0_logd.sem, 1)
                yield
                yield
                dve.wait_ge(ln0_rstd.sem, ln0_rstd.at(b, 1))
                normalise(0, xn_tt, lambda i: x_in[:, i, :]).then_inc(xn_t.sem, 1)
                nc.vector.tensor_copy(h_pad[:, 0:1], v("ts")).then_inc(hpad0.sem, 1)
                yield
                dve.wait_ge(ln0_rstd.sem, ln0_rstd.at(b, 2))
                dve.wait_ge(xn_t.sem, xn_t.at(b, 1))
                for i in range(NT):
                    last = ts_(hn_tt[:, i, :], xn_tt[:, i, :], rstd2[:, i:i + 1], None, ALU.mult)
                last.then_inc(hn_t.sem, 1)
                yield
                yield
                yield
                dve.wait_ge(h_c.sem, h_c.at(b, 1))
                dve.wait_ge(hpad0.sem, hpad0.at(b, 1))
                ts_(e_a[:, :], h_pad[:, 0:T], dv("neg_ts"), None, ALU.mult).then_inc(mix_a.sem, 1)
                yield
                dve.wait_ge(xn_ps.sem, xn_ps.at(b, 1))
                nc.vector.tensor_copy(halves(xn[:, :]), both(6)).then_inc(xn_c.sem, 1)
                yield
                dve.wait_ge(mix_a.sem, mix_a.at(b, 1))
                stt(z_c[:, :], h_pad[:, 1:T + 1], dv("one_plus_ts"), e_a[:, :], ALU.mult, ALU.add).then_inc(mixed.sem, 1)
                yield
                dve.wait_ge(xn_c.sem, xn_c.at(b, 1))
                nc.vector.tensor_reduce(mean_c[:, :], xn[:, :], axis=AX, op=ALU.add).then_inc(mean_done.sem, 1)
                dve.wait_ge(mixed.sem, mixed.at(b, 1))
                for buf in (top, h_pad, aa):
                    nc.vector.memset(buf[:, 0:1], 0.0)
                yield
                yield
                dve.wait_ge(k_sb.sem, k_sb.at(b, 1))
                scan(top[:, 1:T + 1], k_c[:, :], k_c[:, :], 0.0, ALU.max, ALU.max).then_inc(wkv.sem, 1)
                yield
                dve.wait_ge(wkv.sem, wkv.at(b, 1))
                tt(e_a[:, :], top[:, 0:T], top[:, 1:T + 1], ALU.subtract).then_inc(wkv.sem, 1)
                yield
                tt(e_b[:, :], k_c[:, :], top[:, 1:T + 1], ALU.subtract).then_inc(wkv.sem, 1)
                yield
                yield
                yield
                dve.wait_ge(wkv_exp.sem, wkv_exp.at(b, 2))
                scan(e_a[:, :], e_a[:, :], e_b[:, :], 1.0, ALU.mult, ALU.add).then_inc(wkv.sem, 1)
                yield
                yield
                dve.wait_ge(wkv_ln.sem, wkv_ln.at(b, 1))
                tt(top[:, 0:T], top[:, 0:T], h_pad[:, 0:T], ALU.add).then_inc(wkv.sem, 1)
                yield
                dve.wait_ge(wkv.sem, wkv.at(b, 5))
                dve.wait_ge(r_ps.sem, r_ps.at(b, 1))
                tt(z_c[:, :], k_c[:, :], top[:, 0:T], ALU.subtract).then_inc(wkv.sem, 1)
                yield
                dve.wait_ge(wkv.sem, wkv.at(b, 6))
                ts_(e_a[:, :], z_c[:, :], -1.0, 0.0, ALU.mult, ALU.min).then_inc(wkv.sem, 1)
                ts_(e_b[:, :], z_c[:, :], 0.0, None, ALU.min).then_inc(wkv.sem, 1)
                yield
                dve.wait_ge(gc_sb.sem, gc_sb.at(b, 3))
                ts_(c0[:, :], tg[:, :], dv("ar7"), 0.1, ALU.mult, ALU.add).then_inc(gc_c0.sem, 1)
                yield
                dve.wait_ge(wkv_exp2.sem, wkv_exp2.at(b, 2))
                tt(e_b[:, :], e_b[:, :], v_c[:, :], ALU.mult).then_inc(wkv.sem, 1)
                yield
                dve.wait_ge(wkv.sem, wkv.at(b, 9))
                scan(aa[:, 1:T + 1], e_a[:, :], e_b[:, :], 0.0, ALU.mult, ALU.add).then_inc(wkv.sem, 1)
                yield
                dve.wait_ge(wkv.sem, wkv.at(b, 10))
                tt(e_a[:, :], v_c[:, :], aa[:, 0:T], ALU.subtract).then_inc(wkv.sem, 1)
                yield
                dve.wait_ge(wkv.sem, wkv.at(b, 11))
                dve.wait_ge(wkv_gate.sem, wkv_gate.at(b, 1))
                stt(e_a[:, :], z_c[:, :], 1.0, e_a[:, :], ALU.add, ALU.mult).then_inc(wkv.sem, 1)
                yield
                dve.wait_ge(wkv.sem, wkv.at(b, 12))
                stt(e_a[:, :], e_a[:, :], 0.5, aa[:, 0:T], ALU.mult, ALU.add).then_inc(wkv.sem, 1)
                yield
                dve.wait_ge(wkv.sem, wkv.at(b, 13))
                dve.wait_ge(r_sb.sem, r_sb.at(b, 1))
                stt(e_a[:, :], r_c[:, :], 1.0, e_a[:, :], ALU.add, ALU.mult).then_inc(wkv.sem, 1)
                yield
                dve.wait_ge(wkv.sem, wkv.at(b, 14))
                stt(xn1[:, :], e_a[:, :], 0.5, xn[:, :], ALU.mult, ALU.add).then_inc(wkv.sem, 1)
                yield
                dve.wait_ge(gc_c0.sem, gc_c0.at(b, 1))
                for cy in range(CYCLES):
                    for _ in range(8):
                        yield
                    dve.wait_ge(cn_sb.sem, cn_sb.at(b, 4 * cy + 4))
                    ts_(e_a[:, :], e_a[:, :], dv("ar3"), c0[:, :], ALU.mult, ALU.add).then_inc(cycle.sem, 1)
                    yield
                    dve.wait_ge(cycle.sem, cycle.at(b, 3 * cy + 1))
                    dve.wait_ge(cn_ps.sem, cn_ps.at(b, 5 * cy + 5))
                    tt(halves(e_a[:, :]), halves(e_a[:, :]), both(6), ALU.mult).then_inc(cycle.sem, 1)
                    dve.wait_ge(cycle.sem, cycle.at(b, 3 * cy + 2))
                    tt(xn[:, :], xn[:, :], e_a[:, :], ALU.add).then_inc(cycle.sem, 1)
                    yield
                yield
                dve.wait_ge(x1_ps.sem, x1_ps.at(b, 1))
                moments(0, b, bank_tile(6), ln2_stats, ln2_mv)
                yield
                yield
                dve.wait_ge(ln2_rstd.sem, ln2_rstd.at(b, 1))
                normalise(0, hn_tt, bank_tile(6)).then_inc(h2_t.sem, 1)
                yield
                yield
                yield
                dve.wait_ge(h2_c.sem, h2_c.at(b, 1))
                nc.vector.tensor_copy(h_pad[:, 0:1], h_pad[:, T:T + 1]).then_inc(mix2.sem, 1)
                dve.wait_ge(mix2.sem, mix2.at(b, 1))
                ts_(e_a[:, :], h_pad[:, 0:T], v("ts"), None, ALU.mult).then_inc(mix2.sem, 1)
                yield
                dve.wait_ge(mix2.sem, mix2.at(b, 2))
                stt(z_c[:, :], h_pad[:, 1:T + 1], dv("one_minus_ts"), e_a[:, :], ALU.mult, ALU.add).then_inc(mix2.sem, 1)
                yield
                for _ in range(11):
                    yield
                dve.wait_ge(vv_ps.sem, vv_ps.at(b, 1))
                dve.wait_ge(rc_sb.sem, rc_sb.at(b, 1))
                stt(halves(e_a[:, :]), halves(r_c[:, :]), 1.0, both(6), ALU.add, ALU.mult).then_inc(s_mul.sem, 1)
                yield
                dve.wait_ge(s_mul.sem, s_mul.at(b, 1))
                stt(e_a[:, :], e_a[:, :], 0.5, xn1[:, :], ALU.mult, ALU.add).then_inc(s_done.sem, 1)
                yield
                dve.wait_ge(s_done.sem, s_done.at(b, 1))
                tt(e_a[:, :], e_a[:, :], xn[:, :], ALU.mult).then_inc(prod0.sem, 1)
                yield
                dve.wait_ge(prod0.sem, prod0.at(b, 1))
                dve.wait_ge(gate0.sem, gate0.at(b, 1))
                stt(e_a[:, :], e_b[:, :], 1.0, e_a[:, :], ALU.add, ALU.mult).then_inc(prod0.sem, 1)
                yield

                yield
                dve.wait_ge(prod0_ps.sem, prod0_ps.at(b, 1))
                stt(flat(x_in), both(6), 0.5, flat(x_in), ALU.mult, ALU.add).then_inc(x_new.sem, 1)
                dve.wait_ge(x_new.sem, x_new.at(b, 1))
                moments(0, b, lambda i: x_in[:, i, :], ln3_stats, ln3_mv)
                yield
                yield
                dve.wait_ge(ln3_rstd.sem, ln3_rstd.at(b, 1))
                normalise(0, y_tt, lambda i: x_in[:, i, :]).then_inc(y_t.sem, 1)
                for _ in range(5):
                    yield
                for n, th in enumerate((k_c, v_c)):
                    s0 = 5 * n
                    dve.wait_ge(theta.sem, theta.at(b, n + 1))
                    ts_(z_c[:, :], th[:, :], 1.0 / TWO_PI, ROUND, ALU.mult, ALU.add).then_inc(reduce_s.sem, 1)
                    dve.wait_ge(reduce_s.sem, reduce_s.at(b, s0 + 1))
                    ts_(z_c[:, :], z_c[:, :], ROUND, None, ALU.subtract).then_inc(reduce_s.sem, 1)
                    yield
                    for k, part in enumerate((PI2_A, PI2_B)):
                        dve.wait_ge(reduce_s.sem, reduce_s.at(b, s0 + 2 + k))
                        stt(th[:, :], z_c[:, :], -part, th[:, :], ALU.mult, ALU.add).then_inc(reduce_s.sem, 1)
                    yield
                    dve.wait_ge(reduce_s.sem, reduce_s.at(b, s0 + 4))
                    stt(th[:, :], z_c[:, :], -PI2_C, th[:, :], ALU.mult, ALU.add).then_inc(reduce_s.sem, 1)
                    dve.wait_ge(reduce_s.sem, reduce_s.at(b, s0 + 5))
                    ts_(th[:, :], th[:, :], PI_IN, -PI_IN, ALU.min, ALU.max).then_inc(reduced.sem, 1)
                    yield

            def finish(bn):
                dve.wait_ge(y_done.sem, y_done.at(bn * LAYERS, 0))
                dve.wait_ge(ao_sb.sem, ao_sb.at(bn, 0))
                tt(s_att[:, :], s_att[:, :], y[:, :], ALU.mult).then_inc(prod1.sem, 1)
                dve.wait_ge(prod1.sem, prod1.at(bn - 1, 1))
                dve.wait_ge(gate1.sem, gate1.at(bn, 0))
                stt(s_att[:, :], gate_c, 1.0, s_att[:, :], ALU.add, ALU.mult).then_inc(prod1.sem, 1)
                dve.wait_ge(prod1_ps.sem, prod1_ps.at(bn, 0))
                stt(flat(out_tt), both(4), 0.5, flat(x_mid), ALU.mult, ALU.add).then_inc(out_done.sem, 1)

            def similarities(b, after):
                if after:
                    finish(b)
                    dve.wait_ge(out_done.sem, out_done.at(b, 0))
                dve.wait_ge(y_c.sem, y_c.at(b, 1))
                nc.vector.tensor_copy(y[:, :], xn1[:, :]).then_inc(y_in.sem, 1)
                dve.wait_ge(y_in.sem, y_in.at(b, 1))
                dve.wait_ge(x_new.sem, x_new.at(b, 1))
                nc.vector.tensor_copy(x_mid[:, :, :], x_in[:, :, :]).then_inc(x_mid_done.sem, 1)

            def middle_part(b, aside):
                for m in range(NT):
                    dve.wait_ge(pv_ps.sem, pv_ps.at(b, m + 1))
                    nc.vector.reciprocal(rden_att[:, m:m + 1], ps[:, 4 + m % 2, D:D + 1]).then_inc(pv_r.sem, 1)
                    dve.wait_ge(pv_r.sem, pv_r.at(b, m + 1))
                    ts_(o_tt[:, m, :], ps[:, 4 + m % 2, 0:D], rden_att[:, m:m + 1], None, ALU.mult).then_inc(pv_sb.sem, 1)
                    next(aside, None)
                dve.wait_ge(out_sent.sem, out_sent.at(b, 0))

            def layer_part(li, aside):
                nc.vector.tensor_copy(h_s[0:64, :], y[0:64, :]).then_inc(copied.sem, 1)
                dve.wait_ge(mlp_loaded.sem, mlp_loaded.at(li, 32))
                dve.wait_ge(qk4_ps.sem, qk4_ps.at(li, 1))
                nc.vector.memset(k_rot[:, :, 0:WIN], 0.0)

                for i in range(JOBS + 2):
                    if i >= 2:
                        hp, c, slot = (i - 2) // 2, i % 2, i % 2
                        dve.wait_ge(k_sum.sem, k_sum.at(li, i - 1))
                        dve.wait_ge(q_sum.sem, q_sum.at(li, i - 1))
                        dve.wait_ge(norm_ex.sem, norm_ex.at(li, i - 1))
                        stt(k_rot[:, hp, WIN + c * HALF:WIN + (c + 1) * HALF], rn_k[:, slot, :], 1e12, rot[:, slot, 2, :],
                            ALU.min, ALU.mult).then_inc(k_done.sem, 1)
                        dve.wait_ge(k_done.sem, k_done.at(li, i - 1))
                    if i < JOBS:
                        hp, c = i // 2, i % 2
                        for kind, scale in enumerate(("qs", "qs_r", "ks", "ks_r")):
                            if kind == 3:
                                dve.wait_ge(vw_ps.sem, vw_ps.at(li, i + 1))
                                nc.vector.tensor_copy(v_win[:, i, :, :], ps[:, 4, :].rearrange("p (h d) -> p h d", h=HEADS)).then_inc(vw_sb.sem, 1)
                            dve.wait_ge(qk4_ps.sem, qk4_ps.at(li, 4 * i + kind + 1))
                            stt(rot[:, i % 2, kind, :], ps[:, kind, :], lv(scale), table[:, kind, c * HALF:(c + 1) * HALF],
                                ALU.mult, ALU.mult).then_inc(rotated.sem, 1)
                        next(aside, None)
                    if 1 <= i <= JOBS:
                        next(aside, None)
                dve.wait_ge(qn_ex.sem, qn_ex.at(li, 1))
                ts_(rn_q[:, :], rn_q[:, :], 1e12, None, ALU.min).then_inc(qn_cl.sem, 1)
                dve.wait_ge(qn_cl.sem, qn_cl.at(li, 1))

                def tops(n):
                    hp, m = n // NT, n % NT
                    dve.wait_ge(s_ps.sem, s_ps.at(li, n + 1))
                    nc.vector.tensor_reduce(top_s[:, n % 4, :], ps[:, 2 * (n % 2):2 * (n % 2) + 2, 0:KEYS], axis=AX,
                                            op=ALU.max).then_inc(s_top.sem, 1)
                    dve.wait_ge(s_top.sem, s_top.at(li, n + 1))
                    col = (hp * NT + m) * 2
                    stt(neg_top[:, n % 4, :], top_s[:, n % 4, :], -1.0, rn_q[:, col:col + 2], ALU.mult, ALU.mult).then_inc(s_neg.sem, 1)

                def copy_pt(n):
                    dve.wait_ge(pt_ps.sem, pt_ps.at(li, n + 1))
                    if n >= 3:
                        dve.wait_ge(o_ps.sem, o_ps.at(li, n - 2))
                    nc.vector.tensor_copy(pt_win[:, n % 3, :, :, :],
                                          ps[:, 4, :].rearrange("p (e c k) -> p e c k", e=2, c=2)).then_inc(pt_sb[1].sem, 1)

                def sums_of_weights(n):
                    dve.wait_ge(p_sb.sem, p_sb.at(li, n + 1))
                    if n >= 4:
                        dve.wait_ge(p_norm.sem, p_norm.at(li, n - 3))
                    nc.vector.reciprocal(rden[:, n % 4, :], den[:, n % 4, :]).then_inc(p_den.sem, 1)

                def outputs(n):
                    hp, m = n // NT, n % NT
                    dve.wait_ge(o_ps.sem, o_ps.at(li, n + 1))
                    nc.vector.tensor_copy(ff[:, hp, m * P:(m + 1) * P], ps[:, 5, 0:P]).then_inc(o_sb.sem, 1)

                for n in range(STEPS + LAG):
                    if n < STEPS:
                        tops(n)
                    if 1 <= n <= STEPS:
                        sums_of_weights(n - 1)
                    if TURN <= n < STEPS + TURN and (n - TURN) % 2 == 1:
                        copy_pt(n - TURN)
                    if n >= LAG:
                        outputs(n - LAG)
                    if n % 8 in STEP_SLOTS:
                        next(aside, None)
                next(aside, None)
                dve.wait_ge(wo_half.sem, wo_half.at(li, 1))
                tt(y[:, 0:HALF], y[:, 0:HALF], ps[:, 0, :], ALU.add)
                dve.wait_ge(wo_ps.sem, wo_ps.at(li, 1))
                tt(y[:, HALF:T], y[:, HALF:T], ps[:, 1, :], ALU.add).then_inc(y_mid.sem, 1)
                dve.wait_ge(y_mid.sem, y_mid.at(li, 1))
                nc.vector.tensor_copy(h_s[0:64, :], y[0:64, :]).then_inc(copied2.sem, 1)
                dve.wait_ge(lnl_tp.sem, lnl_tp.at(li, 1))
                moments(1, li, bank_tile(2), lnl_stats, lnl_mv)
                next(aside, None)
                dve.wait_ge(lnl_rstd.sem, lnl_rstd.at(li, 1))
                tile = bank_tile(2)
                for i in range(NT):
                    last = ts_(ln_t[:, i, :], tile(i), mv[:, 1, i, 0:1], rstd[:, 1, i:i + 1], ALU.subtract, ALU.mult)
                    if i % 4 == 3:
                        last.then_inc(lnl_t.sem, 1)
                next(aside, None)
                for u in range(UNITS):
                    j, c = u // 2, u % 2
                    n = CHUNKS[j][1]
                    dve.wait_ge(gelu_sb.sem, gelu_sb.at(li, u + 1))
                    stt(ff[0:n, j, c * HALF:(c + 1) * HALF], ps[0:n, 2 * (u % 3), :], lv(f"b1a{j}", n), gelus[0:n, u % 3, :],
                        ALU.add, ALU.mult).then_inc(up_sb.sem, 1)
                    next(aside, None)
                dve.wait_ge(down_ps.sem, down_ps.at(li, 1))
                stt(y[:, 0:HALF], ps[:, 0, :], lv("b2"), y[:, 0:HALF], ALU.add, ALU.add)
                dve.wait_ge(down_ps.sem, down_ps.at(li, 2))
                stt(y[:, HALF:T], ps[:, 1, :], lv("b2"), y[:, HALF:T], ALU.add, ALU.add).then_inc(y_done.sem, 1)
                dve.wait_ge(y_done.sem, y_done.at(li, 1))
                next(aside, None)

            def batch(b, aside):
                middle_part(b, aside)
                for l in range(LAYERS):
                    layer_part(b * LAYERS + l, aside)
                for _ in aside:
                    pass

            for _ in block0(0):
                pass
            similarities(0, after=False)
            with dve.Fori(0, B - 1) as b:
                batch(b, block0(b + 1))
                similarities(b + 1, after=True)
            batch(B - 1, iter(()))
            finish(B)

        @block.gpsimd
        def _(pool):
            add = nc.gpsimd.tensor_tensor

            def block0(b):
                for _ in range(71):
                    yield
                for j in range(4):
                    pool.wait_ge(kc_relu.sem, kc_relu.at(b, j + 1))
                    add(relus[j][:, 0:T], relus[j][:, 0:T], relus[j][:, 0:T], ALU.mult).then_inc(kc_sq.sem, 1)
                    yield
                    yield

            def layer_part(li, aside):
                for i in range(JOBS):
                    hp, c = i // 2, i % 2
                    pool.wait_ge(rotated.sem, rotated.at(li, 4 * i + 2))
                    add(q_rot[:, hp, c * HALF:(c + 1) * HALF], rot[:, i % 2, 0, :], rot[:, i % 2, 1, :], ALU.add).then_inc(q_sum.sem, 1)
                    pool.wait_ge(rotated.sem, rotated.at(li, 4 * i + 4))
                    add(rot[:, i % 2, 2, :], rot[:, i % 2, 2, :], rot[:, i % 2, 3, :], ALU.add).then_inc(k_sum.sem, 1)
                    next(aside, None)
                    next(aside, None)
                for n in range(STEPS + LAG):
                    if 1 <= n <= STEPS:
                        p = p_win[:, (n - 1) % 4, :, 2 * P - KEYS:]
                        pool.wait_ge(p_den.sem, p_den.at(li, n))
                        add(p, p, rden[:, (n - 1) % 4, :].rearrange("p (e u) -> p e u", u=1).broadcast_to((P, 2, KEYS)),
                            ALU.mult).then_inc(p_norm.sem, 1)
                    if n % 8 in STEP_SLOTS:
                        next(aside, None)
                for _ in range(TAIL_SLOTS):
                    next(aside, None)

            def batch(b, aside):
                for m in range(NT):
                    next(aside, None)
                for l in range(LAYERS):
                    layer_part(b * LAYERS + l, aside)
                for _ in aside:
                    pass

            for _ in block0(0):
                pass
            with pool.Fori(0, B - 1) as b:
                batch(b, block0(b + 1))
            batch(B - 1, iter(()))


def _pad_rows(a, rows=P, cols=None):
    a = np.asarray(a, np.float32)
    if a.ndim == 1:
        return _pad_rows(a[:, None], rows)[:, 0]
    out = np.zeros((rows, cols or a.shape[1]), np.float32)
    out[:a.shape[0], :a.shape[1]] = a
    return out


def _column(a, repeat=False):
    a = np.asarray(a, np.float32).reshape(-1)
    return np.repeat(a, P) if repeat else _pad_rows(a)


def _by_chunk(a):
    a = _pad_rows(a, -(-a.shape[0] // P) * P)
    return a.reshape(-1, P, a.shape[1]).transpose(1, 0, 2).reshape(P, -1)


def _constants():
    const = np.zeros((P, CONST_COLS), np.float32)
    const[:, C_ID] = np.eye(P)
    quarter = np.arange(P // 4)
    twist = np.zeros((P, P), np.float32)
    for to, frm, sign in [(0, 64, 1), (32, 96, -1), (64, 0, -1), (96, 32, 1)]:
        twist[frm + quarter, to + quarter] = sign
    const[:, C_TW] = twist
    head = np.arange(P) // DH
    const[:, C_PAIR] = head[:, None] == head[None, :]
    const[:, C_HEAD] = head[:, None] == np.arange(2)[None, :]
    for name, value in [("eps", EPS), ("eps_sq", EPS * EPS), ("tiny", 2.0 ** -64), ("ln_1024", np.log(1024.0)),
                        ("half_pi", np.pi / 2)]:
        const[:, C_CST + CST[name]] = value
    f = np.float32
    half = np.arange(0, DH, 2, dtype=f)
    freq = (f(1.0) / f(10000.0) ** (half / f(DH))).astype(f)
    t = np.arange(T, dtype=f)
    angle = (t[None, :] * freq[:, None]).astype(f)
    base = (half + f(0.4 * DH)) / f(1.4 * DH)
    scale = base[:, None].astype(f) ** ((t - T // 2) / f(WIN // 2))[None, :]
    cos, sin = np.cos(angle), np.sin(angle)
    sign_rows = lambda a: np.concatenate([-a, a, -a, a])
    table = np.stack([np.tile(cos * scale, (4, 1)) * f(QK_SCALE), sign_rows(sin * scale) * f(QK_SCALE),
                      np.tile(cos / scale, (4, 1)), sign_rows(sin / scale)], axis=1).astype(f)
    q, k = np.arange(P)[:, None], np.arange(KEYS)[None, :]
    band = (k >= q) & (k <= q + WIN)
    mask = np.concatenate([np.eye(P), np.where(band, 0.0, -1e30), np.where(band & (k >= WIN), 0.0, -1e30)], axis=1)
    return const, np.ascontiguousarray(table), mask.astype(f)


def _layout(i):
    f = lambda n: np.asarray(i[n], np.float32)
    A, G, C, W = "L0_attn_", "L0_ffn_", "L1_attn_", "L1_ffn_"
    wide = lambda a: np.repeat(a, P, axis=1)
    front = np.concatenate([
        f(A + "Wk").T, f(A + "Wv").T, f(A + "Wr").T, f(A + "Wcr").T, f(A + "Wck").T, _by_chunk(f(A + "Wcv").T),
        f(G + "cn_w1"), f(G + "cn_w2"), _pad_rows(f(G + "cn_w3"), cols=P), _pad_rows(wide(f(G + "cn_w4"))),
        f(G + "gc_w1"), _pad_rows(f(G + "gc_w2"), cols=P), _pad_rows(wide(f(G + "gc_w3"))),
        f(C + "Wq").T, f(C + "Wk").T, f(C + "Wv").T, f(C + "Wo").T], axis=1)
    vec = np.stack([_column(f(n), repeat=n.endswith(("cn_b4", "gc_b3", "range"))) for n in
                    [A + "ln1_w", A + "ln1_b", A + "ln2_w", A + "ln2_b", A + "time_shift", A + "time_first",
                     G + "cn_b1", G + "cn_b2", G + "cn_b3", G + "cn_b4", G + "gc_b1", G + "gc_b2", G + "gc_b3",
                     G + "adaptive_range", C + "wavelengths", C + "phase_bias", C + "bq", C + "bk", C + "bv", C + "bo"]], axis=1)
    swap = (np.arange(DH) + DH // 2) % DH
    layers, mlps, lvecs = [], [], []
    for l in range(LAYERS):
        wqkv = f(W + "wqkv")[l].reshape(D, 3, PAIRS, 2, DH)
        q, k, v = wqkv[:, 0], wqkv[:, 1], wqkv[:, 2]
        wqk = np.stack([q, q[..., swap], k, k[..., swap]], axis=1)
        layers.append(np.concatenate([wqk.reshape(D, -1), v.reshape(D, -1), _by_chunk(f(W + "wo")[l])], axis=1))
        mlps.append(np.concatenate([f(W + "w1")[l], _by_chunk(f(W + "w2")[l])], axis=1))
        qs, ks, b1 = f(W + "q_scale")[l], f(W + "k_scale")[l], f(W + "b1")[l]
        two = lambda a: np.concatenate([a, a])
        lvecs.append(np.stack(
            [two(qs), two(qs[swap]), two(ks), two(ks[swap]), f(W + "ln_g")[l], f(W + "ln_b")[l]]
            + [_column(b1[o + lo:o + lo + n]) for o in (0, HID) for lo, n in CHUNKS] + [f(W + "b2")[l]], axis=1))
    return front, vec, np.stack(layers), np.stack(mlps), np.stack(lvecs)


def kernel(**inputs):
    import concourse.bacc as bacc
    from concourse.bass_utils import run_bass_kernel_spmd

    front, vec, layers, mlps, lvecs = _layout(inputs)
    const, table, mask = _constants()
    arrays = {"x": np.asarray(inputs["L0_attn_x"]), "front": front, "vec": vec, "layers": layers, "mlps": mlps,
              "lvecs": lvecs, "const": const, "table": table, "mask": mask}
    arrays = {"in_" + n: np.ascontiguousarray(a) for n, a in arrays.items()}
    nc = bacc.Bacc("TRN2", target_bir_lowering=False, num_devices=1)
    args = [nc.dram_tensor(n, a.shape, mybir.dt.from_np(a.dtype), kind="ExternalInput").ap() for n, a in arrays.items()]
    out = nc.dram_tensor("out", (B, T, D), F32, kind="ExternalOutput").ap()
    build(nc, *args, out)
    r = run_bass_kernel_spmd(nc, [arrays], core_ids=[0])
    return r.results[0]["out"]
```
